# Optimizing a Trainium2 kernel written in Bass

```python
import numpy as np
import jax
import jax.numpy as jnp

def _softmax(x, axis=-1):
    return jax.nn.softmax(x, axis=axis)

def _gelu(x):
    return jax.nn.gelu(x, approximate=True)

def _silu(x):
    return jax.nn.silu(x)

def _sigmoid(x):
    return jax.nn.sigmoid(x)

def _layernorm(x, axis=-1, eps=1e-05):
    m = jnp.mean(x, axis=axis, keepdims=True)
    v = jnp.var(x, axis=axis, keepdims=True)
    return (x - m) / jnp.sqrt(v + eps)

def _scatter_add(tgt, idx, src, axis=0):
    return tgt.at[idx].add(src)

def _segment_sum(src, seg, n):
    return jax.ops.segment_sum(src, seg, n)
kernel_name = 'mk_seq_preln_d2_jaxref_r4_53f6dd'

def setup_inputs(seed: int=0):
    np.random.seed(seed)
    _w = jnp.asarray

    def _L0_attn_setup():
        import jax, jax.numpy as jnp
        import numpy as np
        B, S, D, N = (8, 1024, 256, 64)
        EPS = 1e-05
        key = jax.random.key(seed)
        ks = jax.random.split(key, 6)
        sD = 1.0 / np.sqrt(D)
        sN = 1.0 / np.sqrt(N)
        return {'x': jax.random.normal(ks[0], (B, S, D), dtype=jnp.float32), 'ln_w': jnp.ones((D,), jnp.float32), 'ln_b': jnp.zeros((D,), jnp.float32), 'Wi': jax.random.normal(ks[1], (N, D), jnp.float32) * sD, 'bi': jnp.zeros((N,), jnp.float32), 'Wf': jax.random.normal(ks[2], (N, D), jnp.float32) * sD, 'bf': jnp.zeros((N,), jnp.float32), 'Wz': jax.random.normal(ks[3], (N, D), jnp.float32) * sD, 'bz': jnp.zeros((N,), jnp.float32), 'Wo': jax.random.normal(ks[4], (N, D), jnp.float32) * sD, 'bo': jnp.zeros((N,), jnp.float32), 'Wp': jax.random.normal(ks[5], (D, N), jnp.float32) * sN, 'bp': jnp.zeros((D,), jnp.float32)}
    _L0_attn_in = _L0_attn_setup()

    def _L0_ffn_setup():
        import jax, jax.numpy as jnp
        import numpy as np
        TOP_K = 2
        key = jax.random.key(seed)
        k1, k2, k3, k4 = jax.random.split(key, 4)
        B, T, D, H, E = (2, 512, 256, 512, 8)
        x = jax.random.normal(k1, (B, T, D), dtype=jnp.float32)
        w12 = jax.random.normal(k2, (E, 2 * H, D), dtype=jnp.float32) * D ** (-0.5)
        w3 = jax.random.normal(k3, (E, D, H), dtype=jnp.float32) * H ** (-0.5)
        gate_w = jax.random.normal(k4, (E, D), dtype=jnp.float32) * D ** (-0.5)
        return {'x': x, 'w12': w12, 'w3': w3, 'gate_w': gate_w}
    _L0_ffn_in = _L0_ffn_setup()

    def _L1_attn_setup():
        import math
        import jax, jax.numpy as jnp
        import numpy as np
        B, C, D = (4, 512, 256)
        DQ = DV = 64
        H = 16
        key = jax.random.key(seed)
        kx, kq, kk, kv, kw = jax.random.split(key, 5)
        x = jax.random.normal(kx, (B, C, D), dtype=jnp.float32)
        Q = jax.random.normal(kq, (DQ, D, H), dtype=jnp.float32) / math.sqrt(D)
        K = jax.random.normal(kk, (DQ, D, H), dtype=jnp.float32) / math.sqrt(D)
        V = jax.random.normal(kv, (DV, D, H), dtype=jnp.float32) / math.sqrt(D)
        W = jax.random.normal(kw, (D, DV, H), dtype=jnp.float32) / math.sqrt(DV)
        return {'x': x, 'Q': Q, 'K': K, 'V': V, 'W': W}
    _L1_attn_in = _L1_attn_setup()

    def _L1_ffn_setup():
        import jax, jax.numpy as jnp
        import numpy as np
        D = 256
        I = 128
        E = 32
        K = 4
        T = 2 * 512
        C = 2 * T * K // E
        key = jax.random.key(seed)
        ks = jax.random.split(key, 9)
        bf = jnp.bfloat16
        std = 0.02
        x = jax.random.normal(ks[0], (2, 512, D), dtype=jnp.float32).astype(bf)
        gate_w = (std * jax.random.normal(ks[1], (E, D), dtype=jnp.float32)).astype(bf)
        bias = jnp.zeros((E,), jnp.float32)
        W1 = (std * jax.random.normal(ks[2], (E, D, I), dtype=jnp.float32)).astype(bf)
        W3 = (std * jax.random.normal(ks[3], (E, D, I), dtype=jnp.float32)).astype(bf)
        W2 = (std * jax.random.normal(ks[4], (E, I, D), dtype=jnp.float32)).astype(bf)
        sw1 = (std * jax.random.normal(ks[5], (I, D), dtype=jnp.float32)).astype(bf)
        sw3 = (std * jax.random.normal(ks[6], (I, D), dtype=jnp.float32)).astype(bf)
        sw2 = (std * jax.random.normal(ks[7], (D, I), dtype=jnp.float32)).astype(bf)
        return {'x': x, 'gate_w': gate_w, 'bias': bias, 'W1': W1, 'W3': W3, 'W2': W2, 'sw1': sw1, 'sw3': sw3, 'sw2': sw2}
    _L1_ffn_in = _L1_ffn_setup()
    _d = {'L0_attn_x': _L0_attn_in['x'], 'L0_attn_ln_w': _L0_attn_in['ln_w'], 'L0_attn_ln_b': _L0_attn_in['ln_b'], 'L0_attn_Wi': _L0_attn_in['Wi'], 'L0_attn_bi': _L0_attn_in['bi'], 'L0_attn_Wf': _L0_attn_in['Wf'], 'L0_attn_bf': _L0_attn_in['bf'], 'L0_attn_Wz': _L0_attn_in['Wz'], 'L0_attn_bz': _L0_attn_in['bz'], 'L0_attn_Wo': _L0_attn_in['Wo'], 'L0_attn_bo': _L0_attn_in['bo'], 'L0_attn_Wp': _L0_attn_in['Wp'], 'L0_attn_bp': _L0_attn_in['bp'], 'L0_ffn_w12': _L0_ffn_in['w12'], 'L0_ffn_w3': _L0_ffn_in['w3'], 'L0_ffn_gate_w': _L0_ffn_in['gate_w'], 'L1_attn_Q': _L1_attn_in['Q'], 'L1_attn_K': _L1_attn_in['K'], 'L1_attn_V': _L1_attn_in['V'], 'L1_attn_W': _L1_attn_in['W'], 'L1_ffn_gate_w': _L1_ffn_in['gate_w'], 'L1_ffn_bias': _L1_ffn_in['bias'], 'L1_ffn_W1': _L1_ffn_in['W1'], 'L1_ffn_W3': _L1_ffn_in['W3'], 'L1_ffn_W2': _L1_ffn_in['W2'], 'L1_ffn_sw1': _L1_ffn_in['sw1'], 'L1_ffn_sw3': _L1_ffn_in['sw3'], 'L1_ffn_sw2': _L1_ffn_in['sw2']}
    _x0 = _d['L0_attn_x']
    _d['L0_attn_x'] = jax.random.normal(jax.random.fold_in(jax.random.key(seed), 1), (4, 1024, 256), dtype=_x0.dtype)
    del _x0
    return _d

def reference(L0_attn_x, L0_attn_ln_w, L0_attn_ln_b, L0_attn_Wi, L0_attn_bi, L0_attn_Wf, L0_attn_bf, L0_attn_Wz, L0_attn_bz, L0_attn_Wo, L0_attn_bo, L0_attn_Wp, L0_attn_bp, L0_ffn_w12, L0_ffn_w3, L0_ffn_gate_w, L1_attn_Q, L1_attn_K, L1_attn_V, L1_attn_W, L1_ffn_gate_w, L1_ffn_bias, L1_ffn_W1, L1_ffn_W3, L1_ffn_W2, L1_ffn_sw1, L1_ffn_sw3, L1_ffn_sw2):

    def _L0_attn_ref(x, ln_w, ln_b, Wi, bi, Wf, bf, Wz, bz, Wo, bo, Wp, bp):
        import jax, jax.numpy as jnp
        import numpy as np
        B, S, D, N = (8, 1024, 256, 64)
        EPS = 1e-05
        mu = jnp.mean(x, axis=-1, keepdims=True)
        var = jnp.mean(jnp.square(x - mu), axis=-1, keepdims=True)
        xn = (x - mu) * jax.lax.rsqrt(var + EPS) * ln_w + ln_b
        log_i = jnp.clip(jnp.einsum('bsd,nd->bsn', xn, Wi) + bi, -20.0, 20.0)
        log_f = jnp.clip(jnp.einsum('bsd,nd->bsn', xn, Wf) + bf, -20.0, 20.0)
        z = jnp.tanh(jnp.einsum('bsd,nd->bsn', xn, Wz) + bz)
        o = jax.nn.sigmoid(jnp.einsum('bsd,nd->bsn', xn, Wo) + bo)

        def step(carry, inp):
            c, m = carry
            li, lf, zt, ot = inp
            m_new = jnp.maximum(m + lf, li)
            i_s = jnp.exp(li - m_new)
            f_s = jnp.exp(m + lf - m_new)
            c = f_s * c + i_s * zt
            h = ot * jnp.tanh(c)
            return ((c, m_new), h)
        c0 = jnp.zeros((x.shape[0], log_i.shape[-1]), x.dtype)
        m0 = jnp.zeros_like(c0)
        tm = lambda a: jnp.swapaxes(a, 0, 1)
        _, h_seq = jax.lax.scan(step, (c0, m0), (tm(log_i), tm(log_f), tm(z), tm(o)))
        h_seq = jnp.swapaxes(h_seq, 0, 1)
        return jnp.einsum('bsn,dn->bsd', h_seq, Wp) + bp

    def _L0_ffn_ref(x, w12, w3, gate_w):
        import jax, jax.numpy as jnp
        import numpy as np
        TOP_K = 2
        E = gate_w.shape[0]
        H = w3.shape[-1]
        scores = jnp.einsum('btd,ed->bte', x, gate_w)
        topk_scores, topk_idx = jax.lax.top_k(scores, TOP_K)
        topk_probs = jax.nn.softmax(topk_scores, axis=-1)
        total_probs = jnp.sum(jax.nn.one_hot(topk_idx, E, dtype=topk_probs.dtype) * topk_probs[..., None], axis=-2)
        h12 = jnp.einsum('btd,ehd->bteh', x, w12)
        h1, h2 = (h12[..., :H], h12[..., H:])
        hidden = jax.nn.silu(h1) * h2
        expert_out = jnp.einsum('bteh,edh->bted', hidden, w3)
        y = jnp.sum(total_probs[..., None] * expert_out, axis=-2)
        return y

    def _L1_attn_ref(x, Q, K, V, W):
        import math
        import jax, jax.numpy as jnp
        import numpy as np
        B, C, D = (4, 512, 256)
        DQ = DV = 64
        H = 16
        d_query, d_embed, num_heads = Q.shape
        d_value = V.shape[0]
        sq = math.sqrt(d_query / d_embed)
        sv = math.sqrt(d_value / d_embed)
        q = jnp.einsum('qdh,bcd->bhcq', Q, x) * sq
        k = jnp.einsum('qdh,bcd->bhcq', K, x) * sq
        v = jnp.einsum('vdh,bcd->bhcv', V, x) * sv
        att = jnp.einsum('bhcq,bhCq->bhcC', q, k) / d_query
        T = x.shape[1]
        causal = jnp.arange(T)[:, None] >= jnp.arange(T)[None, :]
        att = jnp.where(causal, att, -jnp.inf)
        p = jax.nn.softmax(att, axis=-1)
        y = jnp.einsum('bhcC,bhCv->bhcv', p, v)
        z = jnp.einsum('dvh,bhcv->bcd', W, y) * (math.sqrt(d_embed / d_value) / num_heads)
        return z

    def _L1_ffn_ref(x, gate_w, bias, W1, W3, W2, sw1, sw3, sw2):
        import jax, jax.numpy as jnp
        import numpy as np
        D = 256
        I = 128
        E = 32
        K = 4
        T = 2 * 512
        C = 2 * T * K // E
        X = x.reshape(-1, D)
        logits = (X @ gate_w.T).astype(jnp.float32)
        scores = jax.nn.sigmoid(logits)
        _, idx = jax.lax.top_k(scores + bias[None, :], K)
        w = jnp.take_along_axis(scores, idx, axis=-1)
        w = w / jnp.clip(jnp.sum(w, axis=-1, keepdims=True), 1e-12, None)
        w = w.astype(x.dtype)
        eid = idx.reshape(-1)
        onehot = (eid[:, None] == jnp.arange(E)[None, :]).astype(jnp.int32)
        pos = jnp.take_along_axis(jnp.cumsum(onehot, axis=0) - 1, eid[:, None], axis=1)[:, 0]
        valid = pos < C
        posc = jnp.minimum(pos, C - 1)
        Xrep = jnp.repeat(X, K, axis=0)
        xe = jnp.zeros((E, C, D), x.dtype).at[eid, posc].add(jnp.where(valid[:, None], Xrep, jnp.zeros((), x.dtype)))
        h = jax.nn.silu(jnp.einsum('ecd,edi->eci', xe, W1)) * jnp.einsum('ecd,edi->eci', xe, W3)
        ye = jnp.einsum('eci,eid->ecd', h, W2)
        gflat = jnp.where(valid, w.reshape(-1), jnp.zeros((), x.dtype))
        yrows = ye[eid, posc] * gflat[:, None]
        out = yrows.reshape(-1, K, D).sum(axis=1)
        out = out + jax.nn.silu(X @ sw1.T) * (X @ sw3.T) @ sw2.T
        return out.reshape(x.shape)
    x = L0_attn_x
    x = x + _L0_attn_ref(_layernorm(x, axis=-1), L0_attn_ln_w, L0_attn_ln_b, L0_attn_Wi, L0_attn_bi, L0_attn_Wf, L0_attn_bf, L0_attn_Wz, L0_attn_bz, L0_attn_Wo, L0_attn_bo, L0_attn_Wp, L0_attn_bp)
    x = x + _L0_ffn_ref(_layernorm(x, axis=-1), L0_ffn_w12, L0_ffn_w3, L0_ffn_gate_w)
    x = x + _L1_attn_ref(_layernorm(x, axis=-1), L1_attn_Q, L1_attn_K, L1_attn_V, L1_attn_W)
    x = x + _L1_ffn_ref(_layernorm(x, axis=-1), L1_ffn_gate_w, L1_ffn_bias, L1_ffn_W1, L1_ffn_W3, L1_ffn_W2, L1_ffn_sw1, L1_ffn_sw3, L1_ffn_sw2)
    return x

_drawn_inputs = setup_inputs


def setup_inputs(seed=0):
    import zlib

    import numpy as np

    out = dict(_drawn_inputs(seed))
    spreads = {'L0_attn_ln_w': (1.0, 0.2),
     'L0_attn_ln_b': (0.0, 0.1),
     'L0_attn_bi': (0.0, 2.0),
     'L0_attn_bf': (0.0, 0.1),
     'L0_attn_bz': (0.0, 0.1),
     'L0_attn_bo': (0.0, 0.1),
     'L0_attn_bp': (0.0, 0.1),
     'L1_ffn_bias': (0.0, 2.0)}
    factors = {'L1_attn_Q': 8.0, 'L1_attn_K': 8.0}
    for name, (base, spread) in spreads.items():
        noise = np.random.default_rng([zlib.crc32(name.encode()), seed]).standard_normal(out[name].shape)
        drawn = base * np.exp(spread * noise) if base else spread * noise
        out[name] = jnp.asarray(drawn.astype(out[name].dtype))
    for name, factor in factors.items():
        out[name] = (out[name] * factor).astype(out[name].dtype)
    return out
```

```python
from contextlib import ExitStack

import concourse.bass as bass
from concourse import mybir

F32 = mybir.dt.float32
F32R = mybir.dt.float32r
BF16 = mybir.dt.bfloat16
I32 = mybir.dt.int32
U32 = mybir.dt.uint32
ALU = mybir.AluOpType
ACT = mybir.ActivationFunctionType
AX_X = mybir.AxisListType.X

P = 128
EPS = 1e-5
BIG = -1e30


class Steps:

    def __init__(self, eng, sem):
        self.eng, self.sem, self.base, self.n, self.i, self.per = eng, sem, 0, 0, None, 0

    def loop(self, i, rounds, per):
        assert self.i is None
        self.base += self.n
        self.n, self.i, self.rounds, self.per = 0, i, rounds, per

    def end(self):
        assert self.n == self.per, (self.n, self.per)
        self.base += self.rounds * self.per
        self.n, self.i = 0, None

    def done(self, ins):
        ins.then_inc(self.sem, 1)
        self.n += 1

    def sync(self):
        at = self.base + self.n
        self.eng.wait_ge(self.sem, at if self.i is None else self.i * self.per + at)


def network(nc, x_in, ln_w, ln_b, Wi, bi, Wf, bf, Wz, bz, Wo, bo, Wp, bp, w12, w3, gate0,
            Q, K, V, W, gate1, bias1, W1, W3, W2, sw1, sw3, sw2, out):
    B, S, D = x_in.shape
    T = B * S
    NT = T // P
    KD = D // P
    N = Wi.shape[0]
    E0, H0 = w12.shape[0], w3.shape[2]
    K0 = 2
    DQ, _, NH = Q.shape
    E1, _, I1 = W1.shape
    K1 = 4
    C1 = 2 * (2 * 512) * K1 // E1
    G = 4
    GT = G * P
    NG = T // GT
    KH = H0 // P
    HT = 2 * H0 // P
    REGION = T + P
    TILES0 = T * K0 // P + E0
    BIGSLOT = 1 << 20
    NPAIR = NH // 2
    QT = S // P
    NC2 = S // 512
    ATT_SCALE = (DQ / D) / DQ
    Z_SCALE = (DQ / D) ** 0.5 * (D / DQ) ** 0.5 / NH

    x_tiles = x_in.rearrange("b (i p) d -> p (b i) d", p=P)
    out_tiles = out.rearrange("b (i p) d -> p (b i) d", p=P)
    routed0 = nc.dram_tensor("routed0", (E0 * REGION, D), F32).ap()
    expert0 = nc.dram_tensor("expert0", (TILES0 * P, D), F32).ap()
    routed1 = nc.dram_tensor("routed1", (E1 * C1, D), F32).ap()
    expert1 = nc.dram_tensor("expert1", (E1 * C1, D), F32).ap()

    with ExitStack() as ctx:
        def sb(name, shape, dt=F32):
            return ctx.enter_context(nc.sbuf_tensor(name, shape, dt))

        def sem(name):
            return ctx.enter_context(nc.semaphore(name))

        X = sb("X", [P, NT, D])
        ident = sb("ident", [P, P])
        ones = sb("ones", [P, P])
        tri = sb("tri", [P, P], BF16)
        onesb = sb("onesb", [P, P], BF16)
        identb = sb("identb", [P, P], BF16)
        zeros = sb("zeros", [P, D])
        iota = sb("iota", [P, P])
        stat = sb("stat", [P, G, 6])
        mv = sb("mv", [P, G, 2])
        var = sb("var", [P, G])
        rstd = sb("rstd", [P, G])
        rtmp = sb("rtmp", [P, G])
        xn = sb("xn", [P, G, D])

        arena_at = (nc.sbuf_base + 31) // 32 * 32
        arena_size = (nc.sbuf_bytes_remaining - 128) // 4
        ctx.enter_context(nc.sbuf_tensor("arena", [P, arena_size], F32))
        at = [arena_at]

        def place(name, shape, dt=F32):
            n = 2 if dt == BF16 else 4
            for s in shape[1:]:
                n *= s
            t = nc.alloc_sbuf_tensor_at(name, shape, dt, offset=at[0])
            at[0] += (n + 31) // 32 * 32
            assert at[0] <= arena_at + 4 * arena_size, (name, at[0] - arena_at - 4 * arena_size)
            return t

        PS = ctx.enter_context(nc.psum_tensor("PS", [P, 8, 512], F32))

        b_w12T = place("b_w12T", [P, KD, E0 * 2 * H0])
        b_w3T = place("b_w3T", [P, KH, E0 * D])
        after_weights = at[0]
        b_raw = place("b_raw", [P, HT, D])
        b_raw3 = place("b_raw3", [P, KD, H0])

        a_xT = place("a_xT", [P, KD, 2 * S])
        a_wraw = place("a_wraw", [N, 4, D])
        a_wpraw = place("a_wpraw", [P, KD, N])
        a_wT = place("a_wT", [P, KD, 4, N])
        a_wpT = place("a_wpT", [P, D])
        a_bias = place("a_bias", [P, 4])
        a_hbo = place("a_hbo", [P, 1])
        a_bp = place("a_bp", [P, D])
        a_lnw = place("a_lnw", [P, KD])
        a_lnb = place("a_lnb", [P, KD])
        a_lf = place("a_lf", [P, S])
        a_li = place("a_li", [P, S])
        a_z = place("a_z", [P, S])
        a_o = place("a_o", [P, S])
        a_m = place("a_m", [P, 1 + S])
        a_fs = place("a_fs", [P, S])
        a_is = place("a_is", [P, S])
        a_c = a_lf
        a_h = a_li

        at[0] = after_weights
        b_gw = place("b_gw", [E0, D])
        b_gwT = place("b_gwT", [P, KD, E0])
        b_xT = place("b_xT", [P, KD, GT])
        b_s8 = place("b_s8", [P, G, E0])
        b_top = place("b_top", [P, G, 8])
        b_ix = place("b_ix", [P, G, 8], U32)
        b_idx = place("b_idx", [P, G, K0])
        b_gap = place("b_gap", [P, G])
        b_ex = place("b_ex", [P, G])
        b_den = place("b_den", [P, G])
        b_oh = place("b_oh", [P, G, K0, E0])
        b_ohs = place("b_ohs", [P, G, E0], BF16)
        b_sum = place("b_sum", [P, E0], BF16)
        b_gsum = place("b_gsum", [P, E0])
        b_tmp = place("b_tmp", [P, G, K0, E0])
        b_pos = place("b_pos", [P, G, K0])
        b_slot = place("b_slot", [P, G, K0], U32)
        b_posA = place("b_posA", [P, NT, K0])
        b_idxA = place("b_idxA", [P, NT, K0])
        b_prA = place("b_prA", [P, NT, K0])
        b_gix = place("b_gix", [P, NT, K0], U32)
        b_gtmp = place("b_gtmp", [P, NT, K0])
        b_cnt = place("b_cnt", [P, E0])
        b_nti = place("b_nti", [P, E0], I32)
        b_nt = place("b_nt", [P, E0])
        b_end = place("b_end", [P, E0])
        b_start = place("b_start", [P, E0])
        b_zrow = place("b_zrow", [P, E0])
        b_zrowi = place("b_zrowi", [P, E0], I32)
        b_te = place("b_te", [P, TILES0])
        b_ts = place("b_ts", [P, TILES0])
        b_tt = place("b_tt", [P, TILES0])
        b_tei = place("b_tei", [P, TILES0], I32)
        b_rowi = place("b_rowi", [P, TILES0], I32)
        b_xt = place("b_xt", [P, 2, D])
        b_tT = place("b_tT", [P, 2, KD, P])
        b_sg = place("b_sg", [P, 2, H0])
        b_hid = place("b_hid", [P, 2, H0])
        b_hT = place("b_hT", [P, 2, KH, P])
        b_y = place("b_y", [P, 2, D])
        b_gi = place("b_gi", [P, 2, K0], U32)
        b_gat = place("b_gat", [P, 2, K0, D])

        at[0] = arena_at
        c_wqk = [place(f"c_wqk{n}", [P, KD, NH, P], F32R) for n in ("_hi", "_lo")]
        c_wv = [place(f"c_wv{n}", [P, KD, NH * DQ], F32R) for n in ("_hi", "_lo")]
        c_wo = place("c_wo", [P, NPAIR, D])
        c_xT = [place(f"c_xT{n}", [P, KD, S], F32R) for n in ("_hi", "_lo")]
        c_st = [place(f"c_st{n}", [P, 2, KD, P], F32R) for n in ("_hi", "_lo")]
        heads_at = at[0]
        c_q1 = [place(f"c_q1_{h}", [P, S], F32R) for h in range(2)]
        c_k1 = [place(f"c_k1_{h}", [P, S], F32R) for h in range(2)]
        c_q2 = [place(f"c_q2_{h}", [P, S], F32R) for h in range(2)]
        c_k2 = [place(f"c_k2_{h}", [P, S], F32R) for h in range(2)]
        c_v = [place(f"c_v_{h}", [P, QT, P]) for h in range(2)]
        c_p = place("c_p", [P, 4, 512])
        c_mx = [place(f"c_mx_{h}", [P, QT]) for h in range(2)]
        c_den = place("c_den", [P, NC2, 512])
        c_maskq = place("c_maskq", [P, P], BF16)
        c_maskk = place("c_maskk", [P, P], BF16)
        y_at = at[0]
        c_yT = place("c_yT", [P, NPAIR, S])
        at[0] = heads_at
        c_vraw = place("c_vraw", [DQ, D, NH])
        at[0] = y_at
        c_qkraw = place("c_qkraw", [P, D, NH])
        c_wraw = place("c_wraw", [P, KD, DQ, NH])
        c_vst = place("c_vst", [DQ, D])
        c_qkst = place("c_qkst", [P, D])
        c_wst = place("c_wst", [P, KD, 2, DQ])

        at[0] = arena_at
        d_raw = place("d_raw", [P, 2, D], BF16)
        d_raw2 = place("d_raw2", [P, KD, I1], BF16)
        d_gwraw = place("d_gwraw", [E1, D], BF16)
        d_rawf = place("d_rawf", [P, 2, D])
        d_raw2f = place("d_raw2f", [P, KD, I1])
        d_gwf = place("d_gwf", [E1, D])
        d_gwT = place("d_gwT", [P, KD, E1])
        d_s1T = place("d_s1T", [P, KD, 2, I1])
        d_s2T = place("d_s2T", [I1, D])
        d_bias = place("d_bias", [P, E1])
        d_xT = place("d_xT", [P, KD, GT])
        d_th = place("d_th", [P, G, E1])
        d_sc = place("d_sc", [P, G, E1])
        d_sel = place("d_sel", [P, G, E1])
        d_top = place("d_top", [P, G, 8])
        d_ix = place("d_ix", [P, G, 8], U32)
        d_idx = place("d_idx", [P, G, K1])
        d_oh = place("d_oh", [P, G, K1, E1])
        d_ohf = place("d_ohf", [P, G, E1])
        d_ohs = place("d_ohs", [P, G, E1], BF16)
        d_sum = place("d_sum", [P, E1], BF16)
        d_gsum = place("d_gsum", [P, E1])
        d_tmp = place("d_tmp", [P, G, K1, E1])
        d_tmp2 = place("d_tmp2", [P, G, K1, E1])
        d_pos = place("d_pos", [P, G, K1])
        d_w = place("d_w", [P, G, K1])
        d_ws = place("d_ws", [P, G])
        d_ok = place("d_ok", [P, G, K1])
        d_skip = place("d_skip", [P, G, K1])
        d_cl = place("d_cl", [P, G, K1])
        d_slot = place("d_slot", [P, G, K1], U32)
        d_wA = place("d_wA", [P, NT, K1])
        d_gix = place("d_gix", [P, NT, K1], U32)
        d_sth = place("d_sth", [I1, GT])
        d_sh = place("d_sh", [I1, GT])
        d_xe = place("d_xe", [P, 2, C1 // P, D])
        d_wb = place("d_wb", [P, 2, 3 * D], BF16)
        d_wf = place("d_wf", [P, 2, 3 * D])
        d_xeT = place("d_xeT", [P, 2, KD, C1])
        d_eth = place("d_eth", [I1, 2, C1])
        d_eh = place("d_eh", [I1, 2, C1])
        d_y = place("d_y", [P, 2, C1 // P, D])
        d_gi = place("d_gi", [P, 2, K1], U32)
        d_gat = place("d_gat", [P, 2, K1, D])

        stage_end = sem("stage_end")
        s_const = sem("constants_made")
        s_x = [sem(f"x_loaded{g}") for g in range(2 * S // GT)]
        s_out = sem("out_stored")
        s_act = sem("act_steps")
        s_dve = sem("dve_steps")
        s_pool = sem("pool_steps")
        s_pass = sem("wait_passed")
        s_aw = sem("a_weights_loaded")
        s_awt = sem("a_weights_transposed")
        s_awe = sem("a_weights_ready")
        s_axn = sem("a_xn_ready")
        s_atp = sem("a_xn_transposed")
        s_axT = sem("a_xT_ready")
        s_agate = sem("a_gate_ready")
        s_agev = sem("a_gate_taken")
        s_afree = sem("a_gate_buffers_free")
        s_ascan = sem("a_scan_step")
        s_aexp = sem("a_exp_ready")
        s_ah = sem("a_h_ready")
        s_ay = sem("a_proj_ready")
        s_x1 = sem("x1_ready")
        s_braw = sem("b_w12_loaded")
        s_braw3 = sem("b_w3_loaded")
        s_brawf = sem("b_w12_buffer_free")
        s_braw3f = sem("b_w3_buffer_free")
        s_btw = sem("b_weights_transposed")
        s_bwe = sem("b_weights_taken")
        s_bw = sem("b_router_loaded")
        s_bgt = sem("b_router_transposed")
        s_bge = sem("b_router_ready")
        s_bxn = sem("b_xn_ready")
        s_btp = sem("b_xn_transposed")
        s_bxT = sem("b_xT_ready")
        s_bsc = sem("b_scores_ready")
        s_bgap = sem("b_score_gap_ready")
        s_bex = sem("b_gap_exp_ready")
        s_boh = sem("b_onehot_ready")
        s_bpre = sem("b_prefix_ready")
        s_bslot = sem("b_slots_ready")
        s_bscat = sem("b_rows_scattered")
        s_bxnf = sem("b_xn_free")
        s_bcnt = sem("b_counts_ready")
        s_bplan = sem("b_plan_ready")
        s_bzero = sem("b_tails_zeroed")
        s_bin = [sem(f"b_tile_loaded{j}") for j in range(2)]
        s_binf = sem("b_tile_buffer_free")
        s_btt = sem("b_tile_transposed")
        s_btT = sem("b_tileT_ready")
        s_bh = sem("b_hidden_ready")
        s_bsg = sem("b_sigmoid_exp_ready")
        s_bhid = sem("b_gated_ready")
        s_bht = sem("b_gated_transposed")
        s_bhT = sem("b_gatedT_ready")
        s_by = sem("b_y_ready")
        s_bye = sem("b_y_taken")
        s_bst = sem("b_y_stored")
        s_bystf = sem("b_y_buffer_free")
        s_bgat = [sem(f"b_rows_gathered{j}") for j in range(2)]
        s_bgatf = sem("b_gather_buffer_free")
        s_x2 = sem("x2_ready")
        s_cl = sem("c_weights_loaded")
        s_cst = sem("c_weights_staged")
        s_cwt = sem("c_weights_transposed")
        s_cwh = sem("c_weights_hi_ready")
        s_cwl = sem("c_weights_lo_ready")
        s_cset = sem("c_constants_made")
        s_cxn = sem("c_xn_ready")
        s_ctp = sem("c_xn_transposed")
        s_cxh = sem("c_xT_hi_ready")
        s_cxl = sem("c_xT_lo_ready")
        s_cxf = sem("c_xT_free")
        s_cw = sem("c_head_weights_staged")
        s_cqk = sem("c_qk_ready")
        s_cqs = sem("c_qk_hi_ready")
        s_cks = sem("c_qk_lo_ready")
        s_cv = sem("c_v_ready")
        s_cve = sem("c_v_taken")
        s_cS = sem("c_scores_ready")
        s_cmx = sem("c_max_ready")
        s_cmT = sem("c_max_transposed")
        s_cm = sem("c_max_row_ready")
        s_cT = sem("c_scoresT_ready")
        s_cP = sem("c_probs_ready")
        s_cPu = sem("c_probs_used")
        s_cPf = sem("c_probs_buffer_free")
        s_cO = sem("c_out_ready")
        s_cOy = sem("c_out_y_taken")
        s_cOd = sem("c_out_den_taken")
        s_cyn = sem("c_y_normalised")
        s_cyf = sem("c_y_free")
        s_cz = sem("c_z_ready")
        s_x3 = sem("x3_ready")
        s_dve2 = sem("dve_attention_steps")
        s_dz = sem("d_rows_zeroed")
        s_dl = sem("d_weights_loaded")
        s_dcast = sem("d_weights_cast")
        s_dwt = sem("d_weights_transposed")
        s_dwe = sem("d_weights_ready")
        s_dxn = sem("d_xn_ready")
        s_dtp = sem("d_xn_transposed")
        s_dxT = sem("d_xT_ready")
        s_dsc = sem("d_logits_ready")
        s_dth = sem("d_logit_tanh_ready")
        s_doh = sem("d_onehot_ready")
        s_dpre = sem("d_prefix_ready")
        s_dslot = sem("d_slots_ready")
        s_dscat = sem("d_rows_scattered")
        s_dxnf = sem("d_xn_free")
        s_dsh = sem("d_shared_hidden_ready")
        s_dst = sem("d_shared_tanh_ready")
        s_dsg = sem("d_shared_gated_ready")
        s_dsy = sem("d_shared_y_ready")
        s_dsa = sem("d_shared_y_added")
        s_din = [sem(f"d_expert_loaded{j}") for j in range(2)]
        s_dinf = sem("d_expert_buffer_free")
        s_dec = sem("d_expert_weights_cast")
        s_det = sem("d_expert_rows_transposed")
        s_deT = sem("d_expert_rowsT_ready")
        s_deh = sem("d_expert_hidden_ready")
        s_deth = sem("d_expert_tanh_ready")
        s_deg = sem("d_expert_gated_ready")
        s_dey = sem("d_expert_y_ready")
        s_dye = sem("d_expert_y_taken")
        s_dyst = sem("d_expert_y_stored")
        s_dgat = [sem(f"d_rows_gathered{j}") for j in range(2)]
        s_dgatf = sem("d_gather_buffer_free")
        s_x4 = sem("x4_ready")
        s_cstf = sem("c_stage_free")
        s_cwf = sem("c_head_weights_free")
        block = ctx.enter_context(nc.Block())

        def tile_of(t, n):
            return X[:, bass.ds(t + n, 1), :].rearrange("p a d -> p (a d)")

        RSQRT_STEPS = 11

        def rsqrt(dve, st):
            st.done(dve.tensor_scalar(rtmp[:, :].bitcast(I32), var[:, :].bitcast(I32), 1, None, ALU.logical_shift_right))
            st.sync()
            st.done(dve.tensor_scalar(rstd[:, :].bitcast(I32), rtmp[:, :].bitcast(I32), -1.0, float(0x5F3759DF),
                                      ALU.mult, ALU.add))
            for _ in range(3):
                st.sync()
                st.done(dve.tensor_tensor(rtmp[:, :], rstd[:, :], rstd[:, :], ALU.mult))
                st.sync()
                st.done(dve.scalar_tensor_tensor(rtmp[:, :], rtmp[:, :], -0.5, var[:, :], ALU.mult, ALU.mult))
                st.sync()
                st.done(dve.scalar_tensor_tensor(rstd[:, :], rtmp[:, :], 1.5, rstd[:, :], ALU.add, ALU.mult))
            st.sync()

        LN_STEPS = 2 * G + 1 + RSQRT_STEPS

        def normalise_group(dve, st, t, mul, add, xn_ready):
            for q in range(G):
                st.done(dve.bn_stats(stat[:, q, :], tile_of(t, q)))
            st.sync()
            dve.memset(rtmp[:, :], 0.0)
            for q in range(G):
                st.done(dve.bn_aggr(mv[:, q, :], stat[:, q, :]))
            st.sync()
            st.done(dve.tensor_scalar(var[:, :], mv[:, :, 1], mul, add, ALU.mult, ALU.add))
            st.sync()
            rsqrt(dve, st)
            for q in range(G):
                dve.tensor_scalar(xn[:, q, :], tile_of(t, q), mv[:, q, 0:1], rstd[:, q:q + 1],
                                  ALU.subtract, ALU.mult).then_inc(xn_ready, 1)

        def transpose_group(pe, bank):
            for k in range(KD):
                for q in range(G):
                    ins = pe.transpose(PS[:, bank + k, q * P:(q + 1) * P], xn[:, q, k * P:(k + 1) * P], ident[:, :])
            return ins

        def finish_stage(eng, n):
            eng.drain().then_inc(stage_end, 1)
            eng.wait_ge(stage_end, 5 * n)

        PAIR_BLOCKS = 2 * sum(4 * (c + 1) for c in range(NC2))
        GP = 2 * S // GT
        E0P = E0 // 4

        @block.sync
        def _(sp):
            for c in range(NG):
                if c >= GP:
                    sp.wait_ge(s_axn, (c - GP + 1) * G)
                sp.dma_start(X[:, c * G:(c + 1) * G, :], x_tiles[:, c * G:(c + 1) * G, :]).then_inc(s_x[c % GP], 16)
                if c == 0:
                    for k, w in enumerate((Wf, Wi, Wz, Wo)):
                        sp.dma_start(a_wraw[:, k, :], w).then_inc(s_aw, 16)
                    sp.dma_start(a_wpraw[:, :, :], Wp.rearrange("(k p) n -> p k n", p=P)).then_inc(s_aw, 16)
                    for k, b in enumerate((bf, bi, bz, bo)):
                        for h in range(2):
                            sp.dma_start(a_bias[h * N:(h + 1) * N, k:k + 1], b.rearrange("(n a) -> n a", a=1)).then_inc(s_aw, 16)
                    for h in range(2):
                        sp.dma_start(a_bp[h * N:h * N + 1, :], bp.rearrange("(a d) -> a d", a=1)).then_inc(s_aw, 16)
                    for k in range(KD):
                        sp.dma_start(a_lnw[:, k:k + 1], ln_w[k * P:(k + 1) * P].rearrange("(p a) -> p a", a=1)).then_inc(s_aw, 16)
                        sp.dma_start(a_lnb[:, k:k + 1], ln_b[k * P:(k + 1) * P].rearrange("(p a) -> p a", a=1)).then_inc(s_aw, 16)
            sp.wait_ge(s_const, 1)
            with sp.Fori(0, E1 * C1 // P) as r:
                sp.dma_start(routed1[bass.ds(r * P, P), :], zeros[:, :]).then_inc(s_dz, 16)
            with sp.Fori(0, E0) as e:
                sp.wait_ge(s_brawf, e + 1)
                sp.dma_start(b_raw[:, :, :], w12[bass.ds(e, 1), :, :].rearrange("e (a p) d -> p (e a) d", p=P)).then_inc(s_braw, 16)
                sp.wait_ge(s_braw3f, e + 1)
                sp.dma_start(b_raw3[:, :, :], w3[bass.ds(e, 1), :, :].rearrange("e (a p) h -> p (e a) h", p=P)).then_inc(s_braw3, 16)
            finish_stage(sp, 1)
            sp.dma_start(b_gw[:, :], gate0).then_inc(s_bw, 16)
            sp.wait_ge(s_bplan, 1)
            for e in range(E0):
                row = sp.value_load(b_zrowi[0:1, e:e + 1], min_val=0, max_val=E0 * REGION - P)
                sp.dma_start(routed0[bass.ds(row, P), :], zeros[:, :]).then_inc(s_bzero, 16)
            sp.wait_ge(s_bzero, 16 * E0)
            sp.wait_ge(s_bscat, 16 * NT * K0)
            with sp.Fori(0, TILES0 // 2) as i:
                for j in range(2):
                    row = sp.value_load(b_rowi[0:1, bass.ds(i * 2 + j, 1)], min_val=0, max_val=E0 * REGION - P)
                    sp.wait_ge(s_binf, i * 2 + (j + 1))
                    sp.dma_start(b_xt[:, j, :], routed0[bass.ds(row, P), :]).then_inc(s_bin[j], 16)
            finish_stage(sp, 2)
            sp.dma_start(c_qkraw[0:DQ, :, :], Q).then_inc(s_cl, 16)
            sp.dma_start(c_qkraw[DQ:2 * DQ, :, :], K).then_inc(s_cl, 16)
            sp.dma_start(c_vraw[:, :, :], V).then_inc(s_cl, 16)
            sp.dma_start(c_wraw[:, :, :, :], W.rearrange("(k p) v h -> p k v h", p=P)).then_inc(s_cl, 16)
            finish_stage(sp, 3)
            sp.dma_start(d_raw[:, 0, :], sw1).then_inc(s_dl, 16)
            sp.dma_start(d_raw[:, 1, :], sw3).then_inc(s_dl, 16)
            sp.dma_start(d_raw2[:, :, :], sw2.rearrange("(k p) i -> p k i", p=P)).then_inc(s_dl, 16)
            sp.dma_start(d_gwraw[:, :], gate1).then_inc(s_dl, 16)
            sp.dma_start(d_bias[:, :], bias1.rearrange("(a e) -> a e", a=1).broadcast_to([P, E1])).then_inc(s_dl, 16)
            sp.wait_ge(s_dscat, 16 * NT * K1)
            with sp.Fori(0, E1 // 2) as i:
                for j in range(2):
                    sp.wait_ge(s_dinf, i * 2 + (j + 1))
                    e = i * 2 + j
                    sp.dma_start(d_wb[:, j, 0:D].rearrange("p (k i) -> p k i", k=KD),
                                 W1[bass.ds(e, 1), :, :].rearrange("e (k p) i -> p (e k) i", p=P)).then_inc(s_din[j], 16)
                    sp.dma_start(d_wb[:, j, D:2 * D].rearrange("p (k i) -> p k i", k=KD),
                                 W3[bass.ds(e, 1), :, :].rearrange("e (k p) i -> p (e k) i", p=P)).then_inc(s_din[j], 16)
                    sp.dma_start(d_wb[:, j, 2 * D:3 * D], W2[bass.ds(e, 1), :, :].rearrange("e i d -> i (e d)")).then_inc(s_din[j], 16)
                    sp.dma_start(d_xe[:, j, :, :], routed1[bass.ds(e * C1, C1), :].rearrange("(a p) d -> p a d", p=P)).then_inc(s_din[j], 16)
            with sp.Fori(0, NG) as g:
                sp.wait_ge(s_x4, g * G + G)
                sp.dma_start(out_tiles[:, bass.ds(g * G, G), :], X[:, bass.ds(g * G, G), :]).then_inc(s_out, 16)
            sp.wait_ge(s_out, 16 * NG)

        @block.gpsimd
        def _(pool):
            st = Steps(pool, s_pool)
            st.done(pool.memset(ident[:, :], 0.0))
            st.done(pool.memset(identb[:, :], 0.0))
            st.done(pool.memset(ones[:, :], 1.0))
            st.done(pool.memset(onesb[:, :], 1.0))
            st.done(pool.memset(tri[:, :], 1.0))
            st.done(pool.memset(zeros[:, :], 0.0))
            st.done(pool.iota(iota[:, :], pattern=[[1, P]], base=0, channel_multiplier=0,
                              allow_small_or_imprecise_dtypes=True))
            st.sync()
            for m in (ident, identb):
                st.done(pool.affine_select(out=m[:, :], in_=m[:, :], compare_op=ALU.not_equal, fill=1.0,
                                           base=0, pattern=[[-1, P]], channel_multiplier=1))
            st.done(pool.affine_select(out=tri[:, :], in_=tri[:, :], compare_op=ALU.is_gt, fill=0.0,
                                       base=0, pattern=[[1, P]], channel_multiplier=-1))
            st.sync()
            pool.sem_inc(s_const, 1)
            finish_stage(pool, 1)
            with pool.Fori(0, NG) as g:
                pool.wait_ge(s_bslot, g + 1)
                pool.sem_inc(s_pass, 1)
                for q in range(G):
                    for k in range(K0):
                        pool.indirect_dma_start(
                            routed0, bass.IndirectOffsetOnAxis(ap=b_slot[:, q, k:k + 1], axis=0),
                            xn[:, q, :], None).then_inc(s_bscat, 16)
                pool.wait_ge(s_bscat, g * (16 * G * K0) + 16 * G * K0)
                pool.sem_inc(s_bxnf, 1)
            pool.wait_ge(s_bst, 16 * TILES0)
            pool.wait_ge(s_bplan, 2)
            with pool.Fori(0, NT // 2) as i:
                st.loop(i, NT // 2, 2)
                for j in range(2):
                    pool.wait_ge(s_bgatf, i * 2 + (j + 1))
                    pool.sem_inc(s_pass, 1)
                    st.done(pool.tensor_copy(b_gi[:, j, :], b_gix[:, bass.ds(i * 2 + j, 1), :].rearrange("p a k -> p (a k)")))
                    st.sync()
                    pool.sem_inc(s_pass, 1)
                    for k in range(K0):
                        pool.indirect_dma_start(
                            b_gat[:, j, k, :], None, expert0,
                            bass.IndirectOffsetOnAxis(ap=b_gi[:, j, k:k + 1], axis=0)).then_inc(s_bgat[j], 16)
                st.end()
            finish_stage(pool, 2)
            st.done(pool.memset(c_maskq[:, :], 0.0))
            st.done(pool.memset(c_maskk[:, :], 0.0))
            st.sync()
            st.done(pool.affine_select(out=c_maskq[:, :], in_=c_maskq[:, :], compare_op=ALU.is_ge, fill=1.0,
                                       base=0, pattern=[[-1, P]], channel_multiplier=1))
            st.done(pool.affine_select(out=c_maskk[:, :], in_=c_maskk[:, :], compare_op=ALU.is_ge, fill=1.0,
                                       base=0, pattern=[[1, P]], channel_multiplier=-1))
            st.sync()
            pool.sem_inc(s_cset, 1)
            pool.wait_ge(s_cl, 16 * 4)
            with pool.Fori(0, NH) as h:
                pool.wait_ge(s_cstf, h + 1)
                pool.sem_inc(s_pass, 1)
                pool.tensor_copy(c_qkst[:, :], c_qkraw[:, :, bass.ds(h, 1)].rearrange("p d a -> p (d a)")).then_inc(s_cst, 1)
                pool.tensor_copy(c_vst[:, :], c_vraw[:, :, bass.ds(h, 1)].rearrange("p d a -> p (d a)")).then_inc(s_cst, 1)
            with pool.Fori(0, NPAIR) as hp:
                pool.wait_ge(s_cstf, hp + (NH + 1))
                pool.sem_inc(s_pass, 1)
                for h in range(2):
                    pool.tensor_copy(c_wst[:, :, h, :], c_wraw[:, :, :, bass.ds(hp * 2 + h, 1)].rearrange("p k v a -> p k (v a)")).then_inc(s_cst, 1)
            pool.wait_ge(s_cwl, 2 * NH)
            with pool.Fori(0, B) as b:
                with pool.Fori(0, NPAIR) as hp:
                    for h in range(2):
                        pool.wait_ge(s_cwf, b * NH + hp * 2 + (h + 1))
                        pool.sem_inc(s_pass, 1)
                        for n in range(2):
                            pool.tensor_copy(c_st[n][:, h, :, :], c_wqk[n][:, :, bass.ds(hp * 2 + h, 1), :].rearrange("p k a c -> p k (a c)"))\
                                .then_inc(s_cw, 1)
            finish_stage(pool, 3)
            pool.wait_ge(s_dl, 16 * 5)
            pool.tensor_copy(d_rawf[:, :, :], d_raw[:, :, :]).then_inc(s_dcast, 1)
            pool.tensor_copy(d_raw2f[:, :, :], d_raw2[:, :, :]).then_inc(s_dcast, 1)
            pool.tensor_copy(d_gwf[:, :], d_gwraw[:, :]).then_inc(s_dcast, 1)
            pool.wait_ge(s_dz, 16 * (E1 * C1 // P))
            with pool.Fori(0, NG) as g:
                pool.wait_ge(s_dslot, g + 1)
                pool.sem_inc(s_pass, 1)
                for q in range(G):
                    for k in range(K1):
                        pool.indirect_dma_start(
                            routed1, bass.IndirectOffsetOnAxis(ap=d_slot[:, q, k:k + 1], axis=0),
                            xn[:, q, :], None, bounds_check=E1 * C1 - 1, oob_is_err=False).then_inc(s_dscat, 16)
                pool.wait_ge(s_dscat, g * (16 * G * K1) + 16 * G * K1)
                pool.sem_inc(s_dxnf, 1)
            with pool.Fori(0, E1 // 2) as i:
                for j in range(2):
                    pool.wait_ge(s_din[j], i * 64 + 64)
                    pool.sem_inc(s_pass, 1)
                    pool.tensor_copy(d_wf[:, j, :], d_wb[:, j, :]).then_inc(s_dec, 1)
            pool.wait_ge(s_dyst, 16 * E1)
            with pool.Fori(0, NT // 2) as i:
                st.loop(i, NT // 2, 2)
                for j in range(2):
                    pool.wait_ge(s_dgatf, i * 2 + (j + 1))
                    pool.sem_inc(s_pass, 1)
                    st.done(pool.tensor_copy(d_gi[:, j, :], d_gix[:, bass.ds(i * 2 + j, 1), :].rearrange("p a k -> p (a k)")))
                    st.sync()
                    pool.sem_inc(s_pass, 1)
                    for k in range(K1):
                        pool.indirect_dma_start(
                            d_gat[:, j, k, :], None, expert1,
                            bass.IndirectOffsetOnAxis(ap=d_gi[:, j, k:k + 1], axis=0)).then_inc(s_dgat[j], 16)
                st.end()

        def take_experts(act, e0):
            with act.Fori(0, E0P) as f:
                for k in range(KD):
                    act.wait_ge(s_btw, (e0 + f) * 3 + (1 + k))
                    act.activation(b_w12T[:, k, bass.ds((e0 + f) * (2 * H0), 2 * H0)],
                                   PS[:, 2 * k:2 * k + 2, :].rearrange("p a n -> p (a n)"), ACT.Copy).then_inc(s_bwe, 1)
                act.wait_ge(s_btw, (e0 + f) * 3 + 3)
                for k in range(KH):
                    act.activation(b_w3T[:, k, bass.ds((e0 + f) * D, D)], PS[:, 4 + k // 2, (k % 2) * D:(k % 2 + 1) * D],
                                   ACT.Copy).then_inc(s_bwe, 1)

        @block.scalar
        def _(act):
            st = Steps(act, s_act)
            act.wait_ge(s_awt, 1)
            st.done(act.activation(a_wT[:, :, :, :].rearrange("p k g n -> p (k g n)"), PS[:, 0, 0:KD * 4 * N], ACT.Copy))
            for h in range(2):
                st.done(act.activation(a_wpT[h * N:(h + 1) * N, :], PS[0:N, 1, 0:D], ACT.Copy, scale=0.5))
            act.wait_ge(s_aw, 16 * 19)
            st.done(act.activation(a_hbo[:, :], a_bias[:, 3:4], ACT.Copy, scale=0.5))
            st.sync()
            act.sem_inc(s_awe, 1)
            act.sem_inc(s_afree, 1)
            with act.Fori(0, B // 2) as p:
                for g in range(GP):
                    act.wait_ge(s_atp, p * GP + (g + 1))
                    for k in range(KD):
                        act.activation(a_xT[:, k, g * GT:(g + 1) * GT], PS[:, 6 + k, :], ACT.Identity,
                                       bias=a_lnb[:, k:k + 1], scale=a_lnw[:, k:k + 1]).then_inc(s_axT, 1)
                take_experts(act, p * (2 * E0P))
                act.wait_ge(s_afree, p + 1)
                for g in range(4):
                    act.wait_ge(s_agate, p * 4 + (g + 1))
                    dst = (a_lf, a_li, a_z, a_o)[g]
                    fn = (ACT.Identity, ACT.Identity, ACT.Tanh, ACT.Tanh)[g]
                    src = PS[:, 2 * (g % 2):2 * (g % 2) + 2, :].rearrange("p a n -> p (a n)")
                    act.activation(dst[:, :], src, fn, bias=a_hbo[:, 0:1] if g == 3 else a_bias[:, g:g + 1],
                                   scale=0.5 if g == 3 else 1.0).then_inc(s_agev, 1)
                act.wait_ge(s_ascan, p * 3 + 1)
                act.activation(a_fs[:, :], a_fs[:, :], ACT.Exp).then_inc(s_aexp, 1)
                act.wait_ge(s_ascan, p * 3 + 2)
                act.activation(a_is[:, :], a_is[:, :], ACT.Exp).then_inc(s_aexp, 1)
                take_experts(act, p * (2 * E0P) + E0P)
                act.wait_ge(s_ascan, p * 3 + 3)
                act.activation(a_c[:, :], a_c[:, :], ACT.Tanh).then_inc(s_aexp, 1)
            finish_stage(act, 1)
            act.wait_ge(s_bgt, 1)
            act.activation(b_gwT[:, :, :].rearrange("p k e -> p (k e)"), PS[:, 6, 0:KD * E0], ACT.Copy).then_inc(s_bge, 1)
            with act.Fori(0, NG) as g:
                act.wait_ge(s_btp, g + 1)
                act.activation(b_xT[:, :, :].rearrange("p k t -> p (k t)"),
                               PS[:, 6:8, :].rearrange("p a n -> p (a n)"), ACT.Copy).then_inc(s_bxT, 1)
                act.wait_ge(s_bgap, g + 1)
                act.activation(b_ex[:, :], b_gap[:, :], ACT.Exp).then_inc(s_bex, 1)
            act.sem_inc(s_bystf, 2)
            with act.Fori(0, TILES0 // 2) as i:
                for j in range(2):
                    act.wait_ge(s_btt, i * 2 + (j + 1))
                    act.activation(b_tT[:, j, :, :].rearrange("p k t -> p (k t)"), PS[:, 1 + 2 * j, 0:D],
                                   ACT.Copy).then_inc(s_btT, 1)
                for j in range(2):
                    act.wait_ge(s_bh, i * 2 + (j + 1))
                    act.activation(b_sg[:, j, :], PS[:, 1 + 2 * j, :], ACT.Tanh, scale=0.5).then_inc(s_bsg, 1)
                for j in range(2):
                    act.wait_ge(s_bht, i * 2 + (j + 1))
                    act.activation(b_hT[:, j, :, :].rearrange("p k t -> p (k t)"), PS[:, 2 + 2 * j, :], ACT.Copy).then_inc(s_bhT, 1)
                for j in range(2):
                    act.wait_ge(s_by, i * 2 + (j + 1))
                    act.wait_ge(s_bystf, i * 2 + (j + 1))
                    act.activation(b_y[:, j, :], PS[:, 5 + j, 0:D], ACT.Copy).then_inc(s_bye, 1)
                    act.wait_ge(s_bye, i * 2 + (j + 1))
                    act.dma_start(expert0[bass.ds((i * 2 + j) * P, P), :], b_y[:, j, :]).then_inc(s_bst, 16)
                act.wait_ge(s_bst, i * 32 + 32)
                act.sem_inc(s_bystf, 2)
            finish_stage(act, 2)
            with act.Fori(0, NH) as h:
                act.wait_ge(s_cwt, h * 2 + 1)
                act.activation(c_wqk[0][:, :, bass.ds(h, 1), :].rearrange("p k a c -> p k (a c)"),
                               PS[:, 0, 0:KD * P].rearrange("p (k c) -> p k c", k=KD), ACT.Copy).then_inc(s_cwh, 1)
                act.wait_ge(s_cwt, h * 2 + 2)
                act.activation(c_wv[0][:, :, bass.ds(h * DQ, DQ)],
                               PS[:, 1, 0:KD * DQ].rearrange("p (k c) -> p k c", k=KD), ACT.Copy).then_inc(s_cwh, 1)
            with act.Fori(0, NPAIR) as hp:
                act.wait_ge(s_cwt, hp + (2 * NH + 1))
                act.activation(c_wo[:, bass.ds(hp, 1), :].rearrange("p a d -> p (a d)"), PS[:, 2, 0:D], ACT.Copy).then_inc(s_cwh, 1)
            act.wait_ge(s_cset, 2)
            with act.Fori(0, B) as b:
                act.wait_ge(s_cxf, b + 1)
                for g in range(S // GT):
                    act.wait_ge(s_ctp, b * (S // GT) + (g + 1))
                    for k in range(KD):
                        act.activation(c_xT[0][:, k, g * GT:(g + 1) * GT], PS[:, k, :], ACT.Copy).then_inc(s_cxh, 1)
                act.wait_ge(s_cyf, b + 1)
                with act.Fori(0, NPAIR) as hp:
                    pair = b * NPAIR + hp
                    for h in range(2):
                        act.wait_ge(s_cqk, pair * 2 + (h + 1))
                        qk = PS[:, 0:2, :].rearrange("p a n -> p (a n)")
                        for dst, src in ((c_q1[h][0:DQ, :], qk[0:DQ]), (c_q1[h][DQ:P, :], qk[0:DQ]),
                                         (c_k1[h][0:DQ, :], qk[DQ:P]), (c_k2[h][0:DQ, :], qk[DQ:P])):
                            act.activation(dst, src, ACT.Copy).then_inc(s_cqs, 1)
                    for r in range(2):
                        act.wait_ge(s_cv, pair * 2 + (r + 1))
                        for h in range(2):
                            src = PS[:, (2, 7)[r], :].rearrange("p (a c) -> p a c", a=QT // 2)
                            act.activation(c_v[h][:, r * (QT // 2):(r + 1) * (QT // 2), 0:DQ], src[:, :, h * DQ:(h + 1) * DQ],
                                           ACT.Copy).then_inc(s_cve, 1)
                    n = 0
                    for h in range(2):
                        act.wait_ge(s_cmT, pair * 2 + (h + 1))
                        act.activation(c_q2[h][DQ:DQ + 1, :], PS[0:1, 0:2, :].rearrange("p a n -> p (a n)"), ACT.Copy,
                                       scale=-1.0).then_inc(s_cm, 1)
                        for c in range(NC2):
                            for j in range(4 * (c + 1)):
                                off = max(0, j * P - c * 512)
                                act.wait_ge(s_cT, pair * PAIR_BLOCKS + (n + 1))
                                act.wait_ge(s_cPf, pair * PAIR_BLOCKS + (n + 1))
                                act.activation(c_p[:, n % 4, 0:512 - off], PS[:, 3 + n % 4, 0:512 - off], ACT.Exp,
                                               scale=ATT_SCALE).then_inc(s_cP, 1)
                                n += 1
                            act.wait_ge(s_cO, pair * (2 * NC2) + (h * NC2 + c + 1))
                            act.activation(c_yT[h * DQ:(h + 1) * DQ, bass.ds(hp, 1), c * 512:(c + 1) * 512].rearrange("p a n -> p (a n)"),
                                           PS[0:DQ, (7, 2)[c % 2], :], ACT.Copy, scale=Z_SCALE).then_inc(s_cOy, 1)
            finish_stage(act, 3)
            act.wait_ge(s_dwt, 1)
            st.done(act.activation(d_gwT[:, :, :].rearrange("p k e -> p (k e)"), PS[:, 0, 0:KD * E1], ACT.Copy))
            st.done(act.activation(d_s1T[:, :, :, :].rearrange("p k a i -> p (k a i)"), PS[:, 1, 0:KD * 2 * I1], ACT.Copy))
            st.done(act.activation(d_s2T[:, :], PS[:, 2, 0:D], ACT.Copy))
            st.sync()
            act.sem_inc(s_dwe, 1)
            with act.Fori(0, NG) as g:
                act.wait_ge(s_dtp, g + 1)
                act.activation(d_xT[:, :, :].rearrange("p k t -> p (k t)"),
                               PS[:, 6:8, :].rearrange("p a n -> p (a n)"), ACT.Copy).then_inc(s_dxT, 1)
                act.wait_ge(s_dsc, g + 1)
                act.activation(d_th[:, :, :].rearrange("p g e -> p (g e)"), PS[:, 0, 0:G * E1], ACT.Tanh, scale=0.5).then_inc(s_dth, 1)
                act.wait_ge(s_dsh, g + 1)
                act.activation(d_sth[:, :], PS[:, 2, :], ACT.Tanh, scale=0.5).then_inc(s_dst, 1)
            with act.Fori(0, E1 // 2) as i:
                for j in range(2):
                    act.wait_ge(s_det, i * 2 + (j + 1))
                    act.activation(d_xeT[:, j, :, :].rearrange("p k c -> p (k c)"), PS[:, j, :], ACT.Copy).then_inc(s_deT, 1)
                for j in range(2):
                    act.wait_ge(s_deh, i * 2 + (j + 1))
                    act.activation(d_eth[:, j, :], PS[:, 2 + j, 0:C1], ACT.Tanh, scale=0.5).then_inc(s_deth, 1)
                for j in range(2):
                    act.wait_ge(s_dey, i * 2 + (j + 1))
                    act.activation(d_y[:, j, :, :].rearrange("p a d -> p (a d)"), PS[:, 4 + j, :], ACT.Copy).then_inc(s_dye, 1)
                    act.wait_ge(s_dye, i * 2 + (j + 1))
                    act.dma_start(expert1[bass.ds((i * 2 + j) * C1, C1), :].rearrange("(a p) d -> p a d", p=P), d_y[:, j, :, :]).then_inc(s_dyst, 16)
                act.wait_ge(s_dyst, i * 32 + 32)

        @block.vector
        def _(dve):
            st = Steps(dve, s_dve)
            st.done(dve.memset(a_m[:, 0:1], 0.0))
            with dve.Fori(0, B // 2) as p:
                st.loop(p, B // 2, GP * LN_STEPS + 9)
                for g in range(GP):
                    dve.wait_ge(s_x[g], p * 16 + 16)
                    if g:
                        dve.wait_ge(s_atp, p * GP + g)
                    normalise_group(dve, st, p * (GP * G) + g * G, 1.0 + EPS, EPS * EPS, s_axn)
                dve.wait_ge(s_agev, p * 4 + 1)
                st.done(dve.tensor_scalar(a_lf[:, :], a_lf[:, :], -20.0, 20.0, ALU.max, ALU.min))
                dve.wait_ge(s_agev, p * 4 + 2)
                st.done(dve.tensor_scalar(a_li[:, :], a_li[:, :], -20.0, 20.0, ALU.max, ALU.min))
                st.sync()
                st.done(dve.tensor_tensor_scan(a_m[:, 1:], a_lf[:, :], a_li[:, :], 0.0, ALU.add, ALU.max))
                st.sync()
                st.done(dve.tensor_tensor(a_fs[:, :], a_m[:, 0:S], a_lf[:, :], ALU.add))
                st.sync()
                st.done(dve.tensor_tensor(a_fs[:, :], a_fs[:, :], a_m[:, 1:], ALU.subtract))
                st.sync()
                dve.sem_inc(s_ascan, 1)
                st.done(dve.tensor_tensor(a_is[:, :], a_li[:, :], a_m[:, 1:], ALU.subtract))
                st.sync()
                dve.sem_inc(s_ascan, 1)
                dve.wait_ge(s_agev, p * 4 + 4)
                dve.wait_ge(s_aexp, p * 3 + 2)
                st.done(dve.tensor_tensor(a_is[:, :], a_is[:, :], a_z[:, :], ALU.mult))
                st.sync()
                st.done(dve.tensor_tensor_scan(a_c[:, :], a_fs[:, :], a_is[:, :], 0.0, ALU.mult, ALU.add))
                st.sync()
                dve.sem_inc(s_ascan, 1)
                dve.wait_ge(s_aexp, p * 3 + 3)
                st.done(dve.scalar_tensor_tensor(a_h[:, :], a_o[:, :], 1.0, a_c[:, :], ALU.add, ALU.mult))
                st.sync()
                dve.sem_inc(s_ah, 1)
                for n in range(2 * QT):
                    dve.wait_ge(s_ay, p * (2 * QT) + (n + 1))
                    dve.tensor_tensor(tile_of(p * (2 * QT), n), PS[:, 4 + n % 2, 0:D], tile_of(p * (2 * QT), n),
                                      ALU.add).then_inc(s_x1, 1)
                st.end()
                dve.sem_inc(s_afree, 1)
            finish_stage(dve, 1)
            st.done(dve.memset(b_sum[:, :], 0.0))
            st.sync()
            dve.sem_inc(s_bxnf, 1)
            with dve.Fori(0, NG) as g:
                st.loop(g, NG, LN_STEPS + 2 * G + 3 + 1 + G * K0 + 2 + K0 + 3 + 1 + 4)
                dve.wait_ge(s_x1, g * G + G)
                dve.wait_ge(s_bxnf, g + 1)
                normalise_group(dve, st, g * G, 1.0, EPS, s_bxn)
                dve.wait_ge(s_bsc, g + 1)
                st.done(dve.tensor_copy(b_s8[:, :, :].rearrange("p g e -> p (g e)"), PS[:, 0, 0:G * E0]))
                st.sync()
                dve.memset(rtmp[:, :], 0.0)
                for q in range(G):
                    st.done(dve.max(b_top[:, q, :], b_s8[:, q, :]))
                st.sync()
                dve.memset(rtmp[:, :], 0.0)
                for q in range(G):
                    st.done(dve.max_index(b_ix[:, q, :], b_top[:, q, :], b_s8[:, q, :]))
                st.done(dve.tensor_tensor(b_gap[:, :], b_top[:, :, 1], b_top[:, :, 0], ALU.subtract))
                st.sync()
                dve.sem_inc(s_bgap, 1)
                st.done(dve.tensor_copy(b_idx[:, :, :], b_ix[:, :, 0:K0]))
                st.sync()
                st.done(dve.tensor_copy(b_idxA[:, bass.ds(g * G, G), :], b_idx[:, :, :]))
                for q in range(G):
                    for k in range(K0):
                        st.done(dve.tensor_scalar(b_oh[:, q, k, :], iota[:, 0:E0], b_idx[:, q, k:k + 1], None, ALU.is_equal))
                st.sync()
                st.done(dve.tensor_tensor(b_ohs[:, :, :], b_oh[:, :, 0, :], b_oh[:, :, 1, :], ALU.add))
                st.sync()
                dve.sem_inc(s_boh, 1)
                st.done(dve.tensor_reduce(b_gsum[:, :], b_ohs[:, :, :].rearrange("p g e -> p e g"), AX_X, ALU.add))
                dve.wait_ge(s_bpre, g + 1)
                pre = PS[:, 1, 0:G * E0].rearrange("p (g e) -> p g e", g=G)
                for k in range(K0):
                    st.done(dve.tensor_tensor(b_tmp[:, :, k, :], b_oh[:, :, k, :], pre, ALU.mult))
                st.sync()
                st.done(dve.tensor_tensor(b_sum[:, :], b_sum[:, :], b_gsum[:, :], ALU.add))
                st.done(dve.tensor_reduce(b_pos[:, :, :].rearrange("p g k -> p (g k)"),
                                          b_tmp[:, :, :, :].rearrange("p g k e -> p (g k) e"), AX_X, ALU.add))
                st.sync()
                st.done(dve.scalar_tensor_tensor(b_slot[:, :, :], b_idx[:, :, :], float(REGION), b_pos[:, :, :],
                                                 ALU.mult, ALU.add))
                st.sync()
                dve.sem_inc(s_bslot, 1)
                st.done(dve.tensor_copy(b_posA[:, bass.ds(g * G, G), :], b_pos[:, :, :]))
                dve.wait_ge(s_bex, g + 1)
                st.done(dve.tensor_scalar(b_den[:, :], b_ex[:, :], 1.0, None, ALU.add))
                st.sync()
                st.done(dve.reciprocal(b_den[:, :], b_den[:, :]))
                st.sync()
                st.done(dve.tensor_copy(b_prA[:, bass.ds(g * G, G), 0], b_den[:, :]))
                st.done(dve.tensor_tensor(b_prA[:, bass.ds(g * G, G), 1], b_den[:, :], b_ex[:, :], ALU.mult))
                st.sync()
                st.end()
            dve.sem_inc(s_boh, 1)
            dve.wait_ge(s_bcnt, 1)
            st.done(dve.tensor_copy(b_cnt[:, :], PS[:, 0, 0:E0]))
            st.sync()
            st.done(dve.tensor_scalar(b_nti[:, :], b_cnt[:, :], float(P - 1), None, ALU.add))
            st.done(dve.scalar_tensor_tensor(b_zrow[:, :], iota[:, 0:E0], float(REGION), b_cnt[:, :], ALU.mult, ALU.add))
            st.sync()
            st.done(dve.tensor_copy(b_zrowi[:, :], b_zrow[:, :]))
            st.done(dve.tensor_scalar(b_nti[:, :], b_nti[:, :], P.bit_length() - 1, None, ALU.logical_shift_right))
            st.sync()
            st.done(dve.tensor_copy(b_nt[:, :], b_nti[:, :]))
            st.sync()
            st.done(dve.tensor_tensor_scan(b_end[:, :], ones[:, 0:E0], b_nt[:, :], 0.0, ALU.mult, ALU.add))
            st.sync()
            st.done(dve.tensor_tensor(b_start[:, :], b_end[:, :], b_nt[:, :], ALU.subtract))
            tiles = iota[:, 0:TILES0]
            st.done(dve.memset(b_te[:, :], 0.0))
            st.done(dve.memset(b_ts[:, :], 0.0))
            for e in range(E0 - 1):
                st.sync()
                st.done(dve.tensor_scalar(b_tt[:, :], tiles, b_end[:, e:e + 1], b_end[:, e:e + 1], ALU.is_ge, ALU.mult))
                st.done(dve.scalar_tensor_tensor(b_te[:, :], tiles, b_end[:, e:e + 1], b_te[:, :], ALU.is_ge, ALU.add))
                st.sync()
                st.done(dve.tensor_tensor(b_ts[:, :], b_ts[:, :], b_tt[:, :], ALU.max))
            st.sync()
            st.done(dve.tensor_copy(b_tei[:, :], b_te[:, :]))
            st.done(dve.tensor_tensor(b_tt[:, :], tiles, b_ts[:, :], ALU.subtract))
            st.sync()
            st.done(dve.tensor_scalar(b_tt[:, :], b_tt[:, :], float(P), None, ALU.mult))
            st.sync()
            st.done(dve.scalar_tensor_tensor(b_tt[:, :], b_te[:, :], float(REGION), b_tt[:, :], ALU.mult, ALU.add))
            st.sync()
            st.done(dve.tensor_scalar(b_ts[:, :], tiles, b_end[:, E0 - 1:E0], None, ALU.is_lt))
            st.done(dve.tensor_scalar(b_tt[:, :], b_tt[:, :], b_zrow[:, E0 - 1:E0], None, ALU.subtract))
            st.sync()
            st.done(dve.tensor_tensor(b_tt[:, :], b_tt[:, :], b_ts[:, :], ALU.mult))
            st.sync()
            st.done(dve.tensor_scalar(b_rowi[:, :], b_tt[:, :], b_zrow[:, E0 - 1:E0], None, ALU.add))
            st.sync()
            dve.sem_inc(s_bplan, 1)
            for e in range(E0):
                st.done(dve.tensor_scalar(b_gtmp[:, :, :], b_idxA[:, :, :], float(e), b_start[:, e:e + 1],
                                          ALU.is_equal, ALU.mult))
                st.sync()
                st.done(dve.scalar_tensor_tensor(b_posA[:, :, :], b_gtmp[:, :, :], float(P), b_posA[:, :, :],
                                                 ALU.mult, ALU.add))
                st.sync()
            st.done(dve.tensor_copy(b_gix[:, :, :], b_posA[:, :, :]))
            st.sync()
            dve.sem_inc(s_bplan, 1)
            with dve.Fori(0, TILES0 // 2) as i:
                st.loop(i, TILES0 // 2, 2)
                for j in range(2):
                    dve.wait_ge(s_bsg, i * 2 + (j + 1))
                    st.done(dve.scalar_tensor_tensor(b_hid[:, j, :], b_sg[:, j, :], 1.0, PS[:, 1 + 2 * j, :], ALU.add, ALU.mult))
                    st.sync()
                    dve.scalar_tensor_tensor(b_hid[:, j, :], b_hid[:, j, :], 0.5, PS[:, 2 + 2 * j, :], ALU.mult,
                                             ALU.mult).then_inc(s_bhid, 1)
                st.end()
            dve.sem_inc(s_bgatf, 2)
            with dve.Fori(0, NT // 2) as i:
                st.loop(i, NT // 2, 2)
                for j in range(2):
                    t = tile_of(i * 2, j)
                    dve.wait_ge(s_bgat[j], i * (16 * K0) + 16 * K0)
                    st.done(dve.scalar_tensor_tensor(t, b_gat[:, j, 0, :], b_prA[:, bass.ds(i * 2 + j, 1), 0], t, ALU.mult, ALU.add))
                    st.sync()
                    dve.scalar_tensor_tensor(t, b_gat[:, j, 1, :], b_prA[:, bass.ds(i * 2 + j, 1), 1], t, ALU.mult,
                                             ALU.add).then_inc(s_x2, 1)
                    dve.wait_ge(s_x2, i * 2 + (j + 1))
                    dve.sem_inc(s_bgatf, 1)
                st.end()
            finish_stage(dve, 2)
            with dve.Fori(0, NH) as h:
                dve.wait_ge(s_cwh, h * 2 + 1)
                ws = [w[:, :, bass.ds(h, 1), :].rearrange("p k a c -> p k (a c)") for w in c_wqk]
                dve.tensor_tensor(ws[1], PS[:, 0, 0:KD * P].rearrange("p (k c) -> p k c", k=KD), ws[0].bitcast(F32),
                                  ALU.subtract).then_inc(s_cwl, 1)
                dve.wait_ge(s_cwh, h * 2 + 2)
                ws = [w[:, :, bass.ds(h * DQ, DQ)] for w in c_wv]
                dve.tensor_tensor(ws[1], PS[:, 1, 0:KD * DQ].rearrange("p (k c) -> p k c", k=KD), ws[0].bitcast(F32),
                                  ALU.subtract).then_inc(s_cwl, 1)
            dve.wait_ge(s_cset, 1)
            for m in (c_maskq, c_maskk):
                st.done(dve.tensor_scalar(m[:, :], m[:, :], BIG, None, ALU.mult))
            for h in range(2):
                st.done(dve.memset(c_q2[h][DQ:P, :].bitcast(F32), 0.0))
                st.done(dve.memset(c_k2[h][DQ:P, :].bitcast(F32), 0.0))
                st.done(dve.memset(c_v[h][:, :, DQ:P], 1.0))
            st.sync()
            for h in range(2):
                st.done(dve.memset(c_k2[h][DQ:DQ + 1, :].bitcast(F32), 1.0))
            st.sync()
            dve.sem_inc(s_cset, 1)
            pairs = Steps(dve, s_dve2)
            with dve.Fori(0, B) as b:
                st.loop(b, B, (S // GT) * LN_STEPS)
                for g in range(S // GT):
                    dve.wait_ge(s_x2, b * QT + (g + 1) * G)
                    if g:
                        dve.wait_ge(s_ctp, b * (S // GT) + g)
                    normalise_group(dve, st, b * QT + g * G, 1.0, EPS, s_cxn)
                    for k in range(KD):
                        dve.wait_ge(s_cxh, b * (KD * S // GT) + g * KD + k + 1)
                        dve.tensor_tensor(c_xT[1][:, k, g * GT:(g + 1) * GT], PS[:, k, :],
                                          c_xT[0][:, k, g * GT:(g + 1) * GT].bitcast(F32), ALU.subtract).then_inc(s_cxl, 1)
                st.end()
                with dve.Fori(0, NPAIR) as hp:
                    pair = b * NPAIR + hp
                    pairs.loop(pair, B * NPAIR, NC2)
                    for h in range(2):
                        qk = PS[:, 0:2, :].rearrange("p a n -> p (a n)")
                        dve.wait_ge(s_cqs, pair * 8 + 4 * h + 4)
                        dve.tensor_tensor(c_q2[h][0:DQ, :], qk[0:DQ], c_q1[h][0:DQ, :].bitcast(F32), ALU.subtract).then_inc(s_cks, 1)
                        dve.tensor_tensor(c_k1[h][DQ:P, :], qk[DQ:P], c_k1[h][0:DQ, :].bitcast(F32), ALU.subtract).then_inc(s_cks, 1)
                    for h in range(2):
                        for t in range(QT):
                            dve.wait_ge(s_cS, pair * (2 * QT) + (h * QT + t + 1))
                            s = 3 + 2 * (t % 2)
                            dve.tensor_reduce(c_mx[h][:, t:t + 1], PS[:, s:s + 2, :].rearrange("p a n -> p (a n)")[:, 0:(t + 1) * P],
                                              AX_X, ALU.max).then_inc(s_cmx, 1)
                    for h in range(2):
                        for c in range(NC2):
                            dve.wait_ge(s_cO, pair * (2 * NC2) + (h * NC2 + c + 1))
                            dve.tensor_copy(c_den[h * DQ:(h + 1) * DQ, c, :], PS[DQ:P, (7, 2)[c % 2], :]).then_inc(s_cOd, 1)
                    for c in range(NC2):
                        dve.wait_ge(s_cOd, pair * (2 * NC2) + (NC2 + c + 1))
                        pairs.done(dve.reciprocal(c_den[:, c, :], c_den[:, c, :]))
                        pairs.sync()
                        dve.wait_ge(s_cOy, pair * (2 * NC2) + (NC2 + c + 1))
                        y = c_yT[:, bass.ds(hp, 1), c * 512:(c + 1) * 512].rearrange("p a n -> p (a n)")
                        dve.tensor_tensor(y, y, c_den[:, c, :], ALU.mult).then_inc(s_cyn, 1)
                    pairs.end()
                for t in range(QT):
                    dve.wait_ge(s_cz, b * QT + (t + 1))
                    dve.tensor_tensor(tile_of(b * QT, t), PS[:, 3 + t % 4, 0:D], tile_of(b * QT, t), ALU.add).then_inc(s_x3, 1)
            finish_stage(dve, 3)
            st.done(dve.memset(d_sum[:, :], 0.0))
            st.sync()
            dve.sem_inc(s_dxnf, 1)
            dve.wait_ge(s_dl, 16 * 5)
            with dve.Fori(0, NG) as g:
                st.loop(g, NG, LN_STEPS + 3 * G + 2 + G * K1 + 3 + 2 * K1 + 3 + 4 + 3 + 2 + G + 1 + 2)
                dve.wait_ge(s_x3, g * G + G)
                dve.wait_ge(s_dxnf, g + 1)
                normalise_group(dve, st, g * G, 1.0, EPS, s_dxn)
                dve.wait_ge(s_dth, g + 1)
                st.done(dve.tensor_scalar(d_sc[:, :, :], d_th[:, :, :], 0.5, 0.5, ALU.mult, ALU.add))
                st.sync()
                for q in range(G):
                    st.done(dve.tensor_tensor(d_sel[:, q, :], d_sc[:, q, :], d_bias[:, :], ALU.add))
                st.sync()
                dve.memset(rtmp[:, :], 0.0)
                for q in range(G):
                    st.done(dve.max(d_top[:, q, :], d_sel[:, q, :]))
                st.sync()
                dve.memset(rtmp[:, :], 0.0)
                for q in range(G):
                    st.done(dve.max_index(d_ix[:, q, :], d_top[:, q, :], d_sel[:, q, :]))
                st.sync()
                st.done(dve.tensor_copy(d_idx[:, :, :], d_ix[:, :, 0:K1]))
                st.sync()
                for q in range(G):
                    for k in range(K1):
                        st.done(dve.tensor_scalar(d_oh[:, q, k, :], iota[:, 0:E1], d_idx[:, q, k:k + 1], None, ALU.is_equal))
                st.sync()
                for q in range(G):
                    ins = dve.tensor_reduce(d_ohf[:, q, :], d_oh[:, q, :, :].rearrange("p k e -> p e k"), AX_X, ALU.add)
                    if q == G - 1:
                        st.done(ins)
                st.sync()
                st.done(dve.tensor_copy(d_ohs[:, :, :], d_ohf[:, :, :]))
                st.sync()
                dve.sem_inc(s_doh, 1)
                st.done(dve.tensor_reduce(d_gsum[:, :], d_ohs[:, :, :].rearrange("p g e -> p e g"), AX_X, ALU.add))
                dve.wait_ge(s_dpre, g + 1)
                pre = PS[:, 1, 0:G * E1].rearrange("p (g e) -> p g e", g=G)
                for k in range(K1):
                    st.done(dve.tensor_tensor(d_tmp[:, :, k, :], d_oh[:, :, k, :], pre, ALU.mult))
                    st.done(dve.tensor_tensor(d_tmp2[:, :, k, :], d_oh[:, :, k, :], d_sc[:, :, :], ALU.mult))
                st.sync()
                st.done(dve.tensor_tensor(d_sum[:, :], d_sum[:, :], d_gsum[:, :], ALU.add))
                for src, dst in ((d_tmp, d_pos), (d_tmp2, d_w)):
                    st.done(dve.tensor_reduce(dst[:, :, :].rearrange("p g k -> p (g k)"),
                                              src[:, :, :, :].rearrange("p g k e -> p (g k) e"), AX_X, ALU.add))
                st.sync()
                st.done(dve.tensor_reduce(d_ws[:, :], d_w[:, :, :], AX_X, ALU.add))
                st.done(dve.tensor_scalar(d_ok[:, :, :], d_pos[:, :, :], float(C1), None, ALU.is_lt))
                st.done(dve.tensor_scalar(d_cl[:, :, :], d_pos[:, :, :], float(C1 - 1), None, ALU.min))
                st.done(dve.tensor_scalar(d_skip[:, :, :], d_pos[:, :, :], float(C1), float(BIGSLOT), ALU.is_ge, ALU.mult))
                st.sync()
                st.done(dve.tensor_scalar(d_ws[:, :], d_ws[:, :], 1e-12, None, ALU.max))
                st.done(dve.tensor_tensor(d_skip[:, :, :], d_skip[:, :, :], d_pos[:, :, :], ALU.add))
                st.done(dve.scalar_tensor_tensor(d_gix[:, bass.ds(g * G, G), :], d_idx[:, :, :], float(C1), d_cl[:, :, :], ALU.mult, ALU.add))
                st.sync()
                st.done(dve.scalar_tensor_tensor(d_slot[:, :, :], d_idx[:, :, :], float(C1), d_skip[:, :, :], ALU.mult, ALU.add))
                st.done(dve.reciprocal(d_ws[:, :], d_ws[:, :]))
                st.sync()
                dve.sem_inc(s_dslot, 1)
                for q in range(G):
                    st.done(dve.tensor_scalar(d_w[:, q, :], d_w[:, q, :], d_ws[:, q:q + 1], None, ALU.mult))
                st.sync()
                st.done(dve.tensor_tensor(d_wA[:, bass.ds(g * G, G), :], d_w[:, :, :], d_ok[:, :, :], ALU.mult))
                dve.wait_ge(s_dst, g + 1)
                st.done(dve.scalar_tensor_tensor(d_sh[:, :], d_sth[:, :], 1.0, PS[:, 2, :], ALU.add, ALU.mult))
                st.sync()
                st.done(dve.scalar_tensor_tensor(d_sh[:, :], d_sh[:, :], 0.5, PS[:, 3, :], ALU.mult, ALU.mult))
                st.sync()
                dve.sem_inc(s_dsg, 1)
                for q in range(G):
                    dve.wait_ge(s_dsy, g * G + (q + 1))
                    dve.tensor_tensor(tile_of(g * G, q), PS[:, 4 + q % 2, 0:D], tile_of(g * G, q), ALU.add).then_inc(s_dsa, 1)
                st.end()
            with dve.Fori(0, E1 // 2) as i:
                st.loop(i, E1 // 2, 2)
                for j in range(2):
                    dve.wait_ge(s_deth, i * 2 + (j + 1))
                    st.done(dve.scalar_tensor_tensor(d_eh[:, j, :], d_eth[:, j, :], 1.0, PS[:, 2 + j, 0:C1], ALU.add, ALU.mult))
                    st.sync()
                    dve.scalar_tensor_tensor(d_eh[:, j, :], d_eh[:, j, :], 0.5, PS[:, 2 + j, C1:2 * C1], ALU.mult, ALU.mult).then_inc(s_deg, 1)
                st.end()
            dve.sem_inc(s_dgatf, 2)
            dve.wait_ge(s_dsa, NT)
            with dve.Fori(0, NT // 2) as i:
                st.loop(i, NT // 2, 2 * (K1 - 1))
                for j in range(2):
                    t = tile_of(i * 2, j)
                    dve.wait_ge(s_dgat[j], i * (16 * K1) + 16 * K1)
                    for k in range(K1):
                        ins = dve.scalar_tensor_tensor(t, d_gat[:, j, k, :], d_wA[:, bass.ds(i * 2 + j, 1), k], t, ALU.mult, ALU.add)
                        if k < K1 - 1:
                            st.done(ins)
                            st.sync()
                    ins.then_inc(s_x4, 1)
                    dve.wait_ge(s_x4, i * 2 + (j + 1))
                    dve.sem_inc(s_dgatf, 1)
                st.end()

        def transpose_experts(pe, e0, gates=None):
            with pe.Fori(0, E0P) as f:
                if gates is not None:
                    pe.wait_ge(s_agev, gates)
                pe.wait_ge(s_braw, (e0 + f) * 16 + 16)
                for k in range(KD):
                    for a in range(HT):
                        ins = pe.transpose(PS[:, 2 * k + a // 4, (a % 4) * P:(a % 4 + 1) * P], b_raw[:, a, k * P:(k + 1) * P], ident[:, :])
                    ins.then_inc(s_btw, 1)
                pe.wait_ge(s_btw, (e0 + f) * 3 + 2)
                pe.sem_inc(s_brawf, 1)
                pe.wait_ge(s_braw3, (e0 + f) * 16 + 16)
                for k in range(KH):
                    for a in range(KD):
                        c = (k % 2) * D + a * P
                        ins = pe.transpose(PS[:, 4 + k // 2, c:c + P], b_raw3[:, a, k * P:(k + 1) * P], ident[:, :])
                ins.then_inc(s_btw, 1)
                pe.wait_ge(s_btw, (e0 + f) * 3 + 3)
                pe.sem_inc(s_braw3f, 1)
                pe.wait_ge(s_bwe, (e0 + f) * (KD + KH) + KD + KH)

        @block.tensor
        def _(pe):
            pe.wait_ge(s_const, 1)
            pe.sem_inc(s_brawf, 1)
            pe.sem_inc(s_braw3f, 1)
            pe.wait_ge(s_aw, 16 * 19)
            for k in range(KD):
                for g in range(4):
                    c = (k * 4 + g) * N
                    pe.transpose(PS[:, 0, c:c + N], a_wraw[:, g, k * P:(k + 1) * P], ident[0:N, 0:N])
            for k in range(KD):
                ins = pe.transpose(PS[0:N, 1, k * P:(k + 1) * P], a_wpraw[:, k, :], ident[:, :])
            ins.then_inc(s_awt, 1)
            pe.wait_ge(s_awe, 1)
            with pe.Fori(0, B // 2) as p:
                for g in range(GP):
                    pe.wait_ge(s_axn, p * (GP * G) + G * (g + 1))
                    if g:
                        pe.wait_ge(s_axT, (p * GP + g) * KD)
                    transpose_group(pe, 6).then_inc(s_atp, 1)
                transpose_experts(pe, p * (2 * E0P))
                pe.wait_ge(s_axT, (p * GP + GP) * KD)
                for g in range(4):
                    if g >= 2:
                        pe.wait_ge(s_agev, p * 4 + (g - 1))
                    for c in range(NC2):
                        for b in range(2):
                            for k in range(KD):
                                ins = pe.matmul(PS[b * N:(b + 1) * N, 2 * (g % 2) + c, :], a_wT[:, k, g, :],
                                                a_xT[:, k, b * S + c * 512:b * S + (c + 1) * 512],
                                                start=(k == 0), stop=(k == KD - 1))
                    ins.then_inc(s_agate, 1)
                transpose_experts(pe, p * (2 * E0P) + E0P, p * 4 + 4)
                pe.wait_ge(s_ah, p + 1)
                for n in range(2 * QT):
                    b, t = n // QT, n % QT
                    if n >= 2:
                        pe.wait_ge(s_x1, p * (2 * QT) + (n - 1))
                    pe.matmul(PS[:, 4 + n % 2, 0:D], a_h[b * N:(b + 1) * N, t * P:(t + 1) * P], a_wpT[b * N:(b + 1) * N, :],
                              start=True, stop=False)
                    pe.matmul(PS[:, 4 + n % 2, 0:D], ones[b * N:b * N + 1, :], a_bp[b * N:b * N + 1, :],
                              start=False, stop=True).then_inc(s_ay, 1)
                pe.wait_ge(s_x1, p * (2 * QT) + 2 * QT)
            finish_stage(pe, 1)
            pe.wait_ge(s_bw, 16)
            for k in range(KD):
                ins = pe.transpose(PS[:, 6, k * E0:(k + 1) * E0], b_gw[:, k * P:(k + 1) * P], ident[0:E0, 0:E0])
            ins.then_inc(s_bgt, 1)
            pe.wait_ge(s_bge, 1)
            with pe.Fori(0, NG) as g:
                pe.wait_ge(s_bxn, g * G + G)
                transpose_group(pe, 6).then_inc(s_btp, 1)
                pe.wait_ge(s_bxT, g + 1)
                for q in range(G):
                    for k in range(KD):
                        ins = pe.matmul(PS[:, 0, q * E0:(q + 1) * E0], b_xT[:, k, q * P:(q + 1) * P], b_gwT[:, k, :],
                                        start=(k == 0), stop=(k == KD - 1))
                ins.then_inc(s_bsc, 1)
                pe.wait_ge(s_boh, g + 1)
                for q in range(G):
                    dst = PS[:, 1, q * E0:(q + 1) * E0]
                    pe.matmul(dst, onesb[:, :], b_sum[:, :], start=True, stop=False)
                    for r in range(q):
                        pe.matmul(dst, onesb[:, :], b_ohs[:, r, :], start=False, stop=False)
                    ins = pe.matmul(dst, tri[:, :], b_ohs[:, q, :], start=False, stop=True)
                ins.then_inc(s_bpre, 1)
            pe.wait_ge(s_boh, NG + 1)
            pe.matmul(PS[:, 0, 0:E0], onesb[:, :], b_sum[:, :], start=True, stop=True).then_inc(s_bcnt, 1)
            pe.wait_ge(s_bplan, 2)
            pe.sem_inc(s_binf, 2)
            with pe.Fori(0, TILES0 // 2) as i:
                for j in range(2):
                    pe.wait_ge(s_bin[j], i * 16 + 16)
                    for k in range(KD):
                        ins = pe.transpose(PS[:, 1 + 2 * j, k * P:(k + 1) * P], b_xt[:, j, k * P:(k + 1) * P], ident[:, :])
                    ins.then_inc(s_btt, 1)
                for j in range(2):
                    e = pe.value_load(b_tei[0:1, bass.ds(i * 2 + j, 1)], min_val=0, max_val=E0 - 1)
                    pe.wait_ge(s_btT, i * 2 + (j + 1))
                    pe.sem_inc(s_binf, 1)
                    for c in range(2):
                        for k in range(KD):
                            ins = pe.matmul(PS[:, 1 + 2 * j + c, :], b_tT[:, j, k, :],
                                            b_w12T[:, k, bass.ds(e * (2 * H0) + c * H0, H0)],
                                            start=(k == 0), stop=(k == KD - 1))
                    ins.then_inc(s_bh, 1)
                for j in range(2):
                    pe.wait_ge(s_bhid, i * 2 + (j + 1))
                    for k in range(KH):
                        ins = pe.transpose(PS[:, 2 + 2 * j, k * P:(k + 1) * P], b_hid[:, j, k * P:(k + 1) * P], ident[:, :])
                    ins.then_inc(s_bht, 1)
                for j in range(2):
                    e = pe.value_load(b_tei[0:1, bass.ds(i * 2 + j, 1)], min_val=0, max_val=E0 - 1)
                    pe.wait_ge(s_bhT, i * 2 + (j + 1))
                    for k in range(KH):
                        ins = pe.matmul(PS[:, 5 + j, 0:D], b_hT[:, j, k, :], b_w3T[:, k, bass.ds(e * D, D)],
                                        start=(k == 0), stop=(k == KH - 1))
                    ins.then_inc(s_by, 1)
                pe.wait_ge(s_bye, i * 2 + 2)
            finish_stage(pe, 2)
            pe.sem_inc(s_cstf, 1)
            pe.sem_inc(s_cwf, 2)
            pe.sem_inc(s_cxf, 1)
            pe.sem_inc(s_cyf, 1)
            pe.sem_inc(s_cPf, 4)
            with pe.Fori(0, NH) as h:
                pe.wait_ge(s_cst, h * 2 + 2)
                for k in range(KD):
                    ins = pe.transpose(PS[:, 0, k * P:(k + 1) * P], c_qkst[:, k * P:(k + 1) * P], ident[:, :])
                ins.then_inc(s_cwt, 1)
                for k in range(KD):
                    ins = pe.transpose(PS[:, 1, k * DQ:(k + 1) * DQ], c_vst[:, k * P:(k + 1) * P], ident[0:DQ, 0:DQ])
                ins.then_inc(s_cwt, 1)
                pe.wait_ge(s_cwt, h * 2 + 2)
                pe.sem_inc(s_cstf, 1)
                pe.wait_ge(s_cwl, h * 2 + 2)
                pe.wait_ge(s_cwh, h * 2 + 2)
            with pe.Fori(0, NPAIR) as hp:
                pe.wait_ge(s_cst, hp * 2 + (2 * NH + 2))
                for k in range(KD):
                    ins = pe.transpose(PS[:, 2, k * P:(k + 1) * P], c_wst[:, k, :, :].rearrange("p h v -> p (h v)"), ident[:, :])
                ins.then_inc(s_cwt, 1)
                pe.wait_ge(s_cwt, hp + (2 * NH + 1))
                pe.sem_inc(s_cstf, 1)
                pe.wait_ge(s_cwh, hp + (2 * NH + 1))
            pe.wait_ge(s_cset, 2)
            parts = ((0, 0), (1, 0), (0, 1))
            with pe.Fori(0, B) as b:
                for g in range(S // GT):
                    pe.wait_ge(s_cxn, b * QT + (g + 1) * G)
                    if g:
                        pe.wait_ge(s_cxl, b * (KD * S // GT) + g * KD)
                    transpose_group(pe, 0).then_inc(s_ctp, 1)
                pe.wait_ge(s_cxl, b * (KD * S // GT) + KD * S // GT)
                pe.sem_inc(s_pass, 1)
                with pe.Fori(0, NPAIR) as hp:
                    pair = b * NPAIR + hp
                    for h in range(2):
                        pe.wait_ge(s_cw, pair * 4 + 2 * h + 2)
                        if h:
                            pe.wait_ge(s_cks, pair * 4 + 2)
                            pe.wait_ge(s_cqs, pair * 8 + 4)
                        for c in range(NC2):
                            for n, (w, x) in enumerate(parts):
                                for k in range(KD):
                                    ins = pe.matmul(PS[:, c, :], c_st[w][:, h, k, :], c_xT[x][:, k, c * 512:(c + 1) * 512],
                                                    start=(n == 0 and k == 0), stop=(n == 2 and k == KD - 1))
                        ins.then_inc(s_cqk, 1)
                    for r in range(2):
                        for a in range(QT // 2):
                            t = r * (QT // 2) + a
                            for n, (x, w) in enumerate(parts):
                                for k in range(KD):
                                    ins = pe.matmul(PS[:, (2, 7)[r], a * P:(a + 1) * P], c_xT[x][:, k, t * P:(t + 1) * P],
                                                    c_wv[w][:, k, bass.ds(hp * P, P)],
                                                    start=(n == 0 and k == 0), stop=(n == 2 and k == KD - 1))
                        ins.then_inc(s_cv, 1)
                    pe.wait_ge(s_cqk, pair * 2 + 2)
                    pe.sem_inc(s_cwf, 2)
                    for h in range(2):
                        pe.wait_ge(s_cks, pair * 4 + 2 * h + 2)
                        for t in range(QT):
                            s = 3 + 2 * (t % 2)
                            if h * QT + t >= 2:
                                pe.wait_ge(s_cmx, pair * (2 * QT) + (h * QT + t - 1))
                            w = (t + 1) * P
                            for c in range((w + 511) // 512):
                                n = min(512, w - c * 512)
                                last = w <= (c + 1) * 512
                                pe.matmul(PS[:, s + c, 0:n], c_q1[h][:, t * P:(t + 1) * P], c_k1[h][:, c * 512:c * 512 + n],
                                          start=True, stop=not last)
                                if last:
                                    pe.matmul(PS[:, s + c, n - P:n], identb[:, :], c_maskq[:, :], start=False, stop=True).then_inc(s_cS, 1)
                    n = 0
                    for h in range(2):
                        pe.wait_ge(s_cmx, pair * (2 * QT) + (h + 1) * QT)
                        if h:
                            pe.wait_ge(s_cm, pair * 2 + 1)
                        for t in range(QT):
                            ins = pe.transpose(PS[0:1, t // 4, (t % 4) * P:(t % 4 + 1) * P], c_mx[h][:, t:t + 1], ident[:, :])
                        ins.then_inc(s_cmT, 1)
                        if h == 0:
                            pe.wait_ge(s_cmx, pair * (2 * QT) + 2 * QT)
                            pe.wait_ge(s_cve, pair * 4 + 4)
                        pe.wait_ge(s_cm, pair * 2 + (h + 1))
                        blocks = [(c, j) for c in range(NC2) for j in range(4 * (c + 1))]

                        def scores_t(m):
                            c, j = blocks[m]
                            off = max(0, j * P - c * 512)
                            bank = 3 + (h * len(blocks) + m) % 4
                            q = slice(c * 512 + off, (c + 1) * 512)
                            diagonal = j * P >= c * 512
                            pe.matmul(PS[:, bank, 0:512 - off], c_k1[h][:, j * P:(j + 1) * P], c_q1[h][:, q], start=True, stop=False)
                            ins = pe.matmul(PS[:, bank, 0:512 - off], c_k2[h][:, j * P:(j + 1) * P], c_q2[h][:, q], start=False, stop=not diagonal)
                            if diagonal:
                                ins = pe.matmul(PS[:, bank, 0:P], identb[:, :], c_maskk[:, :], start=False, stop=True)
                            ins.then_inc(s_cT, 1)

                        for m in range(2):
                            scores_t(m)
                        for m, (c, j) in enumerate(blocks):
                            off = max(0, j * P - c * 512)
                            if j == 0 and (h or c):
                                if h * NC2 + c >= 2:
                                    pe.wait_ge(s_cOy, pair * (2 * NC2) + (h * NC2 + c - 1))
                                    pe.wait_ge(s_cOd, pair * (2 * NC2) + (h * NC2 + c - 1))
                            pe.wait_ge(s_cP, pair * PAIR_BLOCKS + (h * len(blocks) + m + 1))
                            ins = pe.matmul(PS[:, (7, 2)[c % 2], off:512], c_v[h][:, j, :], c_p[:, (h * len(blocks) + m) % 4, 0:512 - off],
                                            start=(j == 0), stop=(j == 4 * (c + 1) - 1))
                            if j == 4 * (c + 1) - 1:
                                ins.then_inc(s_cO, 1)
                                pe.wait_ge(s_cO, pair * (2 * NC2) + (h * NC2 + c + 1))
                                pe.sem_inc(s_cPf, 1)
                            else:
                                ins.then_inc(s_cPf, 1)
                            if m + 2 < len(blocks):
                                scores_t(m + 2)
                    pe.wait_ge(s_cOy, pair * (2 * NC2) + 2 * NC2)
                    pe.wait_ge(s_cOd, pair * (2 * NC2) + 2 * NC2)
                pe.sem_inc(s_cxf, 1)
                pe.wait_ge(s_cyn, b * (NPAIR * NC2) + NPAIR * NC2)
                for t in range(QT):
                    if t >= 4:
                        pe.wait_ge(s_x3, b * QT + (t - 3))
                    for hp in range(NPAIR):
                        ins = pe.matmul(PS[:, 3 + t % 4, 0:D], c_yT[:, hp, t * P:(t + 1) * P], c_wo[:, hp, :],
                                        start=(hp == 0), stop=(hp == NPAIR - 1))
                    ins.then_inc(s_cz, 1)
                pe.wait_ge(s_x3, b * QT + QT)
                pe.sem_inc(s_cyf, 1)
            finish_stage(pe, 3)
            pe.wait_ge(s_dcast, 3)
            for k in range(KD):
                pe.transpose(PS[:, 0, k * E1:(k + 1) * E1], d_gwf[:, k * P:(k + 1) * P], ident[0:E1, 0:E1])
                for a in range(2):
                    c = (k * 2 + a) * I1
                    pe.transpose(PS[:, 1, c:c + I1], d_rawf[:, a, k * P:(k + 1) * P], ident[:, :])
                ins = pe.transpose(PS[:, 2, k * P:(k + 1) * P], d_raw2f[:, k, :], ident[:, :])
            ins.then_inc(s_dwt, 1)
            pe.wait_ge(s_dwe, 1)
            with pe.Fori(0, NG) as g:
                pe.wait_ge(s_dxn, g * G + G)
                transpose_group(pe, 6).then_inc(s_dtp, 1)
                pe.wait_ge(s_dxT, g + 1)
                for q in range(G):
                    for k in range(KD):
                        ins = pe.matmul(PS[:, 0, q * E1:(q + 1) * E1], d_xT[:, k, q * P:(q + 1) * P], d_gwT[:, k, :],
                                        start=(k == 0), stop=(k == KD - 1))
                ins.then_inc(s_dsc, 1)
                for a in range(2):
                    for k in range(KD):
                        ins = pe.matmul(PS[:, 2 + a, :], d_s1T[:, k, a, :], d_xT[:, k, :], start=(k == 0), stop=(k == KD - 1))
                ins.then_inc(s_dsh, 1)
                pe.wait_ge(s_doh, g + 1)
                for q in range(G):
                    dst = PS[:, 1, q * E1:(q + 1) * E1]
                    pe.matmul(dst, onesb[:, :], d_sum[:, :], start=True, stop=False)
                    for r in range(q):
                        pe.matmul(dst, onesb[:, :], d_ohs[:, r, :], start=False, stop=False)
                    ins = pe.matmul(dst, tri[:, :], d_ohs[:, q, :], start=False, stop=True)
                ins.then_inc(s_dpre, 1)
                pe.wait_ge(s_dsg, g + 1)
                for q in range(G):
                    if q >= 2:
                        pe.wait_ge(s_dsa, g * G + (q - 1))
                    pe.matmul(PS[:, 4 + q % 2, 0:D], d_sh[:, q * P:(q + 1) * P], d_s2T[:, :], start=True, stop=True).then_inc(s_dsy, 1)
                pe.wait_ge(s_dsa, g * G + G)
            pe.sem_inc(s_dinf, 2)
            with pe.Fori(0, E1 // 2) as i:
                for j in range(2):
                    pe.wait_ge(s_din[j], i * 64 + 64)
                    for k in range(KD):
                        for a in range(C1 // P):
                            c = k * C1 + a * P
                            ins = pe.transpose(PS[:, j, c:c + P], d_xe[:, j, a, k * P:(k + 1) * P], ident[:, :])
                    ins.then_inc(s_det, 1)
                for j in range(2):
                    pe.wait_ge(s_deT, i * 2 + (j + 1))
                    pe.wait_ge(s_dec, i * 2 + (j + 1))
                    for a in range(2):
                        for k in range(KD):
                            c = a * D + k * I1
                            ins = pe.matmul(PS[:, 2 + j, a * C1:(a + 1) * C1], d_wf[:, j, c:c + I1], d_xeT[:, j, k, :],
                                            start=(k == 0), stop=(k == KD - 1))
                    ins.then_inc(s_deh, 1)
                for j in range(2):
                    pe.wait_ge(s_deg, i * 2 + (j + 1))
                    for a in range(C1 // P):
                        ins = pe.matmul(PS[:, 4 + j, a * D:(a + 1) * D], d_eh[:, j, a * P:(a + 1) * P], d_wf[:, j, 2 * D:3 * D],
                                        start=True, stop=True)
                    ins.then_inc(s_dey, 1)
                pe.wait_ge(s_dye, i * 2 + 2)
                pe.sem_inc(s_dinf, 2)


_INS = ['L0_attn_x', 'L0_attn_ln_w', 'L0_attn_ln_b', 'L0_attn_Wi', 'L0_attn_bi', 'L0_attn_Wf', 'L0_attn_bf',
        'L0_attn_Wz', 'L0_attn_bz', 'L0_attn_Wo', 'L0_attn_bo', 'L0_attn_Wp', 'L0_attn_bp', 'L0_ffn_w12',
        'L0_ffn_w3', 'L0_ffn_gate_w', 'L1_attn_Q', 'L1_attn_K', 'L1_attn_V', 'L1_attn_W', 'L1_ffn_gate_w',
        'L1_ffn_bias', 'L1_ffn_W1', 'L1_ffn_W3', 'L1_ffn_W2', 'L1_ffn_sw1', 'L1_ffn_sw3', 'L1_ffn_sw2']
_OUTS = [((4, 1024, 256), 'float32')]


def kernel(**inputs):
    import numpy as _np
    import concourse.bacc as _bacc
    from concourse import mybir as _mybir
    from concourse.bass_utils import run_bass_kernel_spmd as _run

    nc = _bacc.Bacc("TRN2", target_bir_lowering=False, num_devices=1)
    arrays, args = {}, []
    for name in _INS:
        a = _np.ascontiguousarray(inputs[name])
        arrays[f"in_{name}_dram"] = a
        args.append(nc.dram_tensor(f"in_{name}_dram", a.shape, _mybir.dt.from_np(a.dtype), kind="ExternalInput").ap())
    for i, (shape, dtype) in enumerate(_OUTS):
        dt = _mybir.dt.from_np(_np.dtype(dtype))
        args.append(nc.dram_tensor(f"out_{i}_dram", shape, dt, kind="ExternalOutput").ap())
    network(nc, *args)
    r = _run(nc, [arrays], core_ids=[0])
    return r.results[0]["out_0_dram"]
```

```python
from contextlib import ExitStack

import concourse.bass as bass
from concourse import mybir

F32 = mybir.dt.float32
F32R = mybir.dt.float32r
BF16 = mybir.dt.bfloat16
I32 = mybir.dt.int32
U32 = mybir.dt.uint32
ALU = mybir.AluOpType
ACT = mybir.ActivationFunctionType
AX_X = mybir.AxisListType.X

P = 128
EPS = 1e-5
BIG = -1e30


class Steps:

    def __init__(self, eng, sem):
        self.eng, self.sem, self.base, self.n, self.i, self.per = eng, sem, 0, 0, None, 0

    def loop(self, i, rounds, per):
        assert self.i is None
        self.base += self.n
        self.n, self.i, self.rounds, self.per = 0, i, rounds, per

    def end(self):
        assert self.n == self.per, (self.n, self.per)
        self.base += self.rounds * self.per
        self.n, self.i = 0, None

    def done(self, ins):
        ins.then_inc(self.sem, 1)
        self.n += 1

    def sync(self):
        at = self.base + self.n
        self.eng.wait_ge(self.sem, at if self.i is None else self.i * self.per + at)


def network(nc, x_in, ln_w, ln_b, Wi, bi, Wf, bf, Wz, bz, Wo, bo, Wp, bp, w12, w3, gate0,
            Q, K, V, W, gate1, bias1, W1, W3, W2, sw1, sw3, sw2, out):
    B, S, D = x_in.shape
    T = B * S
    NT = T // P
    KD = D // P
    N = Wi.shape[0]
    E0, H0 = w12.shape[0], w3.shape[2]
    K0 = 2
    DQ, _, NH = Q.shape
    E1, _, I1 = W1.shape
    K1 = 4
    C1 = 2 * (2 * 512) * K1 // E1
    G = 4
    GT = G * P
    NG = T // GT
    KH = H0 // P
    HT = 2 * H0 // P
    REGION = T + P
    TILES0 = T * K0 // P + E0
    BIGSLOT = 1 << 20
    NPAIR = NH // 2
    QT = S // P
    NC2 = S // 512
    ATT_SCALE = (DQ / D) / DQ
    Z_SCALE = (DQ / D) ** 0.5 * (D / DQ) ** 0.5 / NH

    x_tiles = x_in.rearrange("b (i p) d -> p (b i) d", p=P)
    out_tiles = out.rearrange("b (i p) d -> p (b i) d", p=P)
    routed0 = nc.dram_tensor("routed0", (E0 * REGION, D), F32).ap()
    expert0 = nc.dram_tensor("expert0", (TILES0 * P, D), F32).ap()
    routed1 = nc.dram_tensor("routed1", (E1 * C1, D), F32).ap()
    expert1 = nc.dram_tensor("expert1", (E1 * C1, D), F32).ap()

    with ExitStack() as ctx:
        def sb(name, shape, dt=F32):
            return ctx.enter_context(nc.sbuf_tensor(name, shape, dt))

        def sem(name):
            return ctx.enter_context(nc.semaphore(name))

        X = sb("X", [P, NT, D])
        ident = sb("ident", [P, P])
        ones = sb("ones", [P, P])
        tri = sb("tri", [P, P], BF16)
        onesb = sb("onesb", [P, P], BF16)
        identb = sb("identb", [P, P], BF16)
        zeros = sb("zeros", [P, D])
        iota = sb("iota", [P, P])
        stat = sb("stat", [P, G, 6])
        mv = sb("mv", [P, G, 2])
        var = sb("var", [P, G])
        rstd = sb("rstd", [P, G])
        rtmp = sb("rtmp", [P, G])
        means = sb("means", [P, NT])
        variances = sb("variances", [P, NT])
        rstds = sb("rstds", [P, NT])
        rstds_tmp = sb("rstds_tmp", [P, NT])
        xn = sb("xn", [P, G, D])

        arena_at = (nc.sbuf_base + 31) // 32 * 32
        arena_size = (nc.sbuf_bytes_remaining - 128) // 4
        ctx.enter_context(nc.sbuf_tensor("arena", [P, arena_size], F32))
        at = [arena_at]

        def place(name, shape, dt=F32):
            n = 2 if dt == BF16 else 4
            for s in shape[1:]:
                n *= s
            t = nc.alloc_sbuf_tensor_at(name, shape, dt, offset=at[0])
            at[0] += (n + 31) // 32 * 32
            assert at[0] <= arena_at + 4 * arena_size, (name, at[0] - arena_at - 4 * arena_size)
            return t

        PS = ctx.enter_context(nc.psum_tensor("PS", [P, 8, 512], F32))

        b_w12T = place("b_w12T", [P, KD, E0 * 2 * H0])
        b_w3T = place("b_w3T", [P, KH, E0 * D])
        after_weights = at[0]
        b_raw = place("b_raw", [P, HT, D])
        b_raw3 = place("b_raw3", [P, KD, H0])

        a_xT = place("a_xT", [P, KD, 2 * S])
        a_wraw = place("a_wraw", [N, 4, D])
        a_wpraw = place("a_wpraw", [P, KD, N])
        a_wT = place("a_wT", [P, KD, 4, N])
        a_wpT = [place(f"a_wpT{b}", [P, D]) for b in range(2)]
        a_rows = [xn, place("a_rows1", [P, G, D])]
        a_xstat = place("a_xstat", [P, 2 * QT, 6])
        a_xmv = place("a_xmv", [P, 2 * QT, 2])
        a_var = place("a_var", [P, 2 * QT])
        a_rstd = place("a_rstd", [P, 2 * QT])
        a_tmp = place("a_tmp", [P, 2 * QT])
        a_bias = place("a_bias", [P, 4])
        a_hbo = place("a_hbo", [P, 1])
        a_bp = place("a_bp", [P, D])
        a_lnw = place("a_lnw", [P, KD])
        a_lnb = place("a_lnb", [P, KD])
        a_lf = place("a_lf", [P, S])
        a_li = place("a_li", [P, S])
        a_z = place("a_z", [P, S])
        a_o = place("a_o", [P, S])
        a_m = place("a_m", [P, 1 + S])
        a_fs = place("a_fs", [P, S])
        a_is = place("a_is", [P, S])
        a_stat = place("a_stat", [P, 2 * QT, 6])
        a_mv = place("a_mv", [P, 2 * QT, 2])
        a_c = a_lf
        a_h = a_li

        at[0] = after_weights
        b_gw = place("b_gw", [E0, D])
        b_gwT = place("b_gwT", [P, KD, E0])
        b_xT = [place(f"b_xT{j}", [P, KD, GT]) for j in range(2)]
        b_rows = [xn, place("b_rows1", [P, G, D])]
        b_s8 = place("b_s8", [P, G, E0])
        b_top = place("b_top", [P, G, 8])
        b_ix = place("b_ix", [P, G, 8], U32)
        b_idx = place("b_idx", [P, G * K0, 1])
        b_gap = place("b_gap", [P, G])
        b_ex = place("b_ex", [P, G])
        b_den = place("b_den", [P, G])
        b_oh = place("b_oh", [P, G, K0, E0])
        b_ohs = place("b_ohs", [P, G, E0], BF16)
        b_sum = place("b_sum", [P, E0], BF16)
        b_gsum = place("b_gsum", [P, E0])
        b_tmp = place("b_tmp", [P, G, K0, E0])
        b_pos = place("b_pos", [P, G, K0])
        b_slot = [place(f"b_slot{j}", [P, G, K0], U32) for j in range(2)]
        b_posA = place("b_posA", [P, NT, K0])
        b_idxA = place("b_idxA", [P, NT, K0])
        b_gtmp = place("b_gtmp", [P, NT, K0])
        b_cnt = place("b_cnt", [P, E0])
        b_nti = place("b_nti", [P, E0], I32)
        b_nt = place("b_nt", [P, E0])
        b_end = place("b_end", [P, E0])
        b_start = place("b_start", [P, E0])
        b_zrow = place("b_zrow", [P, E0])
        b_zrowi = place("b_zrowi", [P, E0], I32)
        b_te = place("b_te", [P, TILES0])
        b_ts = place("b_ts", [P, TILES0])
        b_tt = place("b_tt", [P, TILES0])
        b_tei = place("b_tei", [P, TILES0], I32)
        b_rowi = place("b_rowi", [P, TILES0], I32)
        b_xt = place("b_xt", [P, 2, D])
        b_tT = place("b_tT", [P, 2, KD, P])
        b_sg = place("b_sg", [P, 2, H0])
        b_hid = place("b_hid", [P, 2, H0])
        b_hT = place("b_hT", [P, 2, KH, P])
        b_y = place("b_y", [P, 2, D])
        at[0] = (arena_at + 4 * arena_size - 4 * (G * K0 * (D + 1) + 2 * NT * K0)) // 32 * 32 - 64
        b_prA = place("b_prA", [P, NT, K0])
        b_gix = place("b_gix", [P, NT, K0], U32)
        b_gi = place("b_gi", [P, G, K0], U32)
        b_gat = place("b_gat", [P, G, K0, D])

        BLOCKS = [(c, j) for c in range(NC2) for j in range(4 * (c + 1))]
        CHUNKS = [(t, c) for t in range(QT) for c in range(t // 4 + 1)]
        PBUF = 4
        at[0] = arena_at
        c_wqk = [place(f"c_wqk{n}", [P, KD, NH, P], F32R) for n in ("_hi", "_lo")]
        c_wv = [place(f"c_wv{n}", [P, KD, NH * DQ], F32R) for n in ("_hi", "_lo")]
        c_wo = place("c_wo", [P, NPAIR, D])
        c_xT = [place(f"c_xT{n}", [P, KD, S], F32R) for n in ("_hi", "_lo")]
        c_st = [[place(f"c_st{n}_{h}", [P, KD, P], F32R) for n in ("_hi", "_lo")] for h in range(2)]
        c_maskq = place("c_maskq", [P, P], BF16)
        c_maskk = place("c_maskk", [P, P], BF16)
        c_block = place("c_block", [QT, QT, P], BF16)
        heads_at = at[0]
        c_q1 = [place(f"c_q1_{h}", [P, S], F32R) for h in range(2)]
        c_k1 = [place(f"c_k1_{h}", [P, S], F32R) for h in range(2)]
        c_q2 = [place(f"c_q2_{h}", [P, S], F32R) for h in range(2)]
        c_k2 = [place(f"c_k2_{h}", [P, S], F32R) for h in range(2)]
        c_v = place("c_v", [P, QT, NH * DQ])
        c_vh = [place(f"c_vh_{h}", [P, QT, DQ]) for h in range(2)]
        c_p = place("c_p", [P, PBUF, 512])
        c_den = [place(f"c_den_{c}", [P, 512]) for c in range(NC2)]
        c_rden = place("c_rden", [P, 256])
        c_max = place("c_max", [P, QT])
        c_max2 = place("c_max2", [P, 2, QT // 2])
        c_yT = [place(f"c_yT_{n}", [P, S]) for n in range(2)]
        at[0] = heads_at
        c_vraw = place("c_vraw", [DQ, D, NH])
        c_qkraw = place("c_qkraw", [P, D, NH])
        c_wraw = place("c_wraw", [P, KD, DQ, NH])
        c_vst = [place(f"c_vst_{h}", [DQ, D]) for h in range(2)]
        c_qkst = [place(f"c_qkst_{h}", [P, D]) for h in range(2)]
        c_wst = place("c_wst", [P, KD, 2, DQ])

        at[0] = arena_at
        EBUF = 4
        d_raw = place("d_raw", [P, 2, D], BF16)
        d_raw2 = place("d_raw2", [P, KD, I1], BF16)
        d_gwraw = place("d_gwraw", [E1, D], BF16)
        d_rawf = place("d_rawf", [P, 2, D])
        d_raw2f = place("d_raw2f", [P, KD, I1])
        d_gwf = place("d_gwf", [E1, D])
        d_gwT = place("d_gwT", [P, KD, E1])
        d_s1T = place("d_s1T", [P, KD, 2, I1])
        d_s2T = place("d_s2T", [I1, D])
        d_bias = place("d_bias", [P, 1, E1])
        d_xT = [place(f"d_xT{j}", [P, KD, GT]) for j in range(2)]
        d_rows = [xn, place("d_rows1", [P, G, D])]
        d_th = place("d_th", [P, G, E1])
        d_sc = place("d_sc", [P, G, E1])
        d_sel = place("d_sel", [P, G, E1])
        d_top = place("d_top", [P, G, 8])
        d_ix = place("d_ix", [P, G, 8], U32)
        d_idx = place("d_idx", [P, G * K1, 1])
        d_oh = place("d_oh", [P, G, K1, E1])
        d_ohf = place("d_ohf", [P, G, E1])
        d_ohs = place("d_ohs", [P, G, E1], BF16)
        d_sum = place("d_sum", [P, E1], BF16)
        d_gsum = place("d_gsum", [P, E1])
        d_tmp = place("d_tmp", [P, G, K1, E1])
        d_tmp2 = place("d_tmp2", [P, G, K1, E1])
        d_pos = place("d_pos", [P, G, K1])
        d_w = place("d_w", [P, G, K1])
        d_ws = place("d_ws", [P, G])
        d_ok = place("d_ok", [P, G, K1])
        d_skip = place("d_skip", [P, G, K1])
        d_cl = place("d_cl", [P, G, K1])
        d_slot = [place(f"d_slot{j}", [P, G, K1], U32) for j in range(2)]
        d_wA = place("d_wA", [P, NT, K1])
        d_gix = place("d_gix", [P, NT, K1], U32)
        d_sth = place("d_sth", [I1, GT])
        d_sh = place("d_sh", [I1, GT])
        d_xe = place("d_xe", [P, EBUF, C1 // P, D])
        d_wb = place("d_wb", [P, EBUF, 3 * D], BF16)
        d_wf = place("d_wf", [P, EBUF, 3 * D])
        d_xeT = place("d_xeT", [P, 2, KD, C1])
        d_eth = place("d_eth", [I1, 2, C1])
        d_eh = place("d_eh", [I1, 2, C1])
        d_y = place("d_y", [P, 2, C1 // P, D])
        d_gi = place("d_gi", [P, G, K1], U32)
        d_gat = place("d_gat", [P, G, K1, D])

        stage_end = sem("stage_end")
        s_const = sem("constants_made")
        s_x = [sem(f"x_loaded{g}") for g in range(NG)]
        s_out = sem("out_stored")
        s_act = sem("act_steps")
        s_dve = sem("dve_steps")
        s_pool = sem("pool_steps")
        s_pass = sem("wait_passed")
        s_aw = sem("a_weights_loaded")
        s_awt = sem("a_weights_transposed")
        s_awe = sem("a_weights_ready")
        s_axn = sem("a_xn_ready")
        s_atp = sem("a_xn_transposed")
        s_axT = sem("a_xT_ready")
        s_agate = sem("a_gate_ready")
        s_agev = sem("a_gate_taken")
        s_afree = sem("a_gate_buffers_free")
        s_ascan = sem("a_scan_step")
        s_aexp = sem("a_exp_ready")
        s_ah = sem("a_h_ready")
        s_ay = sem("a_proj_ready")
        s_x1 = sem("x1_ready")
        s_braw = sem("b_w12_loaded")
        s_braw3 = sem("b_w3_loaded")
        s_brawf = sem("b_w12_buffer_free")
        s_braw3f = sem("b_w3_buffer_free")
        s_btw = sem("b_weights_transposed")
        s_bwe = sem("b_weights_taken")
        s_bw = sem("b_router_loaded")
        s_bgt = sem("b_router_transposed")
        s_bge = sem("b_router_ready")
        s_bxn = sem("b_xn_ready")
        s_btp = sem("b_xn_transposed")
        s_bxT = sem("b_xT_ready")
        s_bsc = sem("b_scores_ready")
        s_bgap = sem("b_score_gap_ready")
        s_bex = sem("b_gap_exp_ready")
        s_boh = sem("b_onehot_ready")
        s_bpre = sem("b_prefix_ready")
        s_bslot = sem("b_slots_ready")
        s_bscat = sem("b_rows_scattered")
        s_bxnf = sem("b_xn_free")
        s_bcnt = sem("b_counts_ready")
        s_bplan = sem("b_plan_ready")
        s_bzero = sem("b_tails_zeroed")
        s_bin = [sem(f"b_tile_loaded{j}") for j in range(2)]
        s_btt = sem("b_tile_transposed")
        s_btT = sem("b_tileT_ready")
        s_bh1 = sem("b_hidden1_ready")
        s_bh2 = sem("b_hidden2_ready")
        s_bsg = sem("b_sigmoid_exp_ready")
        s_bhid = sem("b_gated_ready")
        s_bht = sem("b_gated_transposed")
        s_bhT = sem("b_gatedT_ready")
        s_by = sem("b_y_ready")
        s_bye = sem("b_y_taken")
        s_bst = [sem(f"b_y_stored{j}") for j in range(2)]
        s_bgat = [sem(f"b_rows_gathered{j}") for j in range(G)]
        s_bgatf = sem("b_gather_buffer_free")
        s_x2 = sem("x2_ready")
        s_cl = sem("c_weights_loaded")
        s_cst = sem("c_weights_staged")
        s_cwt = sem("c_weights_transposed")
        s_cwh = sem("c_weights_hi_ready")
        s_cwl = sem("c_weights_lo_ready")
        s_cset = sem("c_constants_made")
        s_cxn = sem("c_xn_ready")
        s_ctp = sem("c_xn_transposed")
        s_cxh = sem("c_xT_hi_ready")
        s_cxl = sem("c_xT_lo_ready")
        s_cw = [sem(f"c_head_weights_staged{h}") for h in range(2)]
        s_cqk = sem("c_qk_ready")
        s_cqs = sem("c_qk_hi_ready")
        s_cks = sem("c_qk_lo_ready")
        s_ck2 = sem("c_k2_ready")
        s_cv = sem("c_v_ready")
        s_cve = sem("c_v_taken")
        s_cvh = [sem(f"c_head_v_staged{h}") for h in range(2)]
        s_cS = sem("c_scores_ready")
        s_cmx = sem("c_max_ready")
        s_cmT = sem("c_max_transposed")
        s_cm = sem("c_max_rows_ready")
        s_cT = sem("c_scoresT_ready")
        s_cP = sem("c_probs_ready")
        s_cPu = sem("c_probs_multiplied")
        s_cPa = sem("c_probs_added")
        s_cD = sem("c_den_ready")
        s_cr = sem("c_den_inverted")
        s_cyn = sem("c_y_normalised")
        s_cz = sem("c_z_ready")
        s_turn = [sem(f"c_turn_over{r}") for r in range(2)]
        s_dz = sem("d_rows_zeroed")
        s_dl = sem("d_weights_loaded")
        s_dcast = sem("d_weights_cast")
        s_dwt = sem("d_weights_transposed")
        s_dwe = sem("d_weights_ready")
        s_dxn = sem("d_xn_ready")
        s_dtp = sem("d_xn_transposed")
        s_dxT = sem("d_xT_ready")
        s_dsc = sem("d_logits_ready")
        s_dth = sem("d_logit_tanh_ready")
        s_doh = sem("d_onehot_ready")
        s_dpre = sem("d_prefix_ready")
        s_dslot = sem("d_slots_ready")
        s_dscat = sem("d_rows_scattered")
        s_dxnf = sem("d_xn_free")
        s_dsh = sem("d_shared_hidden_ready")
        s_dst = sem("d_shared_tanh_ready")
        s_dsg = sem("d_shared_gated_ready")
        s_dsy = sem("d_shared_y_ready")
        s_dsa = sem("d_shared_y_added")
        s_dxe = [sem(f"d_expert_rows_loaded{q}") for q in range(EBUF)]
        s_dw = [sem(f"d_expert_weights_loaded{q}") for q in range(EBUF)]
        s_dec = sem("d_expert_weights_cast")
        s_det = sem("d_expert_rows_transposed")
        s_deT = sem("d_expert_rowsT_ready")
        s_deh = sem("d_expert_hidden_ready")
        s_deth = sem("d_expert_tanh_ready")
        s_deg = sem("d_expert_gated_ready")
        s_dey = sem("d_expert_y_ready")
        s_dye = sem("d_expert_y_taken")
        s_dyst = [sem(f"d_expert_y_stored{j}") for j in range(2)]
        s_dgat = [sem(f"d_rows_gathered{q}") for q in range(G)]
        s_dgatf = sem("d_gather_buffer_free")
        s_x4 = sem("x4_ready")
        block = ctx.enter_context(nc.Block())

        def tile_of(t, n):
            return X[:, bass.ds(t + n, 1), :].rearrange("p a d -> p (a d)")

        RSQRT_STEPS = 11

        def rsqrt(dve, st, var, rstd, tmp):
            st.done(dve.tensor_scalar(tmp[:, :].bitcast(I32), var[:, :].bitcast(I32), 1, None, ALU.logical_shift_right))
            st.sync()
            st.done(dve.tensor_scalar(rstd[:, :].bitcast(I32), tmp[:, :].bitcast(I32), -1.0, float(0x5F3759DF),
                                      ALU.mult, ALU.add))
            for _ in range(3):
                st.sync()
                st.done(dve.tensor_tensor(tmp[:, :], rstd[:, :], rstd[:, :], ALU.mult))
                st.sync()
                st.done(dve.scalar_tensor_tensor(tmp[:, :], tmp[:, :], -0.5, var[:, :], ALU.mult, ALU.mult))
                st.sync()
                st.done(dve.scalar_tensor_tensor(rstd[:, :], tmp[:, :], 1.5, rstd[:, :], ALU.add, ALU.mult))
            st.sync()

        LN_STEPS = 2 * G + 1 + RSQRT_STEPS

        def group_statistics(dve, st, t, mul, add):
            for q in range(G):
                st.done(dve.bn_stats(stat[:, q, :], tile_of(t, q)))
            st.sync()
            dve.memset(rtmp[:, :], 0.0)
            for q in range(G):
                st.done(dve.bn_aggr(mv[:, q, :], stat[:, q, :]))
            st.sync()
            st.done(dve.tensor_scalar(var[:, :], mv[:, :, 1], mul, add, ALU.mult, ALU.add))
            st.sync()
            rsqrt(dve, st, var, rstd, rtmp)

        def normalise_group(dve, st, t, mul, add, xn_ready):
            group_statistics(dve, st, t, mul, add)
            for q in range(G):
                dve.tensor_scalar(xn[:, q, :], tile_of(t, q), mv[:, q, 0:1], rstd[:, q:q + 1],
                                  ALU.subtract, ALU.mult).then_inc(xn_ready, 1)

        def collect_moments(dve, st, t, n, stat, mv):
            st.sync()
            dve.memset(rtmp[:, :], 0.0)
            for q in range(n):
                st.done(dve.bn_aggr(mv[:, q, :], stat[:, q, :]))
            st.sync()
            st.done(dve.tensor_copy(means[:, bass.ds(t, n)], mv[:, 0:n, 0]))
            st.done(dve.tensor_copy(variances[:, bass.ds(t, n)], mv[:, 0:n, 1]))
            st.sync()

        def all_rstds(dve, st):
            st.done(dve.tensor_scalar(variances[:, :], variances[:, :], 1.0, EPS, ALU.mult, ALU.add))
            st.sync()
            rsqrt(dve, st, variances, rstds, rstds_tmp)

        def apply_norm(dve, t, rows, xn_ready):
            for q in range(G):
                dve.tensor_scalar(rows[:, q, :], tile_of(t, q), means[:, bass.ds(t + q, 1)], rstds[:, bass.ds(t + q, 1)],
                                  ALU.subtract, ALU.mult).then_inc(xn_ready, 1)

        def transpose_group(pe, bank, rows=xn):
            for k in range(KD):
                for q in range(G):
                    ins = pe.transpose(PS[:, bank + k, q * P:(q + 1) * P], rows[:, q, k * P:(k + 1) * P], ident[:, :])
            return ins

        def finish_stage(eng, n):
            eng.drain().then_inc(stage_end, 1)
            eng.wait_ge(stage_end, 5 * n)

        def turns(r, heads, pairs, vs, xts):
            chunks = len(CHUNKS) // 2 + (1 if r == 0 else 0)
            return heads * chunks + pairs * (QT // 4) + vs * QT + xts * (S // GT)

        GP = 2 * S // GT
        E0P = E0 // 4

        @block.sync
        def _(sp):
            for c in range(NG):
                sp.dma_start(X[:, c * G:(c + 1) * G, :], x_tiles[:, c * G:(c + 1) * G, :]).then_inc(s_x[c], 16)
                if c == GP - 1:
                    for k, w in enumerate((Wf, Wi, Wz, Wo)):
                        sp.dma_start(a_wraw[:, k, :], w).then_inc(s_aw, 16)
                    sp.dma_start(a_wpraw[:, :, :], Wp.rearrange("(k p) n -> p k n", p=P)).then_inc(s_aw, 16)
                    for k, b in enumerate((bf, bi, bz, bo)):
                        for h in range(2):
                            sp.dma_start(a_bias[h * N:(h + 1) * N, k:k + 1], b.rearrange("(n a) -> n a", a=1)).then_inc(s_aw, 16)
                    sp.dma_start(a_bp[:, :], bp.rearrange("(a d) -> a d", a=1).broadcast_to([P, D])).then_inc(s_aw, 16)
                    for k in range(KD):
                        sp.dma_start(a_lnw[:, k:k + 1], ln_w[k * P:(k + 1) * P].rearrange("(p a) -> p a", a=1)).then_inc(s_aw, 16)
                        sp.dma_start(a_lnb[:, k:k + 1], ln_b[k * P:(k + 1) * P].rearrange("(p a) -> p a", a=1)).then_inc(s_aw, 16)
            with sp.Fori(0, E0) as e:
                sp.wait_ge(s_brawf, e + 1)
                sp.dma_start(b_raw[:, :, :], w12[bass.ds(e, 1), :, :].rearrange("e (a p) d -> p (e a) d", p=P)).then_inc(s_braw, 16)
                sp.wait_ge(s_braw3f, e + 1)
                sp.dma_start(b_raw3[:, :, :], w3[bass.ds(e, 1), :, :].rearrange("e (a p) h -> p (e a) h", p=P)).then_inc(s_braw3, 16)
            finish_stage(sp, 1)
            sp.dma_start(b_gw[:, :], gate0).then_inc(s_bw, 16)
            sp.wait_ge(s_const, 1)
            with sp.Fori(0, E1 * C1 // P) as r:
                sp.dma_start(routed1[bass.ds(r * P, P), :], zeros[:, :]).then_inc(s_dz, 16)
            sp.wait_ge(s_bplan, 1)
            for e in range(E0):
                row = sp.value_load(b_zrowi[0:1, e:e + 1], min_val=0, max_val=E0 * REGION - P)
                sp.dma_start(routed0[bass.ds(row, P), :], zeros[:, :]).then_inc(s_bzero, 16)
            sp.wait_ge(s_bzero, 16 * E0)
            sp.wait_ge(s_bscat, 16 * NT * K0)
            with sp.Fori(0, TILES0 // 2) as i:
                for j in range(2):
                    row = sp.value_load(b_rowi[0:1, bass.ds(i * 2 + j, 1)], min_val=0, max_val=E0 * REGION - P)
                    sp.wait_ge(s_btt, i * 2 + (j + 1))
                    sp.dma_start(b_xt[:, j, :], routed0[bass.ds(row, P), :]).then_inc(s_bin[j], 16)
            finish_stage(sp, 2)
            sp.dma_start(c_qkraw[0:DQ, :, :], Q).then_inc(s_cl, 16)
            sp.dma_start(c_qkraw[DQ:2 * DQ, :, :], K).then_inc(s_cl, 16)
            sp.dma_start(c_vraw[:, :, :], V).then_inc(s_cl, 16)
            sp.dma_start(c_wraw[:, :, :, :], W.rearrange("(k p) v h -> p k v h", p=P)).then_inc(s_cl, 16)

            def stage_weights(head, h):
                for n in range(2):
                    sp.dma_start(c_st[h][n][:, :, :].bitcast(F32), c_wqk[n][:, :, bass.ds(head, 1), :].rearrange("p k a c -> p k (a c)").bitcast(F32)).then_inc(s_cw[h], 16)

            def stage_v(head, h):
                sp.dma_start(c_vh[h][:, :, :], c_v[:, :, bass.ds(head * DQ, DQ)]).then_inc(s_cvh[h], 16)

            def head_operands(b, hp, h, nxt):
                H = b * NH + hp * 2 + h
                final = isinstance(hp, int) and hp == NPAIR - 1
                if not (final and h == 1):
                    sp.wait_ge(s_cPu, H * len(BLOCKS) + PBUF)
                    stage_v(hp * 2 + (h + 1), 1 - h)
                if nxt or not final:
                    sp.wait_ge(s_cqk, H * NC2 + NC2)
                    stage_weights(h if final else hp * 2 + (h + 2), h)

            def batch_operands(b, nxt):
                def pair_operands(hp):
                    for h in range(2):
                        head_operands(b, hp, h, nxt)
                sp.wait_ge(s_cve, b * 2 + 1)
                stage_v(0, 0)
                sp.wait_ge(s_cve, b * 2 + 2)
                sp.sem_inc(s_pass, 1)
                with sp.Fori(0, NPAIR - 1) as hp:
                    pair_operands(hp)
                pair_operands(NPAIR - 1)

            sp.wait_ge(s_cwl, 4 * NPAIR)
            for h in range(2):
                stage_weights(h, h)
            with sp.Fori(0, B - 1) as b:
                batch_operands(b, True)
            batch_operands(B - 1, False)
            finish_stage(sp, 3)
            sp.dma_start(d_raw[:, 0, :], sw1).then_inc(s_dl, 16)
            sp.dma_start(d_raw[:, 1, :], sw3).then_inc(s_dl, 16)
            sp.dma_start(d_raw2[:, :, :], sw2.rearrange("(k p) i -> p k i", p=P)).then_inc(s_dl, 16)
            sp.dma_start(d_gwraw[:, :], gate1).then_inc(s_dl, 16)
            sp.dma_start(d_bias[:, 0, :], bias1.rearrange("(a e) -> a e", a=1).broadcast_to([P, E1])).then_inc(s_dl, 16)

            def load_weights(e, q):
                sp.wait_ge(s_dec, e + 1)
                for n, w in enumerate((W1, W3)):
                    sp.dma_start(d_wb[:, q, n * D:(n + 1) * D].rearrange("p (k i) -> p k i", k=KD),
                                 w[bass.ds(e, 1), :, :].rearrange("e (k p) i -> p (e k) i", p=P)).then_inc(s_dw[q], 16)
                sp.dma_start(d_wb[:, q, 2 * D:3 * D], W2[bass.ds(e, 1), :, :].rearrange("e i d -> i (e d)")).then_inc(s_dw[q], 16)

            def load_rows(e, q):
                sp.wait_ge(s_det, e + 1)
                sp.dma_start(d_xe[:, q, :, :], routed1[bass.ds(e * C1, C1), :].rearrange("(a p) d -> p a d", p=P)).then_inc(s_dxe[q], 16)

            for q in range(EBUF):
                load_weights(q, q)
            sp.wait_ge(s_dscat, 16 * NT * K1)
            for q in range(EBUF):
                load_rows(q, q)
            with sp.Fori(0, E1 // EBUF - 1) as i:
                for q in range(EBUF):
                    e = i * EBUF + (q + EBUF)
                    load_rows(e, q)
                    load_weights(e, q)
            with sp.Fori(0, NG) as g:
                sp.wait_ge(s_x4, g * G + G)
                sp.dma_start(out_tiles[:, bass.ds(g * G, G), :], X[:, bass.ds(g * G, G), :]).then_inc(s_out, 16)
            sp.wait_ge(s_out, 16 * NG)

        @block.gpsimd
        def _(pool):
            st = Steps(pool, s_pool)
            st.done(pool.memset(ident[:, :], 0.0))
            st.done(pool.memset(identb[:, :], 0.0))
            st.done(pool.memset(ones[:, :], 1.0))
            st.done(pool.memset(onesb[:, :], 1.0))
            st.done(pool.memset(tri[:, :], 1.0))
            st.done(pool.memset(zeros[:, :], 0.0))
            st.done(pool.iota(iota[:, :], pattern=[[1, P]], base=0, channel_multiplier=0,
                              allow_small_or_imprecise_dtypes=True))
            st.sync()
            for m in (ident, identb):
                st.done(pool.affine_select(out=m[:, :], in_=m[:, :], compare_op=ALU.not_equal, fill=1.0,
                                           base=0, pattern=[[-1, P]], channel_multiplier=1))
            st.done(pool.affine_select(out=tri[:, :], in_=tri[:, :], compare_op=ALU.is_gt, fill=0.0,
                                       base=0, pattern=[[1, P]], channel_multiplier=-1))
            st.sync()
            pool.sem_inc(s_const, 1)
            finish_stage(pool, 1)
            with pool.Fori(0, NG // 2) as i:
                for j in range(2):
                    pool.wait_ge(s_bslot, i * 2 + (j + 1))
                    pool.sem_inc(s_pass, 1)
                    for q in range(G):
                        for k in range(K0):
                            pool.indirect_dma_start(
                                routed0, bass.IndirectOffsetOnAxis(ap=b_slot[j][:, q, k:k + 1], axis=0),
                                b_rows[j][:, q, :], None).then_inc(s_bscat, 16)
                    pool.wait_ge(s_bscat, (i * 2 + (j + 1)) * (16 * G * K0))
                    pool.sem_inc(s_bxnf, 1)
            finish_stage(pool, 2)
            st.done(pool.memset(c_maskq[:, :], 0.0))
            st.done(pool.memset(c_maskk[:, :], 0.0))
            st.done(pool.memset(c_block[:, :, :], -1.0))
            st.sync()
            st.done(pool.affine_select(out=c_maskq[:, :], in_=c_maskq[:, :], compare_op=ALU.is_ge, fill=1.0,
                                       base=0, pattern=[[-1, P]], channel_multiplier=1))
            st.done(pool.affine_select(out=c_maskk[:, :], in_=c_maskk[:, :], compare_op=ALU.is_ge, fill=1.0,
                                       base=0, pattern=[[1, P]], channel_multiplier=-1))
            st.done(pool.affine_select(out=c_block[:, :, :], in_=c_block[:, :, :], compare_op=ALU.is_equal, fill=0.0,
                                       base=0, pattern=[[-1, QT], [0, P]], channel_multiplier=1))
            st.sync()
            pool.sem_inc(s_cset, 1)
            with pool.Fori(0, NG) as g:
                st.loop(g, NG, G)
                for q in range(G):
                    pool.wait_ge(s_bgatf, g * G + (q + 1))
                    pool.sem_inc(s_pass, 1)
                    st.done(pool.tensor_copy(b_gi[:, q, :], b_gix[:, bass.ds(g * G + q, 1), :].rearrange("p a k -> p (a k)")))
                    st.sync()
                    pool.sem_inc(s_pass, 1)
                    for k in range(K0):
                        pool.indirect_dma_start(
                            b_gat[:, q, k, :], None, expert0,
                            bass.IndirectOffsetOnAxis(ap=b_gi[:, q, k:k + 1], axis=0)).then_inc(s_bgat[q], 16)
                st.end()

            def copy_k(H, h):
                pool.wait_ge(s_cqs, H * 6 + 6)
                pool.sem_inc(s_pass, 1)
                pool.tensor_copy(c_k2[h][0:DQ, :], c_k1[h][0:DQ, :].bitcast(F32)).then_inc(s_ck2, 1)

            def head_adds(b, hp, h, nxt):
                H = b * NH + hp * 2 + h
                final = isinstance(hp, int) and hp == NPAIR - 1
                for m, (c, j) in enumerate(BLOCKS):
                    off = max(0, j * P - c * 512)
                    pool.wait_ge(s_cP, H * len(BLOCKS) + (m + 3))
                    done, p = H * len(BLOCKS) + (m + PBUF), c_p[:, m % PBUF, 0:512 - off]
                    if j == 0:
                        pool.wait_ge(s_cD, H * NC2 + (c + 1))
                        pool.sem_inc(s_pass, 1)
                        if c == 0:
                            pool.tensor_copy(c_den[c][:, :], p).then_inc(s_cPa, 1)
                    elif j == 1 and c > 0:
                        pool.sem_inc(s_pass, 1)
                        pool.tensor_tensor(c_den[c][:, :], c_p[:, (m - 1) % PBUF, :], p, ALU.add).then_inc(s_cPa, 2)
                    else:
                        pool.wait_ge(s_cPa, done)
                        pool.sem_inc(s_pass, 1)
                        pool.tensor_tensor(c_den[c][:, off:], c_den[c][:, off:], p, ALU.add).then_inc(s_cPa, 1)
                    if m == 4 and (nxt or not (final and h == 1)):
                        copy_k(H + 1, 1 - h)

            def batch_adds(b, nxt):
                def pair_adds(hp):
                    for h in range(2):
                        head_adds(b, hp, h, nxt)
                pair_adds(0)
                with pool.Fori(0, NPAIR // 2 - 1) as i:
                    for n in range(2):
                        pair_adds(i * 2 + (n + 1))
                pair_adds(NPAIR - 1)

            pool.wait_ge(s_cset, 2)
            copy_k(0, 0)
            with pool.Fori(0, B - 1) as b:
                batch_adds(b, True)
            batch_adds(B - 1, False)
            finish_stage(pool, 3)
            pool.wait_ge(s_dl, 16 * 5)
            pool.tensor_copy(d_gwf[:, :], d_gwraw[:, :]).then_inc(s_dcast, 1)
            pool.tensor_copy(d_rawf[:, :, :], d_raw[:, :, :]).then_inc(s_dcast, 1)
            pool.tensor_copy(d_raw2f[:, :, :], d_raw2[:, :, :]).then_inc(s_dcast, 1)
            pool.wait_ge(s_dz, 16 * (E1 * C1 // P))
            with pool.Fori(0, NG // 2) as i:
                for j in range(2):
                    pool.wait_ge(s_dslot, i * 2 + (j + 1))
                    pool.sem_inc(s_pass, 1)
                    for q in range(G):
                        for k in range(K1):
                            pool.indirect_dma_start(
                                routed1, bass.IndirectOffsetOnAxis(ap=d_slot[j][:, q, k:k + 1], axis=0),
                                d_rows[j][:, q, :], None, bounds_check=E1 * C1 - 1, oob_is_err=False).then_inc(s_dscat, 16)
                    pool.wait_ge(s_dscat, (i * 2 + (j + 1)) * (16 * G * K1))
                    pool.sem_inc(s_dxnf, 1)
            with pool.Fori(0, E1 // EBUF) as i:
                for q in range(EBUF):
                    pool.wait_ge(s_dw[q], i * 48 + 48)
                    pool.wait_ge(s_dey, i * EBUF + (q + 1))
                    pool.sem_inc(s_pass, 1)
                    pool.tensor_copy(d_wf[:, q, :], d_wb[:, q, :]).then_inc(s_dec, 1)
            for j in range(2):
                pool.wait_ge(s_dyst[j], 16 * (E1 // 2) + 16)
            with pool.Fori(0, NG) as g:
                st.loop(g, NG, G)
                for q in range(G):
                    pool.wait_ge(s_dgatf, g * G + (q + 1))
                    pool.sem_inc(s_pass, 1)
                    st.done(pool.tensor_copy(d_gi[:, q, :], d_gix[:, bass.ds(g * G + q, 1), :].rearrange("p a k -> p (a k)")))
                    st.sync()
                    pool.sem_inc(s_pass, 1)
                    for k in range(K1):
                        pool.indirect_dma_start(
                            d_gat[:, q, k, :], None, expert1,
                            bass.IndirectOffsetOnAxis(ap=d_gi[:, q, k:k + 1], axis=0)).then_inc(s_dgat[q], 16)
                st.end()

        def take_experts(act, e0):
            with act.Fori(0, E0P) as f:
                for k in range(KD):
                    act.wait_ge(s_btw, (e0 + f) * 3 + (1 + k))
                    act.activation(b_w12T[:, k, bass.ds((e0 + f) * (2 * H0), 2 * H0)],
                                   PS[:, 2 * k:2 * k + 2, :].rearrange("p a n -> p (a n)"), ACT.Copy).then_inc(s_bwe, 1)
                act.wait_ge(s_btw, (e0 + f) * 3 + 3)
                for k in range(KH):
                    act.activation(b_w3T[:, k, bass.ds((e0 + f) * D, D)], PS[:, 4 + k // 2, (k % 2) * D:(k % 2 + 1) * D],
                                   ACT.Copy).then_inc(s_bwe, 1)

        @block.scalar
        def _(act):
            st = Steps(act, s_act)
            act.wait_ge(s_awt, 1)
            st.done(act.activation(a_wT[:, :, :, :].rearrange("p k g n -> p (k g n)"), PS[:, 0, 0:KD * 4 * N], ACT.Copy))
            for h in range(2):
                st.done(act.activation(a_wpT[h][h * N:(h + 1) * N, :], PS[0:N, 1, 0:D], ACT.Copy, scale=0.5))
            act.wait_ge(s_aw, 16 * 18)
            st.done(act.activation(a_hbo[:, :], a_bias[:, 3:4], ACT.Copy, scale=0.5))
            st.sync()
            act.sem_inc(s_awe, 1)
            act.sem_inc(s_afree, 1)
            with act.Fori(0, B // 2) as p:
                for g in range(GP):
                    act.wait_ge(s_atp, p * GP + (g + 1))
                    for k in range(KD):
                        act.activation(a_xT[:, k, g * GT:(g + 1) * GT], PS[:, 6 - 2 * (g % 2) + k, :], ACT.Identity,
                                       bias=a_lnb[:, k:k + 1], scale=a_lnw[:, k:k + 1]).then_inc(s_axT, 1)
                take_experts(act, p * (2 * E0P))
                act.wait_ge(s_afree, p + 1)
                for g in range(4):
                    act.wait_ge(s_agate, p * 4 + (g + 1))
                    dst = (a_lf, a_li, a_z, a_o)[g]
                    fn = (ACT.Identity, ACT.Identity, ACT.Tanh, ACT.Tanh)[g]
                    src = PS[:, 2 * (g % 2):2 * (g % 2) + 2, :].rearrange("p a n -> p (a n)")
                    act.activation(dst[:, :], src, fn, bias=a_hbo[:, 0:1] if g == 3 else a_bias[:, g:g + 1],
                                   scale=0.5 if g == 3 else 1.0).then_inc(s_agev, 1)
                act.wait_ge(s_ascan, p * 3 + 1)
                act.activation(a_fs[:, :], a_fs[:, :], ACT.Exp).then_inc(s_aexp, 1)
                act.wait_ge(s_ascan, p * 3 + 2)
                act.activation(a_is[:, :], a_is[:, :], ACT.Exp).then_inc(s_aexp, 1)
                take_experts(act, p * (2 * E0P) + E0P)
                act.wait_ge(s_ascan, p * 3 + 3)
                act.activation(a_c[:, :], a_c[:, :], ACT.Tanh).then_inc(s_aexp, 1)
            finish_stage(act, 1)
            act.wait_ge(s_bgt, 1)
            act.activation(b_gwT[:, :, :].rearrange("p k e -> p (k e)"), PS[:, 6, 0:KD * E0], ACT.Copy).then_inc(s_bge, 1)
            def take_xT(g, j):
                act.wait_ge(s_btp, g + 1)
                act.activation(b_xT[j][:, :, :].rearrange("p k t -> p (k t)"),
                               PS[:, 6:8, :].rearrange("p a n -> p (a n)"), ACT.Copy).then_inc(s_bxT, 1)

            def router_exps(g, j, follows):
                act.wait_ge(s_bgap, g + 1)
                act.activation(b_ex[:, :], b_gap[:, :], ACT.Exp).then_inc(s_bex, 1)
                if follows:
                    take_xT(g + 1, 1 - j)

            take_xT(0, 0)
            with act.Fori(0, NG // 2 - 1) as i:
                for j in range(2):
                    router_exps(i * 2 + j, j, True)
            for j in range(2):
                router_exps(NG - 2 + j, j, j == 0)
            for j in range(2):
                act.sem_inc(s_bst[j], 16)

            def take_rows(n, j):
                act.wait_ge(s_btt, n + 3)
                act.activation(b_tT[:, j, :, :].rearrange("p k t -> p (k t)"), PS[:, 4, 0:D], ACT.Copy).then_inc(s_btT, 1)

            def tanh_half(n, j):
                act.wait_ge(s_bh1, n + 1)
                act.activation(b_sg[:, j, :], PS[:, 2 * j, :], ACT.Tanh, scale=0.5).then_inc(s_bsg, 1)

            def take_hidden(n, j):
                act.wait_ge(s_bht, n + 1)
                act.activation(b_hT[:, j, :, :].rearrange("p k t -> p (k t)"), PS[:, 5, :], ACT.Copy).then_inc(s_bhT, 1)

            def store_y(n, half, j):
                act.wait_ge(s_by, n + 1)
                act.wait_ge(s_bst[j], half * 16 + 16)
                act.activation(b_y[:, j, :], PS[:, 6 + j, 0:D], ACT.Copy).then_inc(s_bye, 1)
                act.wait_ge(s_bye, n + 3)
                act.dma_start(expert0[bass.ds(n * P, P), :], b_y[:, j, :]).then_inc(s_bst[j], 16)

            take_rows(0, 0)
            tanh_half(0, 0)
            take_rows(1, 1)
            with act.Fori(0, TILES0 // 2 - 1) as i:
                for j in (1, 0):
                    n, half = i * 2 + (2 - j), i + (1 - j)
                    tanh_half(n, j)
                    take_hidden(n - 1, 1 - j)
                    take_rows(n + 1, 1 - j)
                    store_y(n - 1, i, 1 - j)
            last = TILES0 - 1
            tanh_half(last, 1)
            take_hidden(last - 1, 0)
            store_y(last - 1, TILES0 // 2 - 1, 0)
            take_hidden(last, 1)
            store_y(last, TILES0 // 2 - 1, 1)
            for j in range(2):
                act.wait_ge(s_bst[j], 16 * (TILES0 // 2) + 16)
            finish_stage(act, 2)
            act.wait_ge(s_cl, 16 * 4)
            with act.Fori(0, NPAIR) as hp:
                for h in range(2):
                    head = bass.ds(hp * 2 + h, 1)
                    act.activation(c_qkst[h][:, :], c_qkraw[:, :, head].rearrange("p d a -> p (d a)"), ACT.Copy).then_inc(s_cst, 1)
                    act.activation(c_vst[h][:, :], c_vraw[:, :, head].rearrange("p d a -> p (d a)"), ACT.Copy).then_inc(s_cst, 1)
                for k in range(KD):
                    act.activation(c_wst[:, k, :, :], c_wraw[:, k, :, bass.ds(hp * 2, 2)].rearrange("p v h -> p h v"), ACT.Copy).then_inc(s_cst, 1)
                for h in range(2):
                    head = hp * 2 + h
                    act.wait_ge(s_cwt, hp * 5 + (2 * h + 1))
                    act.activation(c_wqk[0][:, :, bass.ds(head, 1), :].rearrange("p k a c -> p k (a c)"),
                                   PS[:, 2 * h, 0:KD * P].rearrange("p (k c) -> p k c", k=KD), ACT.Copy).then_inc(s_cwh, 1)
                    act.wait_ge(s_cwt, hp * 5 + (2 * h + 2))
                    act.activation(c_wv[0][:, :, bass.ds(head * DQ, DQ)],
                                   PS[:, 2 * h + 1, 0:KD * DQ].rearrange("p (k c) -> p k c", k=KD), ACT.Copy).then_inc(s_cwh, 1)
                act.wait_ge(s_cwt, hp * 5 + 5)
                act.activation(c_wo[:, bass.ds(hp, 1), :].rearrange("p a d -> p (a d)"), PS[:, 4, 0:D], ACT.Copy).then_inc(s_cwh, 1)
            act.wait_ge(s_cset, 2)

            def take_xT(batch, g):
                for k in range(KD):
                    act.wait_ge(s_ctp, batch * (KD * S // GT) + (g * KD + k + 1))
                    act.activation(c_xT[0][:, k, g * GT:(g + 1) * GT], PS[:, 2 + k, :], ACT.Copy).then_inc(s_cxh, 1)

            def take_v(batch, a, heads, pairs):
                for t in range(QT):
                    act.wait_ge(s_cv, batch * (2 * QT) + (a * QT + t + 1))
                    act.activation(c_v[:, t, a * 512:(a + 1) * 512], PS[:, 2 + t % 2, :], ACT.Copy).then_inc(s_turn[t % 2], 1)
                for r in range(2):
                    act.wait_ge(s_turn[r], turns(r, heads=heads, pairs=pairs, vs=batch, xts=batch + 1) + ((a + 1) * (QT // 2) + 1))
                act.sem_inc(s_cve, 1)

            def split_hi(H, h, c, part):
                cols = slice(c * 512, (c + 1) * 512)
                act.wait_ge(s_cqk, H * NC2 + (c + 1))
                dst, src = ((c_q1[h][DQ:P, cols], PS[0:DQ, c, :]), (c_q1[h][0:DQ, cols], PS[0:DQ, c, :]),
                            (c_k1[h][0:DQ, cols], PS[DQ:P, c, :]))[part]
                act.activation(dst, src, ACT.Copy).then_inc(s_cqs, 1)

            def head_exps(b, hp, h, nxt):
                H = b * NH + hp * 2 + h
                final = isinstance(hp, int) and hp == NPAIR - 1
                for m, (c, j) in enumerate(BLOCKS):
                    off = max(0, j * P - c * 512)
                    skip = P if off == 512 - P else 0
                    act.wait_ge(s_cT, H * len(BLOCKS) + (m + 1))
                    act.wait_ge(s_cPu, H * len(BLOCKS) + (m + 1))
                    act.wait_ge(s_cPa, H * len(BLOCKS) + (m + 1))
                    act.activation(c_p[:, m % PBUF, 0:512 - off], PS[:, 4 + m % 2, skip:skip + 512 - off], ACT.Exp,
                                   scale=ATT_SCALE).then_inc(s_cP, 1)
                    if m == 0 and (nxt or not (final and h == 1)):
                        split_hi(H + 1, 1 - h, 1, 2)
                    if m in (6, 7, 8, 10, 11) and (nxt or not final):
                        c = 0 if m <= 8 else 1
                        act.wait_ge(s_cT, H * len(BLOCKS) + (len(BLOCKS) if c else 8))
                        split_hi(H + 2, h, c, m - (10 if c else 6))
                    if nxt and final and h == 0 and m in (1, 2):
                        if m == 1:
                            act.wait_ge(s_cqk, (b * NH + NH) * NC2)
                        take_xT(b + 1, m - 1)

            def batch_exps(b, nxt):
                def pair_exps(hp):
                    for h in range(2):
                        head_exps(b, hp, h, nxt)
                pair_exps(0)
                with act.Fori(0, NPAIR // 2 - 1) as i:
                    for n in range(2):
                        pair_exps(i * 2 + (n + 1))
                pair_exps(NPAIR - 1)
                if nxt:
                    for a in range(2):
                        take_v(b + 1, a, b * NH + (NH + 1), b * NPAIR + (NPAIR - 1 + a))

            for g in range(S // GT):
                take_xT(0, g)
            for a in range(2):
                take_v(0, a, 0, 0)
            for n in range(6):
                split_hi(0, 0, n // 3, n % 3)
            for n in range(5):
                split_hi(1, 1, n // 3, n % 3)
            with act.Fori(0, B - 1) as b:
                batch_exps(b, True)
            batch_exps(B - 1, False)
            finish_stage(act, 3)
            act.wait_ge(s_dwt, 1)
            st.done(act.activation(d_gwT[:, :, :].rearrange("p k e -> p (k e)"), PS[:, 0, 0:KD * E1], ACT.Copy))
            st.done(act.activation(d_s1T[:, :, :, :].rearrange("p k a i -> p (k a i)"), PS[:, 1, 0:KD * 2 * I1], ACT.Copy))
            st.done(act.activation(d_s2T[:, :], PS[:, 2, 0:D], ACT.Copy))
            st.sync()
            act.sem_inc(s_dwe, 1)

            def group_tanhs(g, j):
                act.wait_ge(s_dtp, g + 1)
                act.activation(d_xT[j][:, :, :].rearrange("p k t -> p (k t)"),
                               PS[:, 6:8, :].rearrange("p a n -> p (a n)"), ACT.Copy).then_inc(s_dxT, 1)
                act.wait_ge(s_dsc, g + 1)
                act.activation(d_th[:, :, :].rearrange("p g e -> p (g e)"), PS[:, j, 0:G * E1], ACT.Tanh, scale=0.5).then_inc(s_dth, 1)
                act.wait_ge(s_dsh, g + 1)
                act.activation(d_sth[:, :], PS[:, 3, :], ACT.Tanh, scale=0.5).then_inc(s_dst, 1)

            with act.Fori(0, NG // 2) as i:
                for j in range(2):
                    group_tanhs(i * 2 + j, j)

            def take_rows(e, j):
                act.wait_ge(s_det, e + (EBUF + 1))
                act.activation(d_xeT[:, j, :, :].rearrange("p k c -> p (k c)"), PS[:, j, :], ACT.Copy).then_inc(s_deT, 1)

            def tanh_half(e, j):
                act.wait_ge(s_deh, e + 1)
                act.activation(d_eth[:, j, :], PS[:, 2 + j, 0:C1], ACT.Tanh, scale=0.5).then_inc(s_deth, 1)

            def store_y(e, half, j):
                act.wait_ge(s_dey, e + (EBUF + 1))
                act.wait_ge(s_dyst[j], half * 16 + 16)
                act.activation(d_y[:, j, :, :].rearrange("p a d -> p (a d)"), PS[:, 4 + j, :], ACT.Copy).then_inc(s_dye, 1)
                act.wait_ge(s_dye, e + 3)
                act.dma_start(expert1[bass.ds(e * C1, C1), :].rearrange("(a p) d -> p a d", p=P), d_y[:, j, :, :]).then_inc(s_dyst[j], 16)

            def expert_step(e, half, j):
                tanh_half(e, j)
                if not (isinstance(e, int) and e == E1 - 1):
                    take_rows(e + 1, 1 - j)
                store_y(e - 1, half, 1 - j)

            for j in range(2):
                act.sem_inc(s_dyst[j], 16)
            take_rows(0, 0)
            tanh_half(0, 0)
            take_rows(1, 1)
            with act.Fori(0, E1 // EBUF - 1) as i:
                for r in range(EBUF):
                    expert_step(i * EBUF + (r + 1), i * (EBUF // 2) + r // 2, (r + 1) % 2)
            for e in range(E1 - EBUF + 1, E1):
                expert_step(e, (e - 1) // 2, e % 2)
            store_y(E1 - 1, (E1 - 1) // 2, 1)

        @block.vector
        def _(dve):
            st = Steps(dve, s_dve)
            st.done(dve.memset(a_m[:, 0:1], 0.0))
            for b in range(2):
                st.done(dve.memset(a_wpT[b][(1 - b) * N:(2 - b) * N, :], 0.0))

            def x_statistics(p, loads):
                for n in range(2 * QT):
                    if n % G == 0 and n // G < len(loads):
                        dve.wait_ge(s_x[loads[n // G]], 16)
                    st.done(dve.bn_stats(a_xstat[:, n, :], tile_of(p * (2 * QT), n)))
                st.sync()
                dve.memset(rtmp[:, :], 0.0)
                for n in range(2 * QT):
                    st.done(dve.bn_aggr(a_xmv[:, n, :], a_xstat[:, n, :]))
                st.sync()
                st.done(dve.tensor_scalar(a_var[:, :], a_xmv[:, :, 1], 1.0 + EPS, EPS * EPS, ALU.mult, ALU.add))
                st.sync()
                rsqrt(dve, st, a_var, a_rstd, a_tmp)

            def batch_pair(p, follows):
                for g in range(GP):
                    if g >= 2:
                        dve.wait_ge(s_atp, p * GP + (g - 1))
                    for q in range(G):
                        n = g * G + q
                        dve.tensor_scalar(a_rows[g % 2][:, q, :], tile_of(p * (2 * QT), n), a_xmv[:, n, 0:1], a_rstd[:, n:n + 1],
                                          ALU.subtract, ALU.mult).then_inc(s_axn, 1)
                dve.wait_ge(s_aw, 16 * 18)
                dve.wait_ge(s_axn, p * (2 * QT) + 2 * QT)
                for n in range(2 * QT):
                    st.done(dve.tensor_tensor(tile_of(p * (2 * QT), n), tile_of(p * (2 * QT), n), a_bp[:, :], ALU.add))
                if follows:
                    for g in range(GP, NG):
                        dve.wait_ge(s_x[g], 16)
                    dve.sem_inc(s_pass, 1)
                    x_statistics(p + 1, ())
                dve.wait_ge(s_agev, p * 4 + 1)
                st.done(dve.tensor_scalar(a_lf[:, :], a_lf[:, :], -20.0, 20.0, ALU.max, ALU.min))
                dve.wait_ge(s_agev, p * 4 + 2)
                st.done(dve.tensor_scalar(a_li[:, :], a_li[:, :], -20.0, 20.0, ALU.max, ALU.min))
                st.sync()
                st.done(dve.tensor_tensor_scan(a_m[:, 1:], a_lf[:, :], a_li[:, :], 0.0, ALU.add, ALU.max))
                st.sync()
                st.done(dve.tensor_tensor(a_fs[:, :], a_m[:, 0:S], a_lf[:, :], ALU.add))
                st.sync()
                st.done(dve.tensor_tensor(a_fs[:, :], a_fs[:, :], a_m[:, 1:], ALU.subtract))
                st.sync()
                dve.sem_inc(s_ascan, 1)
                st.done(dve.tensor_tensor(a_is[:, :], a_li[:, :], a_m[:, 1:], ALU.subtract))
                st.sync()
                dve.sem_inc(s_ascan, 1)
                dve.wait_ge(s_agev, p * 4 + 4)
                dve.wait_ge(s_aexp, p * 3 + 2)
                st.done(dve.tensor_tensor(a_is[:, :], a_is[:, :], a_z[:, :], ALU.mult))
                st.sync()
                st.done(dve.tensor_tensor_scan(a_c[:, :], a_fs[:, :], a_is[:, :], 0.0, ALU.mult, ALU.add))
                st.sync()
                dve.sem_inc(s_ascan, 1)
                dve.wait_ge(s_aexp, p * 3 + 3)
                st.done(dve.scalar_tensor_tensor(a_h[:, :], a_o[:, :], 1.0, a_c[:, :], ALU.add, ALU.mult))
                st.sync()
                dve.sem_inc(s_ah, 1)
                for n in range(2 * QT):
                    dve.wait_ge(s_ay, p * (2 * QT) + (n + 1))
                    dve.tensor_tensor(tile_of(p * (2 * QT), n), PS[:, 4 + n % 2, 0:D], tile_of(p * (2 * QT), n),
                                      ALU.add).then_inc(s_x1, 1)
                    if n:
                        dve.wait_ge(s_x1, p * (2 * QT) + n)
                        dve.sem_inc(s_pass, 1)
                        st.done(dve.bn_stats(a_stat[:, n - 1, :], tile_of(p * (2 * QT), n - 1)))
                dve.wait_ge(s_x1, p * (2 * QT) + 2 * QT)
                dve.sem_inc(s_pass, 1)
                st.done(dve.bn_stats(a_stat[:, 2 * QT - 1, :], tile_of(p * (2 * QT), 2 * QT - 1)))
                collect_moments(dve, st, p * (2 * QT), 2 * QT, a_stat, a_mv)
                dve.sem_inc(s_afree, 1)

            PAIR_STEPS = 2 * QT + 9 + 2 * (2 * QT) + 2
            x_statistics(0, range(GP))
            with dve.Fori(0, B // 2 - 1) as p:
                st.loop(p, B // 2 - 1, PAIR_STEPS + 2 * (2 * QT) + 1 + RSQRT_STEPS)
                batch_pair(p, True)
                st.end()
            batch_pair(B // 2 - 1, False)
            finish_stage(dve, 1)
            st.done(dve.memset(b_sum[:, :], 0.0))
            st.sync()
            all_rstds(dve, st)
            dve.sem_inc(s_bxnf, 2)

            def rows_of(g, j):
                dve.wait_ge(s_bxnf, g + 1)
                apply_norm(dve, g * G, b_rows[j], s_bxn)

            def route_group(g, j, follows):
                dve.wait_ge(s_bsc, g + 1)
                st.done(dve.tensor_copy(b_s8[:, :, :].rearrange("p g e -> p (g e)"), PS[:, 2 * j, 0:G * E0]))
                st.sync()
                dve.memset(rtmp[:, :], 0.0)
                for q in range(G):
                    st.done(dve.max(b_top[:, q, :], b_s8[:, q, :]))
                st.sync()
                dve.memset(rtmp[:, :], 0.0)
                for q in range(G):
                    st.done(dve.max_index(b_ix[:, q, :], b_top[:, q, :], b_s8[:, q, :]))
                st.done(dve.tensor_tensor(b_gap[:, :], b_top[:, :, 1], b_top[:, :, 0], ALU.subtract))
                st.sync()
                dve.sem_inc(s_bgap, 1)
                idx = b_idx[:, :, 0].rearrange("p (g k) -> p g k", g=G)
                st.done(dve.tensor_copy(idx, b_ix[:, :, 0:K0]))
                st.sync()
                st.done(dve.tensor_copy(b_idxA[:, bass.ds(g * G, G), :], idx))
                st.done(dve.tensor_tensor(b_oh[:, :, :, :].rearrange("p g k e -> p (g k) e"),
                                          iota[:, 0:E0].rearrange("p (a e) -> p a e", a=1).broadcast_to([P, G * K0, E0]),
                                          b_idx[:, :, :].broadcast_to([P, G * K0, E0]), ALU.is_equal))
                st.sync()
                st.done(dve.tensor_tensor(b_ohs[:, :, :], b_oh[:, :, 0, :], b_oh[:, :, 1, :], ALU.add))
                st.sync()
                dve.sem_inc(s_boh, 1)
                st.done(dve.tensor_reduce(b_gsum[:, :], b_ohs[:, :, :].rearrange("p g e -> p e g"), AX_X, ALU.add))
                dve.wait_ge(s_bpre, g + 1)
                pre = PS[:, 1, 0:G * E0].rearrange("p (g e) -> p g e", g=G)
                for k in range(K0):
                    st.done(dve.tensor_tensor(b_tmp[:, :, k, :], b_oh[:, :, k, :], pre, ALU.mult))
                st.sync()
                st.done(dve.tensor_tensor(b_sum[:, :], b_sum[:, :], b_gsum[:, :], ALU.add))
                st.done(dve.tensor_reduce(b_pos[:, :, :].rearrange("p g k -> p (g k)"),
                                          b_tmp[:, :, :, :].rearrange("p g k e -> p (g k) e"), AX_X, ALU.add))
                st.sync()
                st.done(dve.scalar_tensor_tensor(b_slot[j][:, :, :], idx, float(REGION), b_pos[:, :, :], ALU.mult, ALU.add))
                st.sync()
                dve.sem_inc(s_bslot, 1)
                if follows:
                    rows_of(g + 1, 1 - j)
                st.done(dve.tensor_copy(b_posA[:, bass.ds(g * G, G), :], b_pos[:, :, :]))
                dve.wait_ge(s_bex, g + 1)
                st.done(dve.tensor_scalar(b_den[:, :], b_ex[:, :], 1.0, None, ALU.add))
                st.sync()
                st.done(dve.reciprocal(b_den[:, :], b_den[:, :]))
                st.sync()
                st.done(dve.tensor_copy(b_prA[:, bass.ds(g * G, G), 0], b_den[:, :]))
                st.done(dve.tensor_tensor(b_prA[:, bass.ds(g * G, G), 1], b_den[:, :], b_ex[:, :], ALU.mult))
                st.sync()

            rows_of(0, 0)
            with dve.Fori(0, NG // 2 - 1) as i:
                st.loop(i, NG // 2 - 1, 2 * (2 * G + K0 + 15))
                for j in range(2):
                    route_group(i * 2 + j, j, True)
                st.end()
            for j in range(2):
                route_group(NG - 2 + j, j, j == 0)
            dve.sem_inc(s_boh, 1)
            dve.wait_ge(s_bcnt, 1)
            st.done(dve.tensor_copy(b_cnt[:, :], PS[:, 0, 0:E0]))
            st.sync()
            st.done(dve.tensor_scalar(b_nti[:, :], b_cnt[:, :], float(P - 1), None, ALU.add))
            st.done(dve.scalar_tensor_tensor(b_zrow[:, :], iota[:, 0:E0], float(REGION), b_cnt[:, :], ALU.mult, ALU.add))
            st.sync()
            st.done(dve.tensor_copy(b_zrowi[:, :], b_zrow[:, :]))
            st.done(dve.tensor_scalar(b_nti[:, :], b_nti[:, :], P.bit_length() - 1, None, ALU.logical_shift_right))
            st.sync()
            st.done(dve.tensor_copy(b_nt[:, :], b_nti[:, :]))
            st.sync()
            st.done(dve.tensor_tensor_scan(b_end[:, :], ones[:, 0:E0], b_nt[:, :], 0.0, ALU.mult, ALU.add))
            st.sync()
            st.done(dve.tensor_tensor(b_start[:, :], b_end[:, :], b_nt[:, :], ALU.subtract))
            tiles = iota[:, 0:TILES0]
            st.done(dve.memset(b_te[:, :], 0.0))
            st.done(dve.memset(b_ts[:, :], 0.0))
            for e in range(E0 - 1):
                st.sync()
                st.done(dve.tensor_scalar(b_tt[:, :], tiles, b_end[:, e:e + 1], b_end[:, e:e + 1], ALU.is_ge, ALU.mult))
                st.done(dve.scalar_tensor_tensor(b_te[:, :], tiles, b_end[:, e:e + 1], b_te[:, :], ALU.is_ge, ALU.add))
                st.sync()
                st.done(dve.tensor_tensor(b_ts[:, :], b_ts[:, :], b_tt[:, :], ALU.max))
            st.sync()
            st.done(dve.tensor_copy(b_tei[:, :], b_te[:, :]))
            st.done(dve.tensor_tensor(b_tt[:, :], tiles, b_ts[:, :], ALU.subtract))
            st.sync()
            st.done(dve.tensor_scalar(b_tt[:, :], b_tt[:, :], float(P), None, ALU.mult))
            st.sync()
            st.done(dve.scalar_tensor_tensor(b_tt[:, :], b_te[:, :], float(REGION), b_tt[:, :], ALU.mult, ALU.add))
            st.sync()
            st.done(dve.tensor_scalar(b_ts[:, :], tiles, b_end[:, E0 - 1:E0], None, ALU.is_lt))
            st.done(dve.tensor_scalar(b_tt[:, :], b_tt[:, :], b_zrow[:, E0 - 1:E0], None, ALU.subtract))
            st.sync()
            st.done(dve.tensor_tensor(b_tt[:, :], b_tt[:, :], b_ts[:, :], ALU.mult))
            st.sync()
            st.done(dve.tensor_scalar(b_rowi[:, :], b_tt[:, :], b_zrow[:, E0 - 1:E0], None, ALU.add))
            st.sync()
            dve.sem_inc(s_bplan, 1)
            for e in range(E0):
                st.done(dve.tensor_scalar(b_gtmp[:, :, :], b_idxA[:, :, :], float(e), b_start[:, e:e + 1],
                                          ALU.is_equal, ALU.mult))
                st.sync()
                st.done(dve.scalar_tensor_tensor(b_posA[:, :, :], b_gtmp[:, :, :], float(P), b_posA[:, :, :],
                                                 ALU.mult, ALU.add))
                st.sync()
            st.done(dve.tensor_copy(b_gix[:, :, :], b_posA[:, :, :]))
            st.sync()
            dve.sem_inc(s_bplan, 1)
            with dve.Fori(0, TILES0 // 2) as i:
                st.loop(i, TILES0 // 2, 2)
                for j in range(2):
                    dve.wait_ge(s_bsg, i * 2 + (j + 1))
                    st.done(dve.scalar_tensor_tensor(b_hid[:, j, :], b_sg[:, j, :], 1.0, PS[:, 2 * j, :], ALU.add, ALU.mult))
                    st.sync()
                    dve.wait_ge(s_bh2, i * 2 + (j + 1))
                    dve.scalar_tensor_tensor(b_hid[:, j, :], b_hid[:, j, :], 0.5, PS[:, 2 * j + 1, :], ALU.mult,
                                             ALU.mult).then_inc(s_bhid, 1)
                st.end()
            finish_stage(dve, 2)
            assert NPAIR == NG
            dve.sem_inc(s_bgatf, G)
            with dve.Fori(0, NG) as g:
                st.loop(g, NG, G + LN_STEPS + 2)
                for h in range(2):
                    head = g * 2 + h
                    dve.wait_ge(s_cwh, g * 5 + (2 * h + 1))
                    ws = [w[:, :, bass.ds(head, 1), :].rearrange("p k a c -> p k (a c)") for w in c_wqk]
                    dve.tensor_tensor(ws[1], PS[:, 2 * h, 0:KD * P].rearrange("p (k c) -> p k c", k=KD), ws[0].bitcast(F32),
                                      ALU.subtract).then_inc(s_cwl, 1)
                    dve.wait_ge(s_cwh, g * 5 + (2 * h + 2))
                    ws = [w[:, :, bass.ds(head * DQ, DQ)] for w in c_wv]
                    dve.tensor_tensor(ws[1], PS[:, 2 * h + 1, 0:KD * DQ].rearrange("p (k c) -> p k c", k=KD), ws[0].bitcast(F32),
                                      ALU.subtract).then_inc(s_cwl, 1)
                for q in range(G):
                    t = tile_of(g * G, q)
                    dve.wait_ge(s_bgat[q], g * (16 * K0) + 16 * K0)
                    st.done(dve.scalar_tensor_tensor(t, b_gat[:, q, 0, :], b_prA[:, bass.ds(g * G + q, 1), 0], t, ALU.mult, ALU.add))
                    st.sync()
                    dve.scalar_tensor_tensor(t, b_gat[:, q, 1, :], b_prA[:, bass.ds(g * G + q, 1), 1], t, ALU.mult,
                                             ALU.add).then_inc(s_x2, 1)
                    dve.wait_ge(s_x2, g * G + (q + 1))
                    dve.sem_inc(s_bgatf, 1)
                group_statistics(dve, st, g * G, 1.0, EPS)
                st.done(dve.tensor_copy(means[:, bass.ds(g * G, G)], mv[:, :, 0]))
                st.done(dve.tensor_copy(rstds[:, bass.ds(g * G, G)], rstd[:, :]))
                st.sync()
                st.end()
            dve.wait_ge(s_cset, 1)
            dve.wait_ge(s_cwh, 5 * NPAIR)
            for m in (c_maskq, c_maskk):
                st.done(dve.tensor_scalar(m[:, :], m[:, :], BIG, None, ALU.mult))
            for h in range(2):
                st.done(dve.memset(c_q2[h][DQ:P, :].bitcast(F32), 0.0))
                st.done(dve.memset(c_k2[h][DQ:P, :].bitcast(F32), 0.0))
            st.sync()
            for h in range(2):
                st.done(dve.memset(c_k2[h][DQ:DQ + QT, :].bitcast(F32), 1.0))
            st.sync()
            dve.sem_inc(s_cset, 1)

            def make_xn(batch, g):
                if g:
                    dve.wait_ge(s_ctp, batch * (KD * S // GT) + g * KD)
                for q in range(G):
                    t = batch * QT + (g * G + q)
                    dve.tensor_scalar(xn[:, q, :], tile_of(t, 0), means[:, bass.ds(t, 1)], rstds[:, bass.ds(t, 1)],
                                      ALU.subtract, ALU.mult).then_inc(s_cxn, 1)

            def low_xT(batch, g):
                for k in range(KD):
                    dve.wait_ge(s_cxh, batch * (KD * S // GT) + (g * KD + k + 1))
                    dve.tensor_tensor(c_xT[1][:, k, g * GT:(g + 1) * GT], PS[:, 2 + k, :],
                                      c_xT[0][:, k, g * GT:(g + 1) * GT].bitcast(F32), ALU.subtract).then_inc(s_turn[k], 1)

            def split_lo(H, h, c, k):
                cols = slice(c * 512, (c + 1) * 512)
                dst, rows, hi = ((c_q2[h][0:DQ, cols], slice(0, DQ), c_q1[h]), (c_k1[h][DQ:P, cols], slice(DQ, P), c_k1[h]))[k]
                dve.wait_ge(s_cqs, H * 6 + (c * 3 + k + 2))
                dve.tensor_tensor(dst, PS[rows, c, :], hi[0:DQ, cols].bitcast(F32), ALU.subtract).then_inc(s_cks, 1)

            def maximum(H, n):
                t, c = CHUNKS[n]
                w = min(512, (t + 1) * P - c * 512)
                dst = c_max[:, t:t + 1] if t < QT // 2 else c_max2[:, c, t - QT // 2:t - QT // 2 + 1]
                dve.wait_ge(s_cS, H * len(CHUNKS) + (n + 1))
                dve.tensor_reduce(dst, PS[:, 2 + n % 2, 0:w], AX_X, ALU.max).then_inc(s_turn[n % 2], 1)

            def max_rows(H, h, used):
                for r in range(2):
                    dve.wait_ge(s_turn[r], used[r] + 1)
                dve.tensor_tensor(c_max[:, QT // 2:QT], c_max2[:, 0, :], c_max2[:, 1, :], ALU.max).then_inc(s_cmx, 1)
                dve.wait_ge(s_cmT, H + 1)
                dve.tensor_tensor(c_q2[h][DQ:DQ + QT, :].rearrange("p (t q) -> p t q", t=QT),
                                  PS[0:QT, 2:3, 0:P].broadcast_to([QT, QT, P]), c_block[:, :, :], ALU.mult).then_inc(s_turn[0], 1)
                dve.wait_ge(s_turn[0], used[0] + 2)
                dve.sem_inc(s_cm, 1)

            def normalise_y(H, h, c, yT):
                dve.wait_ge(s_cD, H * NC2 + (c + 1 + NC2))
                dve.wait_ge(s_cyn, H * (2 * NC2) + (2 * c + 2 * NC2))
                dve.reciprocal(c_rden[:, :], PS[:, 6 + c, 256:512]).then_inc(s_cr, 1)
                dve.wait_ge(s_cr, H * NC2 + (c + 1))
                for a in range(2):
                    dst = yT[h * DQ:(h + 1) * DQ, c * 512:(c + 1) * 512].rearrange("p (n a q) -> p n a q", n=2, a=2)[:, :, a, :]
                    dve.tensor_tensor(dst, PS[a * DQ:(a + 1) * DQ, 6 + c, 0:256].rearrange("p (n q) -> p n q", n=2),
                                      c_rden[a * DQ:(a + 1) * DQ, :].rearrange("p (n q) -> p n q", n=2), ALU.mult).then_inc(s_cyn, 1)

            def add_z(b, pair):
                for n in range(QT // 2):
                    dve.wait_ge(s_cz, pair * (QT // 2) + (n + 1))
                    x = X[:, bass.ds(b * QT + 2 * n, 2), :].rearrange("p a d -> p (a d)")
                    dve.scalar_tensor_tensor(x, PS[:, 2 + n % 2, :], Z_SCALE, x, ALU.mult, ALU.add).then_inc(s_turn[n % 2], 1)

            def head_steps(b, hp, h, nxt, first, par):
                pair = b * NPAIR + hp
                H = pair * 2 + h
                final = isinstance(hp, int) and hp == NPAIR - 1
                fetch = nxt and final
                follows = nxt or not (final and h == 1)
                zs = h == 0 and not first
                if fetch and h == 0:
                    make_xn(b + 1, 0)
                    split_lo(H + 1, 1 - h, 1, 0)
                    make_xn(b + 1, 1)
                    split_lo(H + 1, 1 - h, 1, 1)
                    for g in range(S // GT):
                        low_xT(b + 1, g)
                    for n in range(4):
                        maximum(H + 1, n)
                elif follows:
                    for k in range(2):
                        for n in range(k * 2, k * 2 + 2):
                            maximum(H + 1, n)
                        split_lo(H + 1, 1 - h, 1, k)
                if h == 1 or not first:
                    normalise_y(H - 1, 1 - h, 1, c_yT[par if h else 1 - par])
                if follows:
                    for n in range(4, 10):
                        maximum(H + 1, n)
                normalise_y(H, h, 0, c_yT[par])
                if follows:
                    for n in range(10, len(CHUNKS)):
                        maximum(H + 1, n)
                    max_rows(H + 1, 1 - h, [turns(r, heads=H + 1, pairs=pair - 1 if zs else pair, vs=b + 1,
                                                  xts=b + (2 if fetch else 1)) + len(CHUNKS) // 2 for r in range(2)])
                if nxt or not final:
                    for k in range(2):
                        split_lo(H + 2, h, 0, k)
                if zs:
                    add_z(b, pair - 1)

            def batch_steps(b, nxt):
                def pair_steps(hp, first, par):
                    for h in range(2):
                        head_steps(b, hp, h, nxt, first, par)
                pair_steps(0, True, 0)
                with dve.Fori(0, NPAIR // 2 - 1) as i:
                    for n in range(2):
                        pair_steps(i * 2 + (n + 1), False, 1 - n)
                pair_steps(NPAIR - 1, False, 1)
                normalise_y(b * NH + (NH - 1), 1, 1, c_yT[1])
                add_z(b, b * NPAIR + (NPAIR - 1))
                for r in range(2):
                    dve.wait_ge(s_turn[r], turns(r, heads=b * NH + (NH + 1 if nxt else NH), pairs=b * NPAIR + NPAIR,
                                                 vs=b + 1, xts=b + (2 if nxt else 1)) + (QT // 2 + 1 if nxt else 1))
                for g in range(QT // G):
                    dve.sem_inc(s_pass, 1)
                    for q in range(G):
                        st.done(dve.bn_stats(stat[:, q, :], tile_of(b * QT + g * G, q)))
                    collect_moments(dve, st, b * QT + g * G, G, stat, mv)

            for g in range(S // GT):
                make_xn(0, g)
                low_xT(0, g)
            for n in range(4):
                split_lo(0, 0, n // 2, n % 2)
            for n in range(len(CHUNKS)):
                maximum(0, n)
            max_rows(0, 0, [turns(r, heads=0, pairs=0, vs=1, xts=1) + len(CHUNKS) // 2 for r in range(2)])
            for k in range(2):
                split_lo(1, 1, 0, k)
            with dve.Fori(0, B - 1) as b:
                st.loop(b, B - 1, (QT // G) * (2 * G + 2))
                batch_steps(b, True)
                st.end()
            batch_steps(B - 1, False)
            finish_stage(dve, 3)
            all_rstds(dve, st)
            st.done(dve.memset(d_sum[:, :], 0.0))
            st.sync()
            dve.sem_inc(s_dxnf, 2)
            dve.wait_ge(s_dl, 16 * 5)

            def rows_of(g, j):
                dve.wait_ge(s_dxnf, g + 1)
                apply_norm(dve, g * G, d_rows[j], s_dxn)

            def route_group(g, j, follows):
                dve.wait_ge(s_dth, g + 1)
                st.done(dve.tensor_scalar(d_sc[:, :, :], d_th[:, :, :], 0.5, 0.5, ALU.mult, ALU.add))
                st.sync()
                st.done(dve.tensor_tensor(d_sel[:, :, :], d_sc[:, :, :], d_bias[:, :, :].broadcast_to([P, G, E1]), ALU.add))
                st.sync()
                dve.memset(rtmp[:, :], 0.0)
                for q in range(G):
                    st.done(dve.max(d_top[:, q, :], d_sel[:, q, :]))
                st.sync()
                dve.memset(rtmp[:, :], 0.0)
                for q in range(G):
                    st.done(dve.max_index(d_ix[:, q, :], d_top[:, q, :], d_sel[:, q, :]))
                st.sync()
                idx = d_idx[:, :, 0].rearrange("p (g k) -> p g k", g=G)
                st.done(dve.tensor_copy(idx, d_ix[:, :, 0:K1]))
                st.sync()
                st.done(dve.tensor_tensor(d_oh[:, :, :, :].rearrange("p g k e -> p (g k) e"),
                                          iota[:, 0:E1].rearrange("p (a e) -> p a e", a=1).broadcast_to([P, G * K1, E1]),
                                          d_idx[:, :, :].broadcast_to([P, G * K1, E1]), ALU.is_equal))
                st.sync()
                st.done(dve.tensor_reduce(d_ohf[:, :, :], d_oh[:, :, :, :].rearrange("p g k e -> p g e k"), AX_X, ALU.add))
                st.sync()
                st.done(dve.tensor_copy(d_ohs[:, :, :], d_ohf[:, :, :]))
                st.sync()
                dve.sem_inc(s_doh, 1)
                st.done(dve.tensor_reduce(d_gsum[:, :], d_ohs[:, :, :].rearrange("p g e -> p e g"), AX_X, ALU.add))
                for k in range(K1):
                    st.done(dve.tensor_tensor(d_tmp2[:, :, k, :], d_oh[:, :, k, :], d_sc[:, :, :], ALU.mult))
                dve.wait_ge(s_dpre, g + 1)
                pre = PS[:, 2, 0:G * E1].rearrange("p (g e) -> p g e", g=G)
                for k in range(K1):
                    st.done(dve.tensor_tensor(d_tmp[:, :, k, :], d_oh[:, :, k, :], pre, ALU.mult))
                st.sync()
                st.done(dve.tensor_tensor(d_sum[:, :], d_sum[:, :], d_gsum[:, :], ALU.add))
                st.done(dve.tensor_reduce(d_pos[:, :, :].rearrange("p g k -> p (g k)"),
                                          d_tmp[:, :, :, :].rearrange("p g k e -> p (g k) e"), AX_X, ALU.add))
                st.sync()
                st.done(dve.tensor_scalar(d_skip[:, :, :], d_pos[:, :, :], float(C1), float(BIGSLOT), ALU.is_ge, ALU.mult))
                st.done(dve.tensor_scalar(d_ok[:, :, :], d_pos[:, :, :], float(C1), None, ALU.is_lt))
                st.done(dve.tensor_scalar(d_cl[:, :, :], d_pos[:, :, :], float(C1 - 1), None, ALU.min))
                st.sync()
                st.done(dve.tensor_tensor(d_skip[:, :, :], d_skip[:, :, :], d_pos[:, :, :], ALU.add))
                st.done(dve.scalar_tensor_tensor(d_gix[:, bass.ds(g * G, G), :], idx, float(C1), d_cl[:, :, :], ALU.mult, ALU.add))
                st.sync()
                st.done(dve.scalar_tensor_tensor(d_slot[j][:, :, :], idx, float(C1), d_skip[:, :, :], ALU.mult, ALU.add))
                st.sync()
                dve.sem_inc(s_dslot, 1)
                if follows:
                    rows_of(g + 1, 1 - j)
                st.done(dve.tensor_reduce(d_w[:, :, :].rearrange("p g k -> p (g k)"),
                                          d_tmp2[:, :, :, :].rearrange("p g k e -> p (g k) e"), AX_X, ALU.add))
                st.sync()
                st.done(dve.tensor_reduce(d_ws[:, :], d_w[:, :, :], AX_X, ALU.add))
                st.sync()
                st.done(dve.tensor_scalar(d_ws[:, :], d_ws[:, :], 1e-12, None, ALU.max))
                st.sync()
                st.done(dve.reciprocal(d_ws[:, :], d_ws[:, :]))
                st.sync()
                for q in range(G):
                    st.done(dve.tensor_scalar(d_w[:, q, :], d_w[:, q, :], d_ws[:, q:q + 1], None, ALU.mult))
                st.sync()
                st.done(dve.tensor_tensor(d_wA[:, bass.ds(g * G, G), :], d_w[:, :, :], d_ok[:, :, :], ALU.mult))
                dve.wait_ge(s_dst, g + 1)
                st.done(dve.scalar_tensor_tensor(d_sh[:, :], d_sth[:, :], 1.0, PS[:, 3, :], ALU.add, ALU.mult))
                st.sync()
                st.done(dve.scalar_tensor_tensor(d_sh[:, :], d_sh[:, :], 0.5, PS[:, 4, :], ALU.mult, ALU.mult))
                st.sync()
                dve.sem_inc(s_dsg, 1)
                for n in range(G // 2):
                    x = X[:, bass.ds(g * G + 2 * n, 2), :].rearrange("p a d -> p (a d)")
                    dve.wait_ge(s_dsy, g * (G // 2) + (n + 1))
                    dve.tensor_tensor(x, PS[:, 5, :], x, ALU.add).then_inc(s_dsa, 1)

            rows_of(0, 0)
            with dve.Fori(0, NG // 2 - 1) as i:
                st.loop(i, NG // 2 - 1, 2 * (3 * G + 2 * K1 + 22))
                for j in range(2):
                    route_group(i * 2 + j, j, True)
                st.end()
            for j in range(2):
                route_group(NG - 2 + j, j, j == 0)
            with dve.Fori(0, E1 // 2) as i:
                st.loop(i, E1 // 2, 2)
                for j in range(2):
                    dve.wait_ge(s_deth, i * 2 + (j + 1))
                    st.done(dve.scalar_tensor_tensor(d_eh[:, j, :], d_eth[:, j, :], 1.0, PS[:, 2 + j, 0:C1], ALU.add, ALU.mult))
                    st.sync()
                    dve.scalar_tensor_tensor(d_eh[:, j, :], d_eh[:, j, :], 0.5, PS[:, 2 + j, C1:2 * C1], ALU.mult, ALU.mult).then_inc(s_deg, 1)
                st.end()
            dve.sem_inc(s_dgatf, G)
            dve.wait_ge(s_dsa, NT // 2)
            with dve.Fori(0, NG) as g:
                st.loop(g, NG, G * (K1 - 1))
                for q in range(G):
                    t = tile_of(g * G, q)
                    dve.wait_ge(s_dgat[q], g * (16 * K1) + 16 * K1)
                    for k in range(K1):
                        ins = dve.scalar_tensor_tensor(t, d_gat[:, q, k, :], d_wA[:, bass.ds(g * G + q, 1), k], t, ALU.mult, ALU.add)
                        if k < K1 - 1:
                            st.done(ins)
                            st.sync()
                    ins.then_inc(s_x4, 1)
                    dve.wait_ge(s_x4, g * G + (q + 1))
                    dve.sem_inc(s_dgatf, 1)
                st.end()

        def transpose_experts(pe, e0, gates=None):
            with pe.Fori(0, E0P) as f:
                if gates is not None:
                    pe.wait_ge(s_agev, gates)
                pe.wait_ge(s_braw, (e0 + f) * 16 + 16)
                for k in range(KD):
                    for a in range(HT):
                        ins = pe.transpose(PS[:, 2 * k + a // 4, (a % 4) * P:(a % 4 + 1) * P], b_raw[:, a, k * P:(k + 1) * P], ident[:, :])
                    ins.then_inc(s_btw, 1)
                pe.wait_ge(s_btw, (e0 + f) * 3 + 2)
                pe.sem_inc(s_brawf, 1)
                pe.wait_ge(s_braw3, (e0 + f) * 16 + 16)
                for k in range(KH):
                    for a in range(KD):
                        c = (k % 2) * D + a * P
                        ins = pe.transpose(PS[:, 4 + k // 2, c:c + P], b_raw3[:, a, k * P:(k + 1) * P], ident[:, :])
                ins.then_inc(s_btw, 1)
                pe.wait_ge(s_btw, (e0 + f) * 3 + 3)
                pe.sem_inc(s_braw3f, 1)
                pe.wait_ge(s_bwe, (e0 + f) * (KD + KH) + KD + KH)

        @block.tensor
        def _(pe):
            pe.wait_ge(s_const, 1)
            pe.sem_inc(s_brawf, 1)
            pe.sem_inc(s_braw3f, 1)
            pe.wait_ge(s_aw, 16 * 18)
            for k in range(KD):
                for g in range(4):
                    c = (k * 4 + g) * N
                    pe.transpose(PS[:, 0, c:c + N], a_wraw[:, g, k * P:(k + 1) * P], ident[0:N, 0:N])
            for k in range(KD):
                ins = pe.transpose(PS[0:N, 1, k * P:(k + 1) * P], a_wpraw[:, k, :], ident[:, :])
            ins.then_inc(s_awt, 1)
            pe.wait_ge(s_awe, 1)
            with pe.Fori(0, B // 2) as p:
                for g in range(GP):
                    pe.wait_ge(s_axn, p * (GP * G) + G * (g + 1))
                    if g >= 2:
                        pe.wait_ge(s_axT, (p * GP + (g - 1)) * KD)
                    transpose_group(pe, 6 - 2 * (g % 2), a_rows[g % 2]).then_inc(s_atp, 1)
                pe.wait_ge(s_axT, (p * GP + GP) * KD)
                pe.sem_inc(s_pass, 1)
                transpose_experts(pe, p * (2 * E0P))
                for g in range(4):
                    if g >= 2:
                        pe.wait_ge(s_agev, p * 4 + (g - 1))
                    for c in range(NC2):
                        for b in range(2):
                            for k in range(KD):
                                ins = pe.matmul(PS[b * N:(b + 1) * N, 2 * (g % 2) + c, :], a_wT[:, k, g, :],
                                                a_xT[:, k, b * S + c * 512:b * S + (c + 1) * 512],
                                                start=(k == 0), stop=(k == KD - 1))
                    ins.then_inc(s_agate, 1)
                transpose_experts(pe, p * (2 * E0P) + E0P, p * 4 + 4)
                pe.wait_ge(s_ah, p + 1)
                for n in range(2 * QT):
                    b, t = n // QT, n % QT
                    if n >= 2:
                        pe.wait_ge(s_x1, p * (2 * QT) + (n - 1))
                    pe.matmul(PS[:, 4 + n % 2, 0:D], a_h[:, t * P:(t + 1) * P], a_wpT[b][:, :], start=True, stop=True).then_inc(s_ay, 1)
                pe.wait_ge(s_x1, p * (2 * QT) + 2 * QT)
            finish_stage(pe, 1)
            pe.wait_ge(s_bw, 16)
            for k in range(KD):
                ins = pe.transpose(PS[:, 6, k * E0:(k + 1) * E0], b_gw[:, k * P:(k + 1) * P], ident[0:E0, 0:E0])
            ins.then_inc(s_bgt, 1)
            pe.wait_ge(s_bge, 1)

            def router_scores(g, j):
                pe.wait_ge(s_bxn, g * G + G)
                if not (isinstance(g, int) and g == 0):
                    pe.wait_ge(s_bxT, g)
                transpose_group(pe, 6, b_rows[j]).then_inc(s_btp, 1)
                pe.wait_ge(s_bxT, g + 1)
                for q in range(G):
                    for k in range(KD):
                        ins = pe.matmul(PS[:, 2 * j, q * E0:(q + 1) * E0], b_xT[j][:, k, q * P:(q + 1) * P], b_gwT[:, k, :],
                                        start=(k == 0), stop=(k == KD - 1))
                ins.then_inc(s_bsc, 1)

            def count_before(g):
                pe.wait_ge(s_boh, g + 1)
                for q in range(G):
                    dst = PS[:, 1, q * E0:(q + 1) * E0]
                    pe.matmul(dst, onesb[:, :], b_sum[:, :], start=True, stop=False)
                    for r in range(q):
                        pe.matmul(dst, onesb[:, :], b_ohs[:, r, :], start=False, stop=False)
                    ins = pe.matmul(dst, tri[:, :], b_ohs[:, q, :], start=False, stop=True)
                ins.then_inc(s_bpre, 1)

            router_scores(0, 0)
            with pe.Fori(0, NG // 2 - 1) as i:
                for j in range(2):
                    count_before(i * 2 + j)
                    router_scores(i * 2 + (j + 1), 1 - j)
            count_before(NG - 2)
            router_scores(NG - 1, 1)
            count_before(NG - 1)
            pe.wait_ge(s_boh, NG + 1)
            pe.matmul(PS[:, 0, 0:E0], onesb[:, :], b_sum[:, :], start=True, stop=True).then_inc(s_bcnt, 1)
            pe.wait_ge(s_bplan, 2)
            pe.sem_inc(s_btt, 2)
            pe.sem_inc(s_bhid, 2)
            pe.sem_inc(s_bye, 2)

            def expert_of(n):
                return pe.value_load(b_tei[0:1, bass.ds(n, 1)], min_val=0, max_val=E0 - 1)

            def transpose_rows(n, half, j):
                pe.wait_ge(s_bin[j], half * 16 + 16)
                if not (isinstance(n, int) and n == 0):
                    pe.wait_ge(s_btT, n)
                for k in range(KD):
                    ins = pe.transpose(PS[:, 4, k * P:(k + 1) * P], b_xt[:, j, k * P:(k + 1) * P], ident[:, :])
                ins.then_inc(s_btt, 1)

            def hidden(n, j, c, e):
                if c == 0:
                    pe.wait_ge(s_btT, n + 1)
                    pe.wait_ge(s_bhid, n + 1)
                    pe.sem_inc(s_pass, 1)
                for k in range(KD):
                    ins = pe.matmul(PS[:, 2 * j + c, :], b_tT[:, j, k, :], b_w12T[:, k, bass.ds(e * (2 * H0) + c * H0, H0)],
                                    start=(k == 0), stop=(k == KD - 1))
                ins.then_inc((s_bh1, s_bh2)[c], 1)

            def transpose_hidden(n, j):
                pe.wait_ge(s_bhid, n + 3)
                for k in range(KH):
                    ins = pe.transpose(PS[:, 5, k * P:(k + 1) * P], b_hid[:, j, k * P:(k + 1) * P], ident[:, :])
                ins.then_inc(s_bht, 1)

            def second_layer(n, j, e):
                pe.wait_ge(s_bhT, n + 1)
                pe.wait_ge(s_bye, n + 1)
                pe.sem_inc(s_pass, 1)
                for k in range(KH):
                    ins = pe.matmul(PS[:, 6 + j, 0:D], b_hT[:, j, k, :], b_w3T[:, k, bass.ds(e * D, D)],
                                    start=(k == 0), stop=(k == KH - 1))
                ins.then_inc(s_by, 1)

            transpose_rows(0, 0, 0)
            e = expert_of(0)
            for c in range(2):
                hidden(0, 0, c, e)
            transpose_rows(1, 0, 1)
            with pe.Fori(0, TILES0 // 2 - 1) as i:
                for j in (1, 0):
                    n = i * 2 + (2 - j)
                    e = expert_of(n)
                    hidden(n, j, 0, e)
                    transpose_hidden(n - 1, 1 - j)
                    hidden(n, j, 1, e)
                    transpose_rows(n + 1, i + 1, 1 - j)
                    second_layer(n - 1, 1 - j, expert_of(n - 1))
            last = TILES0 - 1
            e = expert_of(last)
            hidden(last, 1, 0, e)
            transpose_hidden(last - 1, 0)
            hidden(last, 1, 1, e)
            second_layer(last - 1, 0, expert_of(last - 1))
            transpose_hidden(last, 1)
            second_layer(last, 1, expert_of(last))
            finish_stage(pe, 2)
            pe.sem_inc(s_cPu, PBUF)
            pe.sem_inc(s_cPa, PBUF)
            pe.sem_inc(s_cP, 2)
            pe.sem_inc(s_cyn, 2 * NC2)
            pe.sem_inc(s_cD, NC2)
            for r in range(2):
                pe.sem_inc(s_turn[r], 1)
            with pe.Fori(0, NPAIR) as hp:
                for h in range(2):
                    pe.wait_ge(s_cst, hp * (4 + KD) + (2 * h + 2))
                    for k in range(KD):
                        ins = pe.transpose(PS[:, 2 * h, k * P:(k + 1) * P], c_qkst[h][:, k * P:(k + 1) * P], ident[:, :])
                    ins.then_inc(s_cwt, 1)
                    for k in range(KD):
                        ins = pe.transpose(PS[:, 2 * h + 1, k * DQ:(k + 1) * DQ], c_vst[h][:, k * P:(k + 1) * P], ident[0:DQ, 0:DQ])
                    ins.then_inc(s_cwt, 1)
                pe.wait_ge(s_cst, hp * (4 + KD) + (4 + KD))
                for k in range(KD):
                    ins = pe.transpose(PS[:, 4, k * P:(k + 1) * P], c_wst[:, k, :, :].rearrange("p h v -> p (h v)"), ident[:, :])
                ins.then_inc(s_cwt, 1)
                pe.wait_ge(s_cwh, hp * 5 + 5)
                pe.wait_ge(s_cwl, hp * 4 + 4)
            pe.wait_ge(s_cset, 2)
            pe.sem_inc(s_pass, 1)
            parts = ((0, 0), (1, 0), (0, 1))

            def transpose_x(batch, g, use):
                pe.wait_ge(s_cxn, batch * QT + (g + 1) * G)
                for k in range(KD):
                    pe.wait_ge(s_turn[k], use[k] + (g + 1))
                    for q in range(G):
                        ins = pe.transpose(PS[:, 2 + k, q * P:(q + 1) * P], xn[:, q, k * P:(k + 1) * P], ident[:, :])
                    ins.then_inc(s_ctp, 1)

            def values(batch, a, use):
                for t in range(QT):
                    pe.wait_ge(s_turn[t % 2], use[t % 2] + (t // 2 + 1))
                    for n, (x, w) in enumerate(parts):
                        for k in range(KD):
                            ins = pe.matmul(PS[:, 2 + t % 2, :], c_xT[x][:, k, t * P:(t + 1) * P], c_wv[w][:, k, a * 512:(a + 1) * 512],
                                            start=(n == 0 and k == 0), stop=(n == 2 and k == KD - 1))
                    ins.then_inc(s_cv, 1)

            def project(nth, h, step, taken=None):
                c, n = step // len(parts), step % len(parts)
                w, x = parts[n]
                if step == 0:
                    pe.wait_ge(s_cw[h], nth * 32 + 32)
                if n == 0 and taken is not None:
                    pe.wait_ge(s_cks, taken + 2 * c)
                for k in range(KD):
                    ins = pe.matmul(PS[:, c, :], c_st[h][w][:, k, :], c_xT[x][:, k, c * 512:(c + 1) * 512],
                                    start=(n == 0 and k == 0), stop=(n == 2 and k == KD - 1))
                if n == len(parts) - 1:
                    ins.then_inc(s_cqk, 1)

            def scores(H, h, n, use):
                t, c = CHUNKS[n]
                w = min(512, (t + 1) * P - c * 512)
                if n in (0, 4):
                    pe.wait_ge(s_cks, H * 4 + (4 if n else 2))
                last = (t + 1) * P <= (c + 1) * 512
                pe.wait_ge(s_turn[n % 2], use[n % 2] + (n // 2 + 1))
                ins = pe.matmul(PS[:, 2 + n % 2, 0:max(w, 256)], c_q1[h][:, t * P:(t + 1) * P], c_k1[h][:, c * 512:c * 512 + max(w, 256)],
                                start=True, stop=not last)
                if last:
                    ins = pe.matmul(PS[:, 2 + n % 2, w - P:w], identb[:, :], c_maskq[:, :], start=False, stop=True)
                ins.then_inc(s_cS, 1)

            def transpose_max(H, use):
                pe.wait_ge(s_cmx, H + 1)
                pe.wait_ge(s_turn[0], use[0] + (len(CHUNKS) // 2 + 1))
                pe.transpose(PS[0:QT, 2, 0:P], c_max[:, :], ident[:, :]).then_inc(s_cmT, 1)

            def scores_t(H, h, m):
                c, j = BLOCKS[m]
                off = max(0, j * P - c * 512)
                skip = P if off == 512 - P else 0
                q = slice(c * 512 + off - skip, (c + 1) * 512)
                n = 512 - off + skip
                diagonal = j * P >= c * 512
                if m == 0:
                    pe.wait_ge(s_cm, H + 1)
                    pe.wait_ge(s_ck2, H + 1)
                pe.wait_ge(s_cP, H * len(BLOCKS) + (m + 1))
                pe.matmul(PS[:, 4 + m % 2, 0:n], c_k1[h][:, j * P:(j + 1) * P], c_q1[h][:, q], start=True, stop=False)
                ins = pe.matmul(PS[:, 4 + m % 2, 0:n], c_k2[h][:, j * P:(j + 1) * P], c_q2[h][:, q], start=False, stop=not diagonal)
                if diagonal:
                    ins = pe.matmul(PS[:, 4 + m % 2, skip:skip + P], identb[:, :], c_maskk[:, :], start=False, stop=True)
                ins.then_inc(s_cT, 1)

            def outputs(H, nth, h, m):
                c, j = BLOCKS[m]
                t0 = max(0, j - 4 * c)
                p = c_p[:, m % PBUF, :].rearrange("p (n a q) -> p n a q", n=2, a=2)
                if m == 0:
                    pe.wait_ge(s_cvh[h], nth * 16 + 16)
                pe.wait_ge(s_cP, H * len(BLOCKS) + (m + 3))
                for a in range(2):
                    tiles = [t for t in (a, a + 2) if t >= t0]
                    if not tiles:
                        continue
                    first, n = (tiles[0] - t0), len(tiles)
                    if n == 2:
                        moving = p[:, :, first % 2, :]
                        dst = PS[a * DQ:(a + 1) * DQ, 6 + c, 0:256].rearrange("p (n q) -> p n q", n=2)
                    else:
                        moving = c_p[:, m % PBUF, first * P:(first + 1) * P]
                        dst = PS[a * DQ:(a + 1) * DQ, 6 + c, P:2 * P]
                    ins = pe.matmul(dst, c_vh[h][:, j, :], moving, start=(j == 0), stop=(t0 == 2 + a))
                ins.then_inc(s_cPu, 1)

            def denominators(H, c):
                pe.wait_ge(s_cPa, H * len(BLOCKS) + (PBUF + (4, len(BLOCKS))[c]))
                d = c_den[c][:, :].rearrange("p (n a q) -> p n a q", n=2, a=2)
                for a in range(2):
                    ins = pe.matmul(PS[a * DQ:(a + 1) * DQ, 6 + c, 256:512].rearrange("p (n q) -> p n q", n=2),
                                    ones[:, 0:DQ], d[:, :, a, :], start=True, stop=True)
                ins.then_inc(s_cD, 1)

            def z_of(pair, hp, yT, n, use):
                pe.wait_ge(s_turn[n % 2], use[n % 2] + (n // 2 + 1))
                for a in range(2):
                    t = 2 * n + a
                    ins = pe.matmul(PS[:, 2 + n % 2, a * D:(a + 1) * D], yT[:, t * P:(t + 1) * P],
                                    c_wo[:, bass.ds(hp, 1), :].rearrange("p a d -> p (a d)"), start=True, stop=True)
                ins.then_inc(s_cz, 1)

            def head_products(b, hp, h, nxt, first, par):
                pair = b * NPAIR + hp
                H = pair * 2 + h
                final = isinstance(hp, int) and hp == NPAIR - 1
                fetch = nxt and final
                follows = nxt or not (final and h == 1)
                zs = h == 0 and not first
                use = [turns(r, heads=H + 1, pairs=pair - 1 if zs else pair, vs=b + 1, xts=b + (2 if fetch else 1)) for r in range(2)]
                chunks = {0: (0, 1), 1: (2, 3), 3: (4, 5), 4: (6, 7), 5: (8, 9), 6: (10, 11)}
                if fetch and h == 0:
                    chunks.update({0: (), 1: (), 2: (0, 1, 2, 3)})
                for m in range(len(BLOCKS)):
                    c, j = BLOCKS[m]
                    if m == 0 and (h or not first):
                        denominators(H - 1, 1)
                    if j == 0:
                        pe.wait_ge(s_cyn, H * (2 * NC2) + (2 * c + 2))
                    outputs(H, pair, h, m)
                    if m == 5:
                        denominators(H, 0)
                    if fetch and h == 0 and m < 2:
                        transpose_x(b + 1, m, [u - S // GT for u in use])
                    if follows:
                        for n in chunks.get(m, ()):
                            scores(H + 1, 1 - h, n, use)
                    if 3 <= m <= 8 and (nxt or not final):
                        if fetch and h == 0 and m == 3:
                            for k in range(KD):
                                pe.wait_ge(s_turn[k], use[k] + 1)
                        project(pair + 1, h, m - 3, H * 4 + 6)
                    if follows and m == 8:
                        transpose_max(H + 1, use)
                    if zs and m in (9, 10):
                        if m == 9:
                            pe.wait_ge(s_cyn, pair * (4 * NC2) + 2 * NC2)
                        used = [use[r] + (7, 6)[r] for r in range(2)]
                        for n in range((m - 9) * 2, (m - 9) * 2 + 2):
                            z_of(pair - 1, hp - 1, c_yT[1 - par], n, used)
                    if m + 2 < len(BLOCKS):
                        scores_t(H, h, m + 2)
                    elif follows:
                        scores_t(H + 1, 1 - h, m + 2 - len(BLOCKS))

            def batch_products(b, nxt):
                def pair_products(hp, first, par):
                    for h in range(2):
                        head_products(b, hp, h, nxt, first, par)
                pair_products(0, True, 0)
                with pe.Fori(0, NPAIR // 2 - 1) as i:
                    for n in range(2):
                        pair_products(i * 2 + (n + 1), False, 1 - n)
                pair_products(NPAIR - 1, False, 1)
                pair = b * NPAIR + (NPAIR - 1)
                heads = b * NH + (NH + 1 if nxt else NH)
                xts = b + (2 if nxt else 1)
                denominators(b * NH + (NH - 1), 1)
                use = [turns(r, heads=heads, pairs=pair, vs=b + 1, xts=xts) for r in range(2)]
                if nxt:
                    values(b + 1, 0, use)
                pe.wait_ge(s_cyn, pair * (4 * NC2) + 6 * NC2)
                for n in range(QT // 2):
                    z_of(pair, NPAIR - 1, c_yT[1], n, [u + (QT // 2 if nxt else 0) for u in use])
                if nxt:
                    values(b + 1, 1, [u + (QT // 2 + QT // 4) for u in use])

            for g in range(S // GT):
                transpose_x(0, g, [turns(r, heads=0, pairs=0, vs=0, xts=0) for r in range(2)])
            for k in range(KD):
                pe.wait_ge(s_turn[k], turns(k, heads=0, pairs=0, vs=0, xts=1) + 1)
            for a in range(2):
                values(0, a, [turns(r, heads=0, pairs=0, vs=0, xts=1) + a * (QT // 2) for r in range(2)])
            for step in range(NC2 * len(parts)):
                project(0, 0, step)
            use0 = [turns(r, heads=0, pairs=0, vs=1, xts=1) for r in range(2)]
            for n in range(len(CHUNKS)):
                scores(0, 0, n, use0)
            transpose_max(0, use0)
            for step in range(NC2 * len(parts)):
                project(0, 1, step, 2)
            for m in range(2):
                scores_t(0, 0, m)
            with pe.Fori(0, B - 1) as b:
                batch_products(b, True)
            batch_products(B - 1, False)
            finish_stage(pe, 3)
            pe.wait_ge(s_dcast, 3)
            for k in range(KD):
                pe.transpose(PS[:, 0, k * E1:(k + 1) * E1], d_gwf[:, k * P:(k + 1) * P], ident[0:E1, 0:E1])
                for a in range(2):
                    c = (k * 2 + a) * I1
                    pe.transpose(PS[:, 1, c:c + I1], d_rawf[:, a, k * P:(k + 1) * P], ident[:, :])
                ins = pe.transpose(PS[:, 2, k * P:(k + 1) * P], d_raw2f[:, k, :], ident[:, :])
            ins.then_inc(s_dwt, 1)
            pe.wait_ge(s_dwe, 1)
            for n, sem in ((EBUF, s_det), (EBUF, s_dec), (EBUF, s_dey), (2, s_deT), (2, s_deg), (2, s_dye)):
                pe.sem_inc(sem, n)

            def router_scores(g, j):
                pe.wait_ge(s_dxn, g * G + G)
                transpose_group(pe, 6, d_rows[j]).then_inc(s_dtp, 1)
                pe.wait_ge(s_dxT, g + 1)
                for q in range(G):
                    for k in range(KD):
                        ins = pe.matmul(PS[:, j, q * E1:(q + 1) * E1], d_xT[j][:, k, q * P:(q + 1) * P], d_gwT[:, k, :],
                                        start=(k == 0), stop=(k == KD - 1))
                ins.then_inc(s_dsc, 1)

            def shared_hidden(j):
                for a in range(2):
                    for k in range(KD):
                        ins = pe.matmul(PS[:, 3 + a, :], d_s1T[:, k, a, :], d_xT[j][:, k, :], start=(k == 0), stop=(k == KD - 1))
                ins.then_inc(s_dsh, 1)

            def count_before(g):
                pe.wait_ge(s_doh, g + 1)
                for q in range(G):
                    dst = PS[:, 2, q * E1:(q + 1) * E1]
                    pe.matmul(dst, onesb[:, :], d_sum[:, :], start=True, stop=False)
                    for r in range(q):
                        pe.matmul(dst, onesb[:, :], d_ohs[:, r, :], start=False, stop=False)
                    ins = pe.matmul(dst, tri[:, :], d_ohs[:, q, :], start=False, stop=True)
                ins.then_inc(s_dpre, 1)

            def shared_y(g):
                pe.wait_ge(s_dsg, g + 1)
                for n in range(G // 2):
                    if n or not (isinstance(g, int) and g == 0):
                        pe.wait_ge(s_dsa, g * (G // 2) + n)
                    for a in range(2):
                        q = 2 * n + a
                        ins = pe.matmul(PS[:, 5, a * D:(a + 1) * D], d_sh[:, q * P:(q + 1) * P], d_s2T[:, :], start=True, stop=True)
                    ins.then_inc(s_dsy, 1)

            def group_step(g, j, follows):
                count_before(g)
                if follows:
                    router_scores(g + 1, 1 - j)
                shared_y(g)
                if follows:
                    shared_hidden(1 - j)

            router_scores(0, 0)
            shared_hidden(0)
            for j in range(2):
                group_step(j, j, True)
            with pe.Fori(0, NG // 2 - 2) as i:
                for j in range(2):
                    group_step(i * 2 + (j + 2), j, True)
            for j in range(2):
                group_step(NG - 2 + j, j, j == 0)

            def transpose_rows(e, quarter, q):
                pe.wait_ge(s_dxe[q], quarter * 16 + 16)
                pe.wait_ge(s_deT, e + 1)
                for k in range(KD):
                    for a in range(C1 // P):
                        c = k * C1 + a * P
                        ins = pe.transpose(PS[:, q % 2, c:c + P], d_xe[:, q, a, k * P:(k + 1) * P], ident[:, :])
                ins.then_inc(s_det, 1)

            def hidden(e, q):
                pe.wait_ge(s_deT, e + 3)
                pe.wait_ge(s_dec, e + (EBUF + 1))
                pe.wait_ge(s_deg, e + 1)
                for a in range(2):
                    for k in range(KD):
                        c = a * D + k * I1
                        ins = pe.matmul(PS[:, 2 + q % 2, a * C1:(a + 1) * C1], d_wf[:, q, c:c + I1], d_xeT[:, q % 2, k, :],
                                        start=(k == 0), stop=(k == KD - 1))
                ins.then_inc(s_deh, 1)

            def second_layer(e, q):
                pe.wait_ge(s_deg, e + 3)
                pe.wait_ge(s_dye, e + 1)
                for a in range(C1 // P):
                    ins = pe.matmul(PS[:, 4 + q % 2, a * D:(a + 1) * D], d_eh[:, q % 2, a * P:(a + 1) * P], d_wf[:, q, 2 * D:3 * D],
                                    start=True, stop=True)
                ins.then_inc(s_dey, 1)

            transpose_rows(0, 0, 0)
            hidden(0, 0)
            transpose_rows(1, 0, 1)
            with pe.Fori(0, E1 // EBUF - 1) as i:
                for r in range(EBUF):
                    e = i * EBUF + (r + 1)
                    hidden(e, (r + 1) % EBUF)
                    transpose_rows(e + 1, i + (r + 2) // EBUF, (r + 2) % EBUF)
                    second_layer(e - 1, r)
            for e in range(E1 - EBUF + 1, E1):
                hidden(e, e % EBUF)
                if e + 1 < E1:
                    transpose_rows(e + 1, (e + 1) // EBUF, (e + 1) % EBUF)
                second_layer(e - 1, (e - 1) % EBUF)
            second_layer(E1 - 1, EBUF - 1)


_INS = ['L0_attn_x', 'L0_attn_ln_w', 'L0_attn_ln_b', 'L0_attn_Wi', 'L0_attn_bi', 'L0_attn_Wf', 'L0_attn_bf',
        'L0_attn_Wz', 'L0_attn_bz', 'L0_attn_Wo', 'L0_attn_bo', 'L0_attn_Wp', 'L0_attn_bp', 'L0_ffn_w12',
        'L0_ffn_w3', 'L0_ffn_gate_w', 'L1_attn_Q', 'L1_attn_K', 'L1_attn_V', 'L1_attn_W', 'L1_ffn_gate_w',
        'L1_ffn_bias', 'L1_ffn_W1', 'L1_ffn_W3', 'L1_ffn_W2', 'L1_ffn_sw1', 'L1_ffn_sw3', 'L1_ffn_sw2']
_OUTS = [((4, 1024, 256), 'float32')]


def kernel(**inputs):
    import numpy as _np
    import concourse.bacc as _bacc
    from concourse import mybir as _mybir
    from concourse.bass_utils import run_bass_kernel_spmd as _run

    nc = _bacc.Bacc("TRN2", target_bir_lowering=False, num_devices=1)
    arrays, args = {}, []
    for name in _INS:
        a = _np.ascontiguousarray(inputs[name])
        arrays[f"in_{name}_dram"] = a
        args.append(nc.dram_tensor(f"in_{name}_dram", a.shape, _mybir.dt.from_np(a.dtype), kind="ExternalInput").ap())
    for i, (shape, dtype) in enumerate(_OUTS):
        dt = _mybir.dt.from_np(_np.dtype(dtype))
        args.append(nc.dram_tensor(f"out_{i}_dram", shape, dt, kind="ExternalOutput").ap())
    network(nc, *args)
    r = _run(nc, [arrays], core_ids=[0])
    return r.results[0]["out_0_dram"]
```

```python
from contextlib import ExitStack

import concourse.bass as bass
from concourse import mybir

F32 = mybir.dt.float32
F32R = mybir.dt.float32r
BF16 = mybir.dt.bfloat16
I32 = mybir.dt.int32
U32 = mybir.dt.uint32
ALU = mybir.AluOpType
ACT = mybir.ActivationFunctionType
AX_X = mybir.AxisListType.X

P = 128
EPS = 1e-5
BIG = -1e30


class Steps:

    def __init__(self, eng, sem):
        self.eng, self.sem, self.base, self.n, self.i, self.per = eng, sem, 0, 0, None, 0

    def loop(self, i, rounds, per):
        assert self.i is None
        self.base += self.n
        self.n, self.i, self.rounds, self.per = 0, i, rounds, per

    def end(self):
        assert self.n == self.per, (self.n, self.per)
        self.base += self.rounds * self.per
        self.n, self.i = 0, None

    def done(self, ins):
        ins.then_inc(self.sem, 1)
        self.n += 1

    def sync(self):
        at = self.base + self.n
        self.eng.wait_ge(self.sem, at if self.i is None else self.i * self.per + at)


def network(nc, x_in, ln_w, ln_b, Wi, bi, Wf, bf, Wz, bz, Wo, bo, Wp, bp, w12, w3, gate0,
            Q, K, V, W, gate1, bias1, W1, W3, W2, sw1, sw3, sw2, out):
    B, S, D = x_in.shape
    T = B * S
    NT = T // P
    KD = D // P
    N = Wi.shape[0]
    E0, H0 = w12.shape[0], w3.shape[2]
    K0 = 2
    DQ, _, NH = Q.shape
    E1, _, I1 = W1.shape
    K1 = 4
    C1 = 2 * (2 * 512) * K1 // E1
    G = 4
    GT = G * P
    NG = T // GT
    KH = H0 // P
    HT = 2 * H0 // P
    REGION = T + P
    TILES0 = T * K0 // P + E0
    BIGSLOT = 1 << 20
    NPAIR = NH // 2
    QT = S // P
    NC2 = S // 512
    ATT_SCALE = (DQ / D) / DQ
    Z_SCALE = (DQ / D) ** 0.5 * (D / DQ) ** 0.5 / NH

    x_tiles = x_in.rearrange("b (i p) d -> p (b i) d", p=P)
    out_tiles = out.rearrange("b (i p) d -> p (b i) d", p=P)
    routed0 = nc.dram_tensor("routed0", (E0 * REGION, D), F32).ap()
    expert0 = nc.dram_tensor("expert0", (TILES0 * P, D), F32).ap()
    routed1 = nc.dram_tensor("routed1", (E1 * C1, D), F32).ap()
    expert1 = nc.dram_tensor("expert1", (E1 * C1, D), F32).ap()

    with ExitStack() as ctx:
        def sb(name, shape, dt=F32):
            return ctx.enter_context(nc.sbuf_tensor(name, shape, dt))

        def sem(name):
            return ctx.enter_context(nc.semaphore(name))

        X = sb("X", [P, NT, D])
        ident = sb("ident", [P, P])
        ones = sb("ones", [P, P])
        tri = sb("tri", [P, P], BF16)
        onesb = sb("onesb", [P, P], BF16)
        identb = sb("identb", [P, P], BF16)
        zeros = sb("zeros", [P, D])
        iota = sb("iota", [P, P])
        stat = sb("stat", [P, G, 6])
        mv = sb("mv", [P, G, 2])
        var = sb("var", [P, G])
        rstd = sb("rstd", [P, G])
        rtmp = sb("rtmp", [P, G])
        means = sb("means", [P, NT])
        variances = sb("variances", [P, NT])
        rstds = sb("rstds", [P, NT])
        rstds_tmp = sb("rstds_tmp", [P, NT])
        xn = sb("xn", [P, G, D])

        arena_at = (nc.sbuf_base + 31) // 32 * 32
        arena_size = (nc.sbuf_bytes_remaining - 128) // 4
        ctx.enter_context(nc.sbuf_tensor("arena", [P, arena_size], F32))
        at = [arena_at]

        def place(name, shape, dt=F32):
            n = 2 if dt == BF16 else 4
            for s in shape[1:]:
                n *= s
            t = nc.alloc_sbuf_tensor_at(name, shape, dt, offset=at[0])
            at[0] += (n + 31) // 32 * 32
            assert at[0] <= arena_at + 4 * arena_size, (name, at[0] - arena_at - 4 * arena_size)
            return t

        PS = ctx.enter_context(nc.psum_tensor("PS", [P, 8, 512], F32))

        b_w12T = place("b_w12T", [P, KD, E0 * 2 * H0])
        b_w3T = place("b_w3T", [P, KH, E0 * D])
        after_weights = at[0]
        b_raw = place("b_raw", [P, HT, D])
        b_raw3 = place("b_raw3", [P, KD, H0])

        a_xT = place("a_xT", [P, KD, 2 * S])
        a_wraw = place("a_wraw", [N, 4, D])
        a_wpraw = place("a_wpraw", [P, KD, N])
        a_wT = place("a_wT", [P, KD, 4, N])
        a_wpT = [place(f"a_wpT{b}", [P, D]) for b in range(2)]
        a_rows = [xn, place("a_rows1", [P, G, D])]
        a_xstat = place("a_xstat", [P, 2 * QT, 6])
        a_xmv = place("a_xmv", [P, 2 * QT, 2])
        a_var = place("a_var", [P, 2 * QT])
        a_rstd = place("a_rstd", [P, 2 * QT])
        a_tmp = place("a_tmp", [P, 2 * QT])
        a_bias = place("a_bias", [P, 4])
        a_hbo = place("a_hbo", [P, 1])
        a_bp = place("a_bp", [P, D])
        a_lnw = place("a_lnw", [P, KD])
        a_lnb = place("a_lnb", [P, KD])
        a_lf = place("a_lf", [P, S])
        a_li = place("a_li", [P, S])
        a_z = place("a_z", [P, S])
        a_o = place("a_o", [P, S])
        a_m = place("a_m", [P, 1 + S])
        a_fs = place("a_fs", [P, S])
        a_is = place("a_is", [P, S])
        a_stat = place("a_stat", [P, 2 * QT, 6])
        a_mv = place("a_mv", [P, 2 * QT, 2])
        a_c = a_lf
        a_h = a_li

        RBUF = 4
        at[0] = after_weights
        b_gw = place("b_gw", [E0, D])
        b_gwT = place("b_gwT", [P, KD, E0])
        router_at = at[0]
        b_xT = [place(f"b_xT{j}", [P, KD, GT]) for j in range(2)]
        b_rows = [xn] + [place(f"b_rows{n}", [P, G, D]) for n in range(1, RBUF)]
        b_s8 = place("b_s8", [P, G, E0])
        b_top = place("b_top", [P, G, 8])
        b_ix = place("b_ix", [P, G, 8], U32)
        b_idx = place("b_idx", [P, G * K0, 1])
        b_gap = place("b_gap", [P, G])
        b_ex = place("b_ex", [P, G])
        b_den = place("b_den", [P, G])
        b_oh = place("b_oh", [P, G, K0, E0])
        b_ohs = place("b_ohs", [P, G, E0], BF16)
        b_sum = place("b_sum", [P, E0], BF16)
        b_gsum = place("b_gsum", [P, E0])
        b_tmp = place("b_tmp", [P, G, K0, E0])
        b_pos = place("b_pos", [P, G, K0])
        b_slot = [place(f"b_slot{n}", [P, G, K0], U32) for n in range(RBUF)]
        b_posA = place("b_posA", [P, NT, K0])
        b_idxA = place("b_idxA", [P, NT, K0])
        b_gtmp = place("b_gtmp", [P, NT, K0])
        b_cnt = place("b_cnt", [P, E0])
        b_nti = place("b_nti", [P, E0], I32)
        b_nt = place("b_nt", [P, E0])
        b_end = place("b_end", [P, E0])
        b_start = place("b_start", [P, E0])
        b_zrow = place("b_zrow", [P, E0])
        b_zrowi = place("b_zrowi", [P, E0], I32)
        b_te = place("b_te", [P, TILES0])
        b_ts = place("b_ts", [P, TILES0])
        b_tt = place("b_tt", [P, TILES0])
        b_tei = place("b_tei", [P, TILES0], I32)
        b_rowi = place("b_rowi", [P, TILES0], I32)
        b_xt = place("b_xt", [P, 2, D])
        b_tT = place("b_tT", [P, 2, KD, P])
        b_sg = place("b_sg", [P, 2, H0])
        b_hid = place("b_hid", [P, 2, H0])
        b_hT = place("b_hT", [P, 2, KH, P])
        b_y = place("b_y", [P, 2, D])
        after_tiles = at[0]
        at[0] = (arena_at + 4 * arena_size - 4 * (G * K0 * (D + 1) + 2 * NT * K0)) // 32 * 32 - 64
        b_prA = place("b_prA", [P, NT, K0])
        b_gix = place("b_gix", [P, NT, K0], U32)
        b_gi = place("b_gi", [P, G, K0], U32)
        b_gat = place("b_gat", [P, G, K0, D])

        BLOCKS = [(c, j) for c in range(NC2) for j in range(4 * (c + 1))]
        CHUNKS = [(t, c) for t in range(QT) for c in range(t // 4 + 1)]
        PBUF = 4
        at[0] = arena_at
        c_wqk = [place(f"c_wqk{n}", [P, KD, NH, P], F32R) for n in ("_hi", "_lo")]
        c_wv = [place(f"c_wv{n}", [P, KD, NH * DQ], F32R) for n in ("_hi", "_lo")]
        c_wo = place("c_wo", [P, NPAIR, D])
        c_xT = [place(f"c_xT{n}", [P, KD, S], F32R) for n in ("_hi", "_lo")]
        c_st = [[place(f"c_st{n}_{h}", [P, KD, P], F32R) for n in ("_hi", "_lo")] for h in range(2)]
        c_maskq = place("c_maskq", [P, P], BF16)
        c_maskk = place("c_maskk", [P, P], BF16)
        c_block = place("c_block", [QT, QT, P], BF16)
        heads_at = at[0]
        c_q1 = [place(f"c_q1_{h}", [P, S], F32R) for h in range(2)]
        c_k1 = [place(f"c_k1_{h}", [P, S], F32R) for h in range(2)]
        c_q2 = [place(f"c_q2_{h}", [P, S], F32R) for h in range(2)]
        c_k2 = [place(f"c_k2_{h}", [P, S], F32R) for h in range(2)]
        c_v = place("c_v", [P, QT, NH * DQ])
        c_vh = [place(f"c_vh_{h}", [P, QT, DQ]) for h in range(2)]
        c_p = place("c_p", [P, PBUF, 512])
        c_den = [place(f"c_den_{c}", [P, 512]) for c in range(NC2)]
        c_max = place("c_max", [P, QT])
        c_max2 = place("c_max2", [P, 2, QT // 2])
        c_rden = place("c_rden", [P, 256])
        c_yT = [place(f"c_yT_{n}", [P, S]) for n in range(2)]
        RAW_STEPS = 16
        at[0] = router_at
        c_vraw = place("c_vraw", [DQ, D, NH])
        c_wraw = [place("c_wraw0", [P, DQ, NH])]
        at[0] = after_tiles
        c_qkraw = place("c_qkraw", [P, D, NH])
        c_wraw.append(place("c_wraw1", [P, DQ, NH]))
        at[0] = heads_at
        c_vst = [place(f"c_vst_{h}", [DQ, D]) for h in range(2)]
        c_qkst = [place(f"c_qkst_{h}", [P, D]) for h in range(2)]
        c_wst = place("c_wst", [P, KD, 2, DQ])

        at[0] = arena_at
        EBUF = 4
        d_raw = place("d_raw", [P, 2, D], BF16)
        d_raw2 = place("d_raw2", [P, KD, I1], BF16)
        d_gwraw = place("d_gwraw", [E1, D], BF16)
        d_rawf = place("d_rawf", [P, 2, D])
        d_raw2f = place("d_raw2f", [P, KD, I1])
        d_gwf = place("d_gwf", [E1, D])
        d_gwT = place("d_gwT", [P, KD, E1])
        d_s1T = place("d_s1T", [P, KD, 2, I1])
        d_s2T = place("d_s2T", [I1, D])
        d_bias = place("d_bias", [P, 1, E1])
        d_xT = [place(f"d_xT{j}", [P, KD, GT]) for j in range(2)]
        d_rows = [xn] + [place(f"d_rows{n}", [P, G, D]) for n in range(1, RBUF)]
        d_th = [place(f"d_th{j}", [P, G, E1]) for j in range(2)]
        d_sc = place("d_sc", [P, G, E1])
        d_sel = place("d_sel", [P, G, E1])
        d_top = place("d_top", [P, G, 8])
        d_ix = place("d_ix", [P, G, 8], U32)
        d_idx = place("d_idx", [P, G * K1, 1])
        d_oh = place("d_oh", [P, G, K1, E1])
        d_ohf = place("d_ohf", [P, G, E1])
        d_ohs = place("d_ohs", [P, G, E1], BF16)
        d_sum = place("d_sum", [P, E1], BF16)
        d_gsum = place("d_gsum", [P, E1])
        d_tmp = place("d_tmp", [P, G, K1, E1])
        d_tmp2 = place("d_tmp2", [P, G, K1, E1])
        d_pos = place("d_pos", [P, G, K1])
        d_w = place("d_w", [P, G, K1])
        d_ws = place("d_ws", [P, G])
        d_ok = place("d_ok", [P, G, K1])
        d_skip = place("d_skip", [P, G, K1])
        d_cl = place("d_cl", [P, G, K1])
        d_slot = [place(f"d_slot{n}", [P, G, K1], U32) for n in range(RBUF)]
        d_wA = place("d_wA", [P, NT, K1])
        d_gix = place("d_gix", [P, NT, K1], U32)
        d_sth = place("d_sth", [I1, GT])
        d_sh = place("d_sh", [I1, GT])
        d_xe = place("d_xe", [P, EBUF, C1 // P, D])
        d_wb = place("d_wb", [P, EBUF, 3 * D], BF16)
        d_wf = place("d_wf", [P, EBUF, 3 * D], F32R)
        d_xeT = [place(f"d_xeT{n}", [P, 2, KD, C1], F32R) for n in ("_hi", "_lo")]
        d_eth = place("d_eth", [I1, 2, C1])
        d_eh = place("d_eh", [I1, 2, C1])
        d_ehs = [place(f"d_eh{n}", [I1, 2, C1], F32R) for n in ("_hi", "_lo")]
        d_y = place("d_y", [P, 2, C1 // P, D])
        d_gi = place("d_gi", [P, G, K1], U32)
        d_gat = place("d_gat", [P, G, K1, D])

        stage_end = sem("stage_end")
        s_const = sem("constants_made")
        s_x = [sem(f"x_loaded{g}") for g in range(NG)]
        s_out = sem("out_stored")
        s_act = sem("act_steps")
        s_dve = sem("dve_steps")
        s_pool = sem("pool_steps")
        s_pass = sem("wait_passed")
        s_aw = sem("a_weights_loaded")
        s_wt = sem("small_weights_transposed")
        s_we = sem("small_weights_ready")
        s_axn = sem("a_xn_ready")
        s_atp = sem("a_xn_transposed")
        s_axT = sem("a_xT_ready")
        s_agate = sem("a_gate_ready")
        s_agev = sem("a_gate_taken")
        s_afree = sem("a_gate_buffers_free")
        s_ascan = sem("a_scan_step")
        s_aexp = sem("a_exp_ready")
        s_ah = sem("a_h_ready")
        s_ay = sem("a_proj_ready")
        s_x1 = sem("x1_ready")
        s_braw = sem("b_w12_loaded")
        s_braw3 = sem("b_w3_loaded")
        s_brawf = sem("b_w12_buffer_free")
        s_braw3f = sem("b_w3_buffer_free")
        s_btw = sem("b_weights_transposed")
        s_bwe = sem("b_weights_taken")
        s_bw = sem("b_router_loaded")
        s_bxn = sem("b_xn_ready")
        s_btp = sem("b_xn_transposed")
        s_bxT = sem("b_xT_ready")
        s_bsc = sem("b_scores_ready")
        s_bgap = sem("b_score_gap_ready")
        s_bex = sem("b_gap_exp_ready")
        s_boh = sem("b_onehot_ready")
        s_bpre = sem("b_prefix_ready")
        s_bslot = sem("b_slots_ready")
        s_bscat = [sem(f"b_rows_scattered{n}") for n in range(RBUF)]
        s_bxnf = sem("b_xn_free")
        s_bcnt = sem("b_counts_ready")
        s_bplan = sem("b_plan_ready")
        s_bzero = sem("b_tails_zeroed")
        s_bin = [sem(f"b_tile_loaded{j}") for j in range(2)]
        s_btt = sem("b_tile_transposed")
        s_btT = sem("b_tileT_ready")
        s_bh1 = sem("b_hidden1_ready")
        s_bh2 = sem("b_hidden2_ready")
        s_bsg = sem("b_sigmoid_exp_ready")
        s_bhid = sem("b_gated_ready")
        s_bht = sem("b_gated_transposed")
        s_bhT = sem("b_gatedT_ready")
        s_by = sem("b_y_ready")
        s_bye = sem("b_y_taken")
        s_bst = [sem(f"b_y_stored{j}") for j in range(2)]
        s_bgat = [sem(f"b_rows_gathered{j}") for j in range(G)]
        s_bgatf = sem("b_gather_buffer_free")
        s_x2 = sem("x2_ready")
        s_cl = sem("c_weights_loaded")
        s_cst = sem("c_weights_staged")
        s_cwt = sem("c_weights_transposed")
        s_cwh = sem("c_weights_hi_ready")
        s_cwl = sem("c_weights_lo_ready")
        s_cset = sem("c_constants_made")
        s_cxn = sem("c_xn_ready")
        s_ctp = sem("c_xn_transposed")
        s_cxh = sem("c_xT_hi_ready")
        s_cw = [sem(f"c_head_weights_staged{h}") for h in range(2)]
        s_cqk = sem("c_qk_ready")
        s_cqs = sem("c_qk_hi_ready")
        s_cks = sem("c_qk_lo_ready")
        s_ck2 = sem("c_k2_ready")
        s_cv = sem("c_v_ready")
        s_cve = sem("c_v_taken")
        s_cvh = [sem(f"c_head_v_staged{h}") for h in range(2)]
        s_cS = sem("c_scores_ready")
        s_cmx = sem("c_max_ready")
        s_cmT = sem("c_max_transposed")
        s_cm = sem("c_max_rows_ready")
        s_cT = sem("c_scoresT_ready")
        s_cP = sem("c_probs_ready")
        s_cPu = sem("c_probs_multiplied")
        s_cPa = sem("c_probs_added")
        s_cD = sem("c_den_ready")
        s_cr = sem("c_den_inverted")
        s_cyn = sem("c_y_normalised")
        s_cz = sem("c_z_ready")
        s_turn = [sem(f"c_turn_over{r}") for r in range(2)]
        s_dz = sem("d_rows_zeroed")
        s_dl = sem("d_weights_loaded")
        s_dcast = sem("d_weights_cast")
        s_dxn = sem("d_xn_ready")
        s_dtp = sem("d_xn_transposed")
        s_dxT = sem("d_xT_ready")
        s_dsc = sem("d_logits_ready")
        s_dth = sem("d_logit_tanh_ready")
        s_doh = sem("d_onehot_ready")
        s_dpre = sem("d_prefix_ready")
        s_dslot = sem("d_slots_ready")
        s_dscat = [sem(f"d_rows_scattered{n}") for n in range(RBUF)]
        s_dxnf = sem("d_xn_free")
        s_dsh = sem("d_shared_hidden_ready")
        s_dst = sem("d_shared_tanh_ready")
        s_dsg = sem("d_shared_gated_ready")
        s_dsy = sem("d_shared_y_ready")
        s_dsa = sem("d_shared_y_added")
        s_dxe = [sem(f"d_expert_rows_loaded{q}") for q in range(EBUF)]
        s_dw = [sem(f"d_expert_weights_loaded{q}") for q in range(EBUF)]
        s_dec = sem("d_expert_weights_cast")
        s_det = sem("d_expert_rows_transposed")
        s_deT = sem("d_expert_rowsT_ready")
        s_deh = sem("d_expert_hidden_ready")
        s_deth = sem("d_expert_tanh_ready")
        s_deg = sem("d_expert_hidden_lo_ready")
        s_dey = sem("d_expert_y_ready")
        s_dye = sem("d_expert_y_taken")
        s_dyst = [sem(f"d_expert_y_stored{j}") for j in range(2)]
        s_dgat = [sem(f"d_rows_gathered{q}") for q in range(G)]
        s_dgatf = sem("d_gather_buffer_free")
        s_x4 = sem("x4_ready")
        s_dec2 = sem("d_expert_w2_cast")
        s_deL = sem("d_expert_rows_lo_ready")
        s_dep = sem("d_expert_gated_ready")
        s_dehh = sem("d_expert_hidden_hi_ready")
        block = ctx.enter_context(nc.Block())

        def tile_of(t, n):
            return X[:, bass.ds(t + n, 1), :].rearrange("p a d -> p (a d)")

        RSQRT_STEPS = 11

        def rsqrt(dve, st, var, rstd, tmp):
            st.done(dve.tensor_scalar(tmp[:, :].bitcast(I32), var[:, :].bitcast(I32), 1, None, ALU.logical_shift_right))
            st.sync()
            st.done(dve.tensor_scalar(rstd[:, :].bitcast(I32), tmp[:, :].bitcast(I32), -1.0, float(0x5F3759DF),
                                      ALU.mult, ALU.add))
            for _ in range(3):
                st.sync()
                st.done(dve.tensor_tensor(tmp[:, :], rstd[:, :], rstd[:, :], ALU.mult))
                st.sync()
                st.done(dve.scalar_tensor_tensor(tmp[:, :], tmp[:, :], -0.5, var[:, :], ALU.mult, ALU.mult))
                st.sync()
                st.done(dve.scalar_tensor_tensor(rstd[:, :], tmp[:, :], 1.5, rstd[:, :], ALU.add, ALU.mult))
            st.sync()

        def collect_moments(dve, st, t, n, stat, mv):
            st.sync()
            dve.memset(rtmp[:, :], 0.0)
            for q in range(n):
                st.done(dve.bn_aggr(mv[:, q, :], stat[:, q, :]))
            st.sync()
            st.done(dve.tensor_copy(means[:, bass.ds(t, n)], mv[:, 0:n, 0]))
            st.done(dve.tensor_copy(variances[:, bass.ds(t, n)], mv[:, 0:n, 1]))
            st.sync()

        def all_rstds(dve, st, t=0, n=NT):
            v = variances[:, t:t + n]
            st.done(dve.tensor_scalar(v, v, 1.0, EPS, ALU.mult, ALU.add))
            st.sync()
            rsqrt(dve, st, v, rstds[:, t:t + n], rstds_tmp[:, t:t + n])

        def apply_norm(dve, t, rows, xn_ready):
            for q in range(G):
                dve.tensor_scalar(rows[:, q, :], tile_of(t, q), means[:, bass.ds(t + q, 1)], rstds[:, bass.ds(t + q, 1)],
                                  ALU.subtract, ALU.mult).then_inc(xn_ready, 1)

        def transpose_group(pe, bank, rows=xn):
            for k in range(KD):
                for q in range(G):
                    ins = pe.transpose(PS[:, bank + k, q * P:(q + 1) * P], rows[:, q, k * P:(k + 1) * P], ident[:, :])
            return ins

        def finish_stage(eng, n):
            eng.drain().then_inc(stage_end, 1)
            eng.wait_ge(stage_end, 5 * n)

        def turns(r, heads, pairs, vs, xts):
            chunks = len(CHUNKS) // 2 + (1 if r == 0 else 0)
            return heads * chunks + pairs * (QT // 4) + vs * QT + xts * (S // GT)

        GP = 2 * S // GT
        E0P = E0 // 4

        @block.sync
        def _(sp):
            for c in range(NG):
                sp.dma_start(X[:, c * G:(c + 1) * G, :], x_tiles[:, c * G:(c + 1) * G, :]).then_inc(s_x[c], 16)
                if c == GP - 1:
                    for k, w in enumerate((Wf, Wi, Wz, Wo)):
                        sp.dma_start(a_wraw[:, k, :], w).then_inc(s_aw, 16)
                    sp.dma_start(a_wpraw[:, :, :], Wp.rearrange("(k p) n -> p k n", p=P)).then_inc(s_aw, 16)
                    for k, b in enumerate((bf, bi, bz, bo)):
                        for h in range(2):
                            sp.dma_start(a_bias[h * N:(h + 1) * N, k:k + 1], b.rearrange("(n a) -> n a", a=1)).then_inc(s_aw, 16)
                    sp.dma_start(a_bp[:, :], bp.rearrange("(a d) -> a d", a=1).broadcast_to([P, D])).then_inc(s_aw, 16)
                    for k in range(KD):
                        sp.dma_start(a_lnw[:, k:k + 1], ln_w[k * P:(k + 1) * P].rearrange("(p a) -> p a", a=1)).then_inc(s_aw, 16)
                        sp.dma_start(a_lnb[:, k:k + 1], ln_b[k * P:(k + 1) * P].rearrange("(p a) -> p a", a=1)).then_inc(s_aw, 16)
            with sp.Fori(0, E0) as e:
                sp.wait_ge(s_brawf, e + 1)
                sp.dma_start(b_raw[:, :, :], w12[bass.ds(e, 1), :, :].rearrange("e (a p) d -> p (e a) d", p=P)).then_inc(s_braw, 16)
                sp.wait_ge(s_braw3f, e + 1)
                sp.dma_start(b_raw3[:, :, :], w3[bass.ds(e, 1), :, :].rearrange("e (a p) h -> p (e a) h", p=P)).then_inc(s_braw3, 16)
            finish_stage(sp, 1)
            sp.dma_start(b_gw[:, :], gate0).then_inc(s_bw, 16)
            sp.wait_ge(s_const, 1)
            with sp.Fori(0, E1 * C1 // P) as r:
                sp.dma_start(routed1[bass.ds(r * P, P), :], zeros[:, :]).then_inc(s_dz, 16)
            sp.wait_ge(s_bplan, 1)
            sp.sem_inc(s_pass, 1)
            for e in range(E0):
                row = sp.value_load(b_zrowi[0:1, e:e + 1], min_val=0, max_val=E0 * REGION - P)
                sp.dma_start(routed0[bass.ds(row, P), :], zeros[:, :]).then_inc(s_bzero, 16)
            sp.wait_ge(s_bplan, 2)
            sp.wait_ge(s_bzero, 16 * E0)
            for n in range(RBUF):
                sp.wait_ge(s_bscat[n], 16 * NT * K0 // RBUF)
            with sp.Fori(0, TILES0 // 2) as i:
                for j in range(2):
                    row = sp.value_load(b_rowi[0:1, bass.ds(i * 2 + j, 1)], min_val=0, max_val=E0 * REGION - P)
                    sp.wait_ge(s_btt, i * 2 + (j + 1))
                    sp.dma_start(b_xt[:, j, :], routed0[bass.ds(row, P), :]).then_inc(s_bin[j], 16)
            finish_stage(sp, 2)
            def stage_weights(head, h):
                for n in range(2):
                    sp.dma_start(c_st[h][n][:, :, :].bitcast(F32), c_wqk[n][:, :, bass.ds(head, 1), :].rearrange("p k a c -> p k (a c)").bitcast(F32)).then_inc(s_cw[h], 16)

            def stage_v(head, h):
                sp.dma_start(c_vh[h][:, :, :], c_v[:, :, bass.ds(head * DQ, DQ)]).then_inc(s_cvh[h], 16)

            def head_operands(b, hp, h, nxt):
                H = b * NH + hp * 2 + h
                final = isinstance(hp, int) and hp == NPAIR - 1
                if not (final and h == 1):
                    sp.wait_ge(s_cPu, H * len(BLOCKS) + PBUF)
                    stage_v(hp * 2 + (h + 1), 1 - h)
                if nxt or not final:
                    sp.wait_ge(s_cqk, H * NC2 + NC2)
                    stage_weights(h if final else hp * 2 + (h + 2), h)

            def batch_operands(b, nxt):
                def pair_operands(hp):
                    for h in range(2):
                        head_operands(b, hp, h, nxt)
                sp.wait_ge(s_cve, b * 2 + 1)
                stage_v(0, 0)
                sp.wait_ge(s_cve, b * 2 + 2)
                sp.sem_inc(s_pass, 1)
                with sp.Fori(0, NPAIR - 1) as hp:
                    pair_operands(hp)
                pair_operands(NPAIR - 1)

            sp.wait_ge(s_cwl, 4 * NPAIR)
            for h in range(2):
                stage_weights(h, h)
            with sp.Fori(0, B - 1) as b:
                batch_operands(b, True)
            batch_operands(B - 1, False)
            for h in range(2):
                sp.wait_ge(s_cw[h], B * NPAIR * 32)
            sp.dma_start(d_raw[:, 0, :], sw1).then_inc(s_dl, 16)
            sp.dma_start(d_raw[:, 1, :], sw3).then_inc(s_dl, 16)
            sp.dma_start(d_raw2[:, :, :], sw2.rearrange("(k p) i -> p k i", p=P)).then_inc(s_dl, 16)
            sp.dma_start(d_gwraw[:, :], gate1).then_inc(s_dl, 16)
            sp.dma_start(d_bias[:, 0, :], bias1.rearrange("(a e) -> a e", a=1).broadcast_to([P, E1])).then_inc(s_dl, 16)
            finish_stage(sp, 3)
            def load_weights(e, q):
                sp.wait_ge(s_dec, e + 1)
                sp.wait_ge(s_dec2, e + 1)
                for n, w in enumerate((W1, W3)):
                    sp.dma_start(d_wb[:, q, n * D:(n + 1) * D].rearrange("p (k i) -> p k i", k=KD),
                                 w[bass.ds(e, 1), :, :].rearrange("e (k p) i -> p (e k) i", p=P)).then_inc(s_dw[q], 16)
                sp.dma_start(d_wb[:, q, 2 * D:3 * D], W2[bass.ds(e, 1), :, :].rearrange("e i d -> i (e d)")).then_inc(s_dw[q], 16)

            def load_rows(e, q):
                sp.wait_ge(s_det, e + 1)
                sp.dma_start(d_xe[:, q, :, :], routed1[bass.ds(e * C1, C1), :].rearrange("(a p) d -> p a d", p=P)).then_inc(s_dxe[q], 16)

            for q in range(EBUF):
                load_weights(q, q)
            for n in range(RBUF):
                sp.wait_ge(s_dscat[n], 16 * NT * K1 // RBUF)
            for q in range(EBUF):
                load_rows(q, q)
            with sp.Fori(0, E1 // EBUF - 1) as i:
                for q in range(EBUF):
                    e = i * EBUF + (q + EBUF)
                    load_rows(e, q)
                    load_weights(e, q)
            with sp.Fori(0, NG) as g:
                sp.wait_ge(s_x4, g * G + G)
                sp.dma_start(out_tiles[:, bass.ds(g * G, G), :], X[:, bass.ds(g * G, G), :]).then_inc(s_out, 16)
            sp.wait_ge(s_out, 16 * NG)

        @block.gpsimd
        def _(pool):
            st = Steps(pool, s_pool)
            st.done(pool.memset(ident[:, :], 0.0))
            st.done(pool.memset(identb[:, :], 0.0))
            st.done(pool.memset(ones[:, :], 1.0))
            st.done(pool.memset(onesb[:, :], 1.0))
            st.done(pool.memset(tri[:, :], 1.0))
            st.done(pool.memset(zeros[:, :], 0.0))
            st.done(pool.iota(iota[:, :], pattern=[[1, P]], base=0, channel_multiplier=0,
                              allow_small_or_imprecise_dtypes=True))
            st.sync()
            for m in (ident, identb):
                st.done(pool.affine_select(out=m[:, :], in_=m[:, :], compare_op=ALU.not_equal, fill=1.0,
                                           base=0, pattern=[[-1, P]], channel_multiplier=1))
            st.done(pool.affine_select(out=tri[:, :], in_=tri[:, :], compare_op=ALU.is_gt, fill=0.0,
                                       base=0, pattern=[[1, P]], channel_multiplier=-1))
            st.sync()
            pool.sem_inc(s_const, 1)
            finish_stage(pool, 1)
            with pool.Fori(0, NG // RBUF) as i:
                for n in range(RBUF):
                    pool.wait_ge(s_bslot, i * RBUF + (n + 1))
                    pool.sem_inc(s_pass, 1)
                    for q in range(G):
                        for k in range(K0):
                            pool.indirect_dma_start(
                                routed0, bass.IndirectOffsetOnAxis(ap=b_slot[n][:, q, k:k + 1], axis=0),
                                b_rows[n][:, q, :], None).then_inc(s_bscat[n], 16)
                    for m in [n - 1] * (n > 0) + [n] * (n == RBUF - 1):
                        pool.wait_ge(s_bscat[m], i * (16 * G * K0) + 16 * G * K0)
                        pool.sem_inc(s_bxnf, 1)
            pool.wait_ge(s_bplan, 2)
            pool.sem_inc(s_pass, 1)
            for e in range(E0):
                st.done(pool.tensor_scalar(b_gtmp[:, :, :], b_idxA[:, :, :], float(e), b_start[:, e:e + 1],
                                           ALU.is_equal, ALU.mult))
                st.sync()
                st.done(pool.tensor_tensor(b_posA[:, :, :], b_posA[:, :, :], b_gtmp[:, :, :], ALU.add))
                st.sync()
            st.done(pool.tensor_copy(b_gix[:, :, :], b_posA[:, :, :]))
            with pool.Fori(0, RAW_STEPS) as i:
                d, v = bass.ds(i * (D // RAW_STEPS), D // RAW_STEPS), bass.ds(i * (DQ // RAW_STEPS), DQ // RAW_STEPS)
                pool.dma_start(c_qkraw[0:DQ, d, :], Q[:, d, :]).then_inc(s_cl, 16)
                pool.dma_start(c_qkraw[DQ:2 * DQ, d, :], K[:, d, :]).then_inc(s_cl, 16)
                pool.dma_start(c_vraw[:, d, :], V[:, d, :]).then_inc(s_cl, 16)
                for k in range(KD):
                    pool.dma_start(c_wraw[k][:, v, :], W[k * P:(k + 1) * P, v, :]).then_inc(s_cl, 16)
                pool.wait_ge(s_cl, i * (16 * (3 + KD)) + 16 * (3 + KD))
                pool.sem_inc(s_pass, 1)
            finish_stage(pool, 2)
            st.done(pool.memset(c_maskq[:, :], 0.0))
            st.done(pool.memset(c_maskk[:, :], 0.0))
            st.done(pool.memset(c_block[:, :, :], -1.0))
            st.sync()
            st.done(pool.affine_select(out=c_maskq[:, :], in_=c_maskq[:, :], compare_op=ALU.is_ge, fill=1.0,
                                       base=0, pattern=[[-1, P]], channel_multiplier=1))
            st.done(pool.affine_select(out=c_maskk[:, :], in_=c_maskk[:, :], compare_op=ALU.is_ge, fill=1.0,
                                       base=0, pattern=[[1, P]], channel_multiplier=-1))
            st.done(pool.affine_select(out=c_block[:, :, :], in_=c_block[:, :, :], compare_op=ALU.is_equal, fill=0.0,
                                       base=0, pattern=[[-1, QT], [0, P]], channel_multiplier=1))
            st.sync()
            pool.sem_inc(s_cset, 1)
            with pool.Fori(0, NG) as g:
                st.loop(g, NG, G)
                for q in range(G):
                    pool.wait_ge(s_bgatf, g * G + (q + 1))
                    pool.sem_inc(s_pass, 1)
                    st.done(pool.tensor_copy(b_gi[:, q, :], b_gix[:, bass.ds(g * G + q, 1), :].rearrange("p a k -> p (a k)")))
                    st.sync()
                    pool.sem_inc(s_pass, 1)
                    for k in range(K0):
                        pool.indirect_dma_start(
                            b_gat[:, q, k, :], None, expert0,
                            bass.IndirectOffsetOnAxis(ap=b_gi[:, q, k:k + 1], axis=0)).then_inc(s_bgat[q], 16)
                st.end()

            def copy_k(H, h):
                pool.wait_ge(s_cqs, H * 6 + 6)
                pool.sem_inc(s_pass, 1)
                pool.tensor_copy(c_k2[h][0:DQ, :], c_k1[h][0:DQ, :].bitcast(F32)).then_inc(s_ck2, 1)

            def head_adds(b, hp, h, nxt):
                H = b * NH + hp * 2 + h
                final = isinstance(hp, int) and hp == NPAIR - 1
                for m, (c, j) in enumerate(BLOCKS):
                    off = max(0, j * P - c * 512)
                    pool.wait_ge(s_cP, H * len(BLOCKS) + (m + 3))
                    done, p = H * len(BLOCKS) + (m + PBUF), c_p[:, m % PBUF, 0:512 - off]
                    if j == 0:
                        pool.wait_ge(s_cD, H * NC2 + (c + 1))
                        pool.sem_inc(s_pass, 1)
                        if c == 0:
                            pool.tensor_copy(c_den[c][:, :], p).then_inc(s_cPa, 1)
                    elif j == 1 and c > 0:
                        pool.sem_inc(s_pass, 1)
                        pool.tensor_tensor(c_den[c][:, :], c_p[:, (m - 1) % PBUF, :], p, ALU.add).then_inc(s_cPa, 2)
                    else:
                        pool.wait_ge(s_cPa, done)
                        pool.sem_inc(s_pass, 1)
                        pool.tensor_tensor(c_den[c][:, off:], c_den[c][:, off:], p, ALU.add).then_inc(s_cPa, 1)
                    if m == 4 and (nxt or not (final and h == 1)):
                        copy_k(H + 1, 1 - h)

            def batch_adds(b, nxt):
                def pair_adds(hp):
                    for h in range(2):
                        head_adds(b, hp, h, nxt)
                pair_adds(0)
                with pool.Fori(0, NPAIR // 2 - 1) as i:
                    for n in range(2):
                        pair_adds(i * 2 + (n + 1))
                pair_adds(NPAIR - 1)

            pool.wait_ge(s_cset, 3)
            copy_k(0, 0)
            with pool.Fori(0, B - 1) as b:
                batch_adds(b, True)
            batch_adds(B - 1, False)
            pool.wait_ge(s_dl, 16 * 5)
            pool.tensor_copy(d_gwf[:, :], d_gwraw[:, :]).then_inc(s_dcast, 1)
            pool.tensor_copy(d_rawf[:, :, :], d_raw[:, :, :]).then_inc(s_dcast, 1)
            pool.tensor_copy(d_raw2f[:, :, :], d_raw2[:, :, :]).then_inc(s_dcast, 1)
            finish_stage(pool, 3)
            pool.wait_ge(s_dz, 16 * (E1 * C1 // P))
            with pool.Fori(0, NG // RBUF) as i:
                for n in range(RBUF):
                    pool.wait_ge(s_dslot, i * RBUF + (n + 1))
                    pool.sem_inc(s_pass, 1)
                    for q in range(G):
                        for k in range(K1):
                            pool.indirect_dma_start(
                                routed1, bass.IndirectOffsetOnAxis(ap=d_slot[n][:, q, k:k + 1], axis=0),
                                d_rows[n][:, q, :], None, bounds_check=E1 * C1 - 1, oob_is_err=False).then_inc(s_dscat[n], 16)
                    for m in [n - 1] * (n > 0) + [n] * (n == RBUF - 1):
                        pool.wait_ge(s_dscat[m], i * (16 * G * K1) + 16 * G * K1)
                        pool.sem_inc(s_dxnf, 1)
            with pool.Fori(0, E1 // EBUF) as i:
                for q in range(EBUF):
                    pool.wait_ge(s_dw[q], i * 48 + 48)
                    pool.wait_ge(s_deh, i * EBUF + (q + 1))
                    pool.sem_inc(s_pass, 1)
                    pool.tensor_copy(d_wf[:, q, 0:2 * D], d_wb[:, q, 0:2 * D]).then_inc(s_dec, 1)
            for j in range(2):
                pool.wait_ge(s_dyst[j], 16 * (E1 // 2) + 16)
            with pool.Fori(0, NG) as g:
                st.loop(g, NG, G)
                for q in range(G):
                    pool.wait_ge(s_dgatf, g * G + (q + 1))
                    pool.sem_inc(s_pass, 1)
                    st.done(pool.tensor_copy(d_gi[:, q, :], d_gix[:, bass.ds(g * G + q, 1), :].rearrange("p a k -> p (a k)")))
                    st.sync()
                    pool.sem_inc(s_pass, 1)
                    for k in range(K1):
                        pool.indirect_dma_start(
                            d_gat[:, q, k, :], None, expert1,
                            bass.IndirectOffsetOnAxis(ap=d_gi[:, q, k:k + 1], axis=0)).then_inc(s_dgat[q], 16)
                st.end()

        def take_experts(act, e0):
            with act.Fori(0, E0P) as f:
                for k in range(KD):
                    act.wait_ge(s_btw, (e0 + f) * 3 + (1 + k))
                    act.activation(b_w12T[:, k, bass.ds((e0 + f) * (2 * H0), 2 * H0)],
                                   PS[:, 2 * k:2 * k + 2, :].rearrange("p a n -> p (a n)"), ACT.Copy).then_inc(s_bwe, 1)
                act.wait_ge(s_btw, (e0 + f) * 3 + 3)
                for k in range(KH):
                    act.activation(b_w3T[:, k, bass.ds((e0 + f) * D, D)], PS[:, 4 + k // 2, (k % 2) * D:(k % 2 + 1) * D],
                                   ACT.Copy).then_inc(s_bwe, 1)

        @block.scalar
        def _(act):
            st = Steps(act, s_act)
            act.wait_ge(s_wt, 1)
            st.done(act.activation(a_wT[:, :, :, :].rearrange("p k g n -> p (k g n)"), PS[:, 0, 0:KD * 4 * N], ACT.Copy))
            for h in range(2):
                st.done(act.activation(a_wpT[h][h * N:(h + 1) * N, :], PS[0:N, 1, 0:D], ACT.Copy, scale=0.5))
            act.wait_ge(s_aw, 16 * 18)
            st.done(act.activation(a_hbo[:, :], a_bias[:, 3:4], ACT.Copy, scale=0.5))
            st.sync()
            act.sem_inc(s_we, 1)
            act.sem_inc(s_afree, 1)
            with act.Fori(0, B // 2) as p:
                for g in range(GP):
                    act.wait_ge(s_atp, p * GP + (g + 1))
                    for k in range(KD):
                        act.activation(a_xT[:, k, g * GT:(g + 1) * GT], PS[:, 6 - 2 * (g % 2) + k, :], ACT.Identity,
                                       bias=a_lnb[:, k:k + 1], scale=a_lnw[:, k:k + 1]).then_inc(s_axT, 1)
                take_experts(act, p * (2 * E0P))
                act.wait_ge(s_afree, p + 1)
                for g in range(4):
                    act.wait_ge(s_agate, p * 4 + (g + 1))
                    dst = (a_lf, a_li, a_z, a_o)[g]
                    fn = (ACT.Identity, ACT.Identity, ACT.Tanh, ACT.Tanh)[g]
                    src = PS[:, 2 * (g % 2):2 * (g % 2) + 2, :].rearrange("p a n -> p (a n)")
                    act.activation(dst[:, :], src, fn, bias=a_hbo[:, 0:1] if g == 3 else a_bias[:, g:g + 1],
                                   scale=0.5 if g == 3 else 1.0).then_inc(s_agev, 1)
                act.wait_ge(s_ascan, p * 3 + 1)
                act.activation(a_fs[:, :], a_fs[:, :], ACT.Exp).then_inc(s_aexp, 1)
                act.wait_ge(s_ascan, p * 3 + 2)
                act.activation(a_is[:, :], a_is[:, :], ACT.Exp).then_inc(s_aexp, 1)
                take_experts(act, p * (2 * E0P) + E0P)
                act.wait_ge(s_ascan, p * 3 + 3)
                act.activation(a_c[:, :], a_c[:, :], ACT.Tanh).then_inc(s_aexp, 1)
            finish_stage(act, 1)
            act.wait_ge(s_wt, 2)
            act.activation(b_gwT[:, :, :].rearrange("p k e -> p (k e)"), PS[:, 6, 0:KD * E0], ACT.Copy).then_inc(s_we, 1)
            def take_xT(g, j):
                act.wait_ge(s_btp, g + 1)
                act.activation(b_xT[j][:, :, :].rearrange("p k t -> p (k t)"),
                               PS[:, 6:8, :].rearrange("p a n -> p (a n)"), ACT.Copy).then_inc(s_bxT, 1)

            def router_exps(g, n, ahead):
                act.wait_ge(s_bgap, g + 1)
                act.activation(b_ex[:, :], b_gap[:, :], ACT.Exp).then_inc(s_bex, 1)
                if ahead:
                    take_xT(g + 2, n % 2)

            for g in range(2):
                take_xT(g, g)
            with act.Fori(0, NG // RBUF - 1) as i:
                for n in range(RBUF):
                    router_exps(i * RBUF + n, n, True)
            for n in range(RBUF):
                router_exps(NG - RBUF + n, n, n < RBUF - 2)
            for j in range(2):
                act.sem_inc(s_bst[j], 16)

            def take_rows(n, j):
                act.wait_ge(s_btt, n + 3)
                act.activation(b_tT[:, j, :, :].rearrange("p k t -> p (k t)"), PS[:, 4, 0:D], ACT.Copy).then_inc(s_btT, 1)

            def tanh_half(n, j):
                act.wait_ge(s_bh1, n + 1)
                act.activation(b_sg[:, j, :], PS[:, 2 * j, :], ACT.Tanh, scale=0.5).then_inc(s_bsg, 1)

            def take_hidden(n, j):
                act.wait_ge(s_bht, n + 1)
                act.activation(b_hT[:, j, :, :].rearrange("p k t -> p (k t)"), PS[:, 5, :], ACT.Copy).then_inc(s_bhT, 1)

            def store_y(n, half, j):
                act.wait_ge(s_by, n + 1)
                act.wait_ge(s_bst[j], half * 16 + 16)
                act.activation(b_y[:, j, :], PS[:, 6 + j, 0:D], ACT.Copy).then_inc(s_bye, 1)
                act.wait_ge(s_bye, n + 3)
                act.dma_start(expert0[bass.ds(n * P, P), :], b_y[:, j, :]).then_inc(s_bst[j], 16)

            take_rows(0, 0)
            tanh_half(0, 0)
            take_rows(1, 1)
            with act.Fori(0, TILES0 // 2 - 1) as i:
                for j in (1, 0):
                    n, half = i * 2 + (2 - j), i + (1 - j)
                    tanh_half(n, j)
                    take_hidden(n - 1, 1 - j)
                    take_rows(n + 1, 1 - j)
                    store_y(n - 1, i, 1 - j)
            last = TILES0 - 1
            tanh_half(last, 1)
            take_hidden(last - 1, 0)
            store_y(last - 1, TILES0 // 2 - 1, 0)
            take_hidden(last, 1)
            store_y(last, TILES0 // 2 - 1, 1)
            for j in range(2):
                act.wait_ge(s_bst[j], 16 * (TILES0 // 2) + 16)
            finish_stage(act, 2)
            act.wait_ge(s_cl, 16 * (3 + KD) * RAW_STEPS)
            with act.Fori(0, NPAIR) as hp:
                for h in range(2):
                    head = bass.ds(hp * 2 + h, 1)
                    act.activation(c_qkst[h][:, :], c_qkraw[:, :, head].rearrange("p d a -> p (d a)"), ACT.Copy).then_inc(s_cst, 1)
                    act.activation(c_vst[h][:, :], c_vraw[:, :, head].rearrange("p d a -> p (d a)"), ACT.Copy).then_inc(s_cst, 1)
                for k in range(KD):
                    act.activation(c_wst[:, k, :, :], c_wraw[k][:, :, bass.ds(hp * 2, 2)].rearrange("p v h -> p h v"), ACT.Copy).then_inc(s_cst, 1)
                for h in range(2):
                    head = hp * 2 + h
                    act.wait_ge(s_cwt, hp * 5 + (2 * h + 1))
                    act.activation(c_wqk[0][:, :, bass.ds(head, 1), :].rearrange("p k a c -> p k (a c)"),
                                   PS[:, 2 * h, 0:KD * P].rearrange("p (k c) -> p k c", k=KD), ACT.Copy).then_inc(s_cwh, 1)
                    act.wait_ge(s_cwt, hp * 5 + (2 * h + 2))
                    act.activation(c_wv[0][:, :, bass.ds(head * DQ, DQ)],
                                   PS[:, 2 * h + 1, 0:KD * DQ].rearrange("p (k c) -> p k c", k=KD), ACT.Copy).then_inc(s_cwh, 1)
                act.wait_ge(s_cwt, hp * 5 + 5)
                act.activation(c_wo[:, bass.ds(hp, 1), :].rearrange("p a d -> p (a d)"), PS[:, 4, 0:D], ACT.Copy).then_inc(s_cwh, 1)
            for m in c_q2 + c_k2:
                st.done(act.activation(m[DQ:P, :], zeros[DQ:P, 0:1].broadcast_to([P - DQ, S]), ACT.Copy))
            st.sync()
            act.wait_ge(s_cset, 1)
            act.sem_inc(s_cset, 1)

            def take_xT(batch, g):
                for k in range(KD):
                    act.wait_ge(s_ctp, batch * (KD * S // GT) + (g * KD + k + 1))
                    act.activation(c_xT[0][:, k, g * GT:(g + 1) * GT], PS[:, 2 + k, :], ACT.Copy).then_inc(s_cxh, 1)

            def take_v(batch, a, heads, pairs):
                for t in range(QT):
                    act.wait_ge(s_cv, batch * (2 * QT) + (a * QT + t + 1))
                    act.activation(c_v[:, t, a * 512:(a + 1) * 512], PS[:, 2 + t % 2, :], ACT.Copy).then_inc(s_turn[t % 2], 1)
                for r in range(2):
                    act.wait_ge(s_turn[r], turns(r, heads=heads, pairs=pairs, vs=batch, xts=batch + 1) + ((a + 1) * (QT // 2) + 1))
                act.sem_inc(s_cve, 1)

            def split_hi(H, h, c, part):
                cols = slice(c * 512, (c + 1) * 512)
                act.wait_ge(s_cqk, H * NC2 + (c + 1))
                dst, src = ((c_q1[h][DQ:P, cols], PS[0:DQ, c, :]), (c_q1[h][0:DQ, cols], PS[0:DQ, c, :]),
                            (c_k1[h][0:DQ, cols], PS[DQ:P, c, :]))[part]
                act.activation(dst, src, ACT.Copy).then_inc(s_cqs, 1)

            def head_exps(b, hp, h, nxt):
                H = b * NH + hp * 2 + h
                final = isinstance(hp, int) and hp == NPAIR - 1
                for m, (c, j) in enumerate(BLOCKS):
                    off = max(0, j * P - c * 512)
                    skip = P if off == 512 - P else 0
                    act.wait_ge(s_cT, H * len(BLOCKS) + (m + 1))
                    act.wait_ge(s_cPu, H * len(BLOCKS) + (m + 1))
                    act.wait_ge(s_cPa, H * len(BLOCKS) + (m + 1))
                    act.activation(c_p[:, m % PBUF, 0:512 - off], PS[:, 4 + m % 2, skip:skip + 512 - off], ACT.Exp,
                                   scale=ATT_SCALE).then_inc(s_cP, 1)
                    if m == 0 and (nxt or not (final and h == 1)):
                        split_hi(H + 1, 1 - h, 1, 2)
                    if m in (6, 7, 8, 10, 11) and (nxt or not final):
                        c = 0 if m <= 8 else 1
                        act.wait_ge(s_cT, H * len(BLOCKS) + (len(BLOCKS) if c else 8))
                        split_hi(H + 2, h, c, m - (10 if c else 6))
                    if nxt and final and h == 0 and m in (1, 2):
                        if m == 1:
                            act.wait_ge(s_cqk, (b * NH + NH) * NC2)
                        take_xT(b + 1, m - 1)

            def batch_exps(b, nxt):
                def pair_exps(hp):
                    for h in range(2):
                        head_exps(b, hp, h, nxt)
                pair_exps(0)
                with act.Fori(0, NPAIR // 2 - 1) as i:
                    for n in range(2):
                        pair_exps(i * 2 + (n + 1))
                pair_exps(NPAIR - 1)
                if nxt:
                    for a in range(2):
                        take_v(b + 1, a, b * NH + (NH + 1), b * NPAIR + (NPAIR - 1 + a))

            for g in range(S // GT):
                take_xT(0, g)
            for a in range(2):
                take_v(0, a, 0, 0)
            for n in range(6):
                split_hi(0, 0, n // 3, n % 3)
            for n in range(5):
                split_hi(1, 1, n // 3, n % 3)
            with act.Fori(0, B - 1) as b:
                batch_exps(b, True)
            batch_exps(B - 1, False)
            act.wait_ge(s_wt, 3)
            st.done(act.activation(d_gwT[:, :, :].rearrange("p k e -> p (k e)"), PS[:, 0, 0:KD * E1], ACT.Copy))
            st.done(act.activation(d_s1T[:, :, :, :].rearrange("p k a i -> p (k a i)"), PS[:, 1, 0:KD * 2 * I1], ACT.Copy))
            st.done(act.activation(d_s2T[:, :], PS[:, 4, 0:D], ACT.Copy))
            st.sync()
            act.sem_inc(s_we, 1)
            finish_stage(act, 3)
            def router_tanhs(g, j):
                act.wait_ge(s_dtp, g + 1)
                act.activation(d_xT[j][:, :, :].rearrange("p k t -> p (k t)"),
                               PS[:, 6:8, :].rearrange("p a n -> p (a n)"), ACT.Copy).then_inc(s_dxT, 1)
                act.wait_ge(s_dsc, g + 1)
                act.activation(d_th[j][:, :, :].rearrange("p g e -> p (g e)"), PS[:, j, 0:G * E1], ACT.Tanh, scale=0.5).then_inc(s_dth, 1)

            def shared_tanhs(g):
                act.wait_ge(s_dsh, g + 1)
                act.activation(d_sth[:, :], PS[:, 3, :], ACT.Tanh, scale=0.5).then_inc(s_dst, 1)

            for g in range(2):
                router_tanhs(g, g)
            with act.Fori(0, NG // 2 - 1) as i:
                for j in range(2):
                    shared_tanhs(i * 2 + j)
                    router_tanhs(i * 2 + (j + 2), j)
            for g in range(NG - 2, NG):
                shared_tanhs(g)

            def take_rows(e, j):
                act.wait_ge(s_det, e + (EBUF + 1))
                act.activation(d_xeT[0][:, j, :, :].rearrange("p k c -> p (k c)"), PS[:, j, :], ACT.Copy).then_inc(s_deT, 1)

            def tanh_half(e, j):
                act.wait_ge(s_deh, e + (EBUF + 1))
                act.activation(d_eth[:, j, :], PS[:, 2 + j, 0:C1], ACT.Tanh, scale=0.5).then_inc(s_deth, 1)

            def take_hidden(e, j):
                act.wait_ge(s_dep, e + 3)
                act.activation(d_ehs[0][:, j, :], d_eh[:, j, :], ACT.Copy).then_inc(s_dehh, 1)

            def store_y(e, half, j):
                act.wait_ge(s_dey, e + (EBUF + 1))
                act.wait_ge(s_dyst[j], half * 16 + 16)
                act.activation(d_y[:, j, :, :].rearrange("p a d -> p (a d)"), PS[:, 4 + j, :], ACT.Copy).then_inc(s_dye, 1)
                act.wait_ge(s_dye, e + 3)
                act.dma_start(expert1[bass.ds(e * C1, C1), :].rearrange("(a p) d -> p a d", p=P), d_y[:, j, :, :]).then_inc(s_dyst[j], 16)

            for j in range(2):
                act.sem_inc(s_dyst[j], 16)
                take_rows(j, j)
            for e in range(2):
                tanh_half(e, e)
                take_rows(e + 2, e)
                take_hidden(e, e)
            with act.Fori(0, E1 // EBUF - 1) as i:
                for r in range(EBUF):
                    e, j = i * EBUF + (r + 2), r % 2
                    tanh_half(e, j)
                    take_rows(e + 2, j)
                    store_y(e - 2, i * (EBUF // 2) + r // 2, j)
                    take_hidden(e, j)
            for e in range(E1 - 2, E1):
                tanh_half(e, e % 2)
                store_y(e - 2, (e - 2) // 2, e % 2)
                take_hidden(e, e % 2)
            for e in range(E1 - 2, E1):
                store_y(e, e // 2, e % 2)

        @block.vector
        def _(dve):
            st = Steps(dve, s_dve)
            st.done(dve.memset(a_m[:, 0:1], 0.0))
            for b in range(2):
                st.done(dve.memset(a_wpT[b][(1 - b) * N:(2 - b) * N, :], 0.0))

            def x_statistics(p, loads):
                for n in range(2 * QT):
                    if n % G == 0 and n // G < len(loads):
                        dve.wait_ge(s_x[loads[n // G]], 16)
                    st.done(dve.bn_stats(a_xstat[:, n, :], tile_of(p * (2 * QT), n)))
                st.sync()
                dve.memset(rtmp[:, :], 0.0)
                for n in range(2 * QT):
                    st.done(dve.bn_aggr(a_xmv[:, n, :], a_xstat[:, n, :]))
                st.sync()
                st.done(dve.tensor_scalar(a_var[:, :], a_xmv[:, :, 1], 1.0 + EPS, EPS * EPS, ALU.mult, ALU.add))
                st.sync()
                rsqrt(dve, st, a_var, a_rstd, a_tmp)

            def batch_pair(p, follows):
                for g in range(GP):
                    if g >= 2:
                        dve.wait_ge(s_atp, p * GP + (g - 1))
                    for q in range(G):
                        n = g * G + q
                        dve.tensor_scalar(a_rows[g % 2][:, q, :], tile_of(p * (2 * QT), n), a_xmv[:, n, 0:1], a_rstd[:, n:n + 1],
                                          ALU.subtract, ALU.mult).then_inc(s_axn, 1)
                dve.wait_ge(s_aw, 16 * 18)
                dve.wait_ge(s_axn, p * (2 * QT) + 2 * QT)
                for n in range(2 * QT):
                    st.done(dve.tensor_tensor(tile_of(p * (2 * QT), n), tile_of(p * (2 * QT), n), a_bp[:, :], ALU.add))
                if follows:
                    for g in range(GP, NG):
                        dve.wait_ge(s_x[g], 16)
                    dve.sem_inc(s_pass, 1)
                    x_statistics(p + 1, ())
                dve.wait_ge(s_agev, p * 4 + 1)
                st.done(dve.tensor_scalar(a_lf[:, :], a_lf[:, :], -20.0, 20.0, ALU.max, ALU.min))
                dve.wait_ge(s_agev, p * 4 + 2)
                st.done(dve.tensor_scalar(a_li[:, :], a_li[:, :], -20.0, 20.0, ALU.max, ALU.min))
                st.sync()
                st.done(dve.tensor_tensor_scan(a_m[:, 1:], a_lf[:, :], a_li[:, :], 0.0, ALU.add, ALU.max))
                st.sync()
                st.done(dve.tensor_tensor(a_fs[:, :], a_m[:, 0:S], a_lf[:, :], ALU.add))
                st.sync()
                st.done(dve.tensor_tensor(a_fs[:, :], a_fs[:, :], a_m[:, 1:], ALU.subtract))
                st.sync()
                dve.sem_inc(s_ascan, 1)
                st.done(dve.tensor_tensor(a_is[:, :], a_li[:, :], a_m[:, 1:], ALU.subtract))
                st.sync()
                dve.sem_inc(s_ascan, 1)
                dve.wait_ge(s_agev, p * 4 + 4)
                dve.wait_ge(s_aexp, p * 3 + 2)
                st.done(dve.tensor_tensor(a_is[:, :], a_is[:, :], a_z[:, :], ALU.mult))
                st.sync()
                st.done(dve.tensor_tensor_scan(a_c[:, :], a_fs[:, :], a_is[:, :], 0.0, ALU.mult, ALU.add))
                st.sync()
                dve.sem_inc(s_ascan, 1)
                dve.wait_ge(s_aexp, p * 3 + 3)
                st.done(dve.scalar_tensor_tensor(a_h[:, :], a_o[:, :], 1.0, a_c[:, :], ALU.add, ALU.mult))
                st.sync()
                dve.sem_inc(s_ah, 1)
                for n in range(2 * QT):
                    dve.wait_ge(s_ay, p * (2 * QT) + (n + 1))
                    dve.tensor_tensor(tile_of(p * (2 * QT), n), PS[:, 4 + n % 2, 0:D], tile_of(p * (2 * QT), n),
                                      ALU.add).then_inc(s_x1, 1)
                    if n:
                        dve.wait_ge(s_x1, p * (2 * QT) + n)
                        dve.sem_inc(s_pass, 1)
                        st.done(dve.bn_stats(a_stat[:, n - 1, :], tile_of(p * (2 * QT), n - 1)))
                dve.wait_ge(s_x1, p * (2 * QT) + 2 * QT)
                dve.sem_inc(s_pass, 1)
                st.done(dve.bn_stats(a_stat[:, 2 * QT - 1, :], tile_of(p * (2 * QT), 2 * QT - 1)))
                collect_moments(dve, st, p * (2 * QT), 2 * QT, a_stat, a_mv)
                dve.sem_inc(s_afree, 1)

            PAIR_STEPS = 2 * QT + 9 + 2 * (2 * QT) + 2
            x_statistics(0, range(GP))
            with dve.Fori(0, B // 2 - 1) as p:
                st.loop(p, B // 2 - 1, PAIR_STEPS + 2 * (2 * QT) + 1 + RSQRT_STEPS)
                batch_pair(p, True)
                st.end()
            batch_pair(B // 2 - 1, False)
            finish_stage(dve, 1)
            st.done(dve.memset(b_sum[:, :], 0.0))
            st.sync()
            all_rstds(dve, st)
            dve.sem_inc(s_bxnf, RBUF)

            def rows_of(g, n):
                dve.wait_ge(s_bxnf, g + 1)
                apply_norm(dve, g * G, b_rows[n], s_bxn)

            def route_group(g, n, ahead):
                dve.wait_ge(s_bsc, g + 1)
                st.done(dve.tensor_copy(b_s8[:, :, :].rearrange("p g e -> p (g e)"), PS[:, 2 * (n % 2), 0:G * E0]))
                st.sync()
                dve.memset(rtmp[:, :], 0.0)
                for q in range(G):
                    st.done(dve.max(b_top[:, q, :], b_s8[:, q, :]))
                st.sync()
                dve.memset(rtmp[:, :], 0.0)
                for q in range(G):
                    st.done(dve.max_index(b_ix[:, q, :], b_top[:, q, :], b_s8[:, q, :]))
                st.done(dve.tensor_tensor(b_gap[:, :], b_top[:, :, 1], b_top[:, :, 0], ALU.subtract))
                st.sync()
                dve.sem_inc(s_bgap, 1)
                idx = b_idx[:, :, 0].rearrange("p (g k) -> p g k", g=G)
                st.done(dve.tensor_copy(idx, b_ix[:, :, 0:K0]))
                st.sync()
                st.done(dve.tensor_copy(b_idxA[:, bass.ds(g * G, G), :], idx))
                st.done(dve.tensor_tensor(b_oh[:, :, :, :].rearrange("p g k e -> p (g k) e"),
                                          iota[:, 0:E0].rearrange("p (a e) -> p a e", a=1).broadcast_to([P, G * K0, E0]),
                                          b_idx[:, :, :].broadcast_to([P, G * K0, E0]), ALU.is_equal))
                st.sync()
                st.done(dve.tensor_tensor(b_ohs[:, :, :], b_oh[:, :, 0, :], b_oh[:, :, 1, :], ALU.add))
                st.sync()
                dve.sem_inc(s_boh, 1)
                st.done(dve.tensor_reduce(b_gsum[:, :], b_ohs[:, :, :].rearrange("p g e -> p e g"), AX_X, ALU.add))
                dve.wait_ge(s_bpre, g + 1)
                pre = PS[:, 1, 0:G * E0].rearrange("p (g e) -> p g e", g=G)
                for k in range(K0):
                    st.done(dve.tensor_tensor(b_tmp[:, :, k, :], b_oh[:, :, k, :], pre, ALU.mult))
                st.sync()
                st.done(dve.tensor_tensor(b_sum[:, :], b_sum[:, :], b_gsum[:, :], ALU.add))
                st.done(dve.tensor_reduce(b_pos[:, :, :].rearrange("p g k -> p (g k)"),
                                          b_tmp[:, :, :, :].rearrange("p g k e -> p (g k) e"), AX_X, ALU.add))
                st.sync()
                st.done(dve.scalar_tensor_tensor(b_slot[n][:, :, :], idx, float(REGION), b_pos[:, :, :], ALU.mult, ALU.add))
                st.sync()
                dve.sem_inc(s_bslot, 1)
                if ahead:
                    rows_of(g + 2, (n + 2) % RBUF)
                st.done(dve.tensor_copy(b_posA[:, bass.ds(g * G, G), :], b_pos[:, :, :]))
                dve.wait_ge(s_bex, g + 1)
                st.done(dve.tensor_scalar(b_den[:, :], b_ex[:, :], 1.0, None, ALU.add))
                st.sync()
                st.done(dve.reciprocal(b_den[:, :], b_den[:, :]))
                st.sync()
                st.done(dve.tensor_copy(b_prA[:, bass.ds(g * G, G), 0], b_den[:, :]))
                st.done(dve.tensor_tensor(b_prA[:, bass.ds(g * G, G), 1], b_den[:, :], b_ex[:, :], ALU.mult))
                st.sync()

            for g in range(2):
                rows_of(g, g)
            with dve.Fori(0, NG // RBUF - 1) as i:
                st.loop(i, NG // RBUF - 1, RBUF * (2 * G + K0 + 15))
                for n in range(RBUF):
                    route_group(i * RBUF + n, n, True)
                st.end()
            for n in range(RBUF):
                route_group(NG - RBUF + n, n, n < RBUF - 2)
            dve.sem_inc(s_boh, 1)
            dve.wait_ge(s_bcnt, 1)
            st.done(dve.tensor_copy(b_cnt[:, :], PS[:, 0, 0:E0]))
            st.sync()
            st.done(dve.tensor_scalar(b_nti[:, :], b_cnt[:, :], float(P - 1), None, ALU.add))
            st.done(dve.scalar_tensor_tensor(b_zrow[:, :], iota[:, 0:E0], float(REGION), b_cnt[:, :], ALU.mult, ALU.add))
            st.sync()
            st.done(dve.tensor_copy(b_zrowi[:, :], b_zrow[:, :]))
            st.sync()
            dve.sem_inc(s_bplan, 1)
            st.done(dve.tensor_scalar(b_nti[:, :], b_nti[:, :], P.bit_length() - 1, None, ALU.logical_shift_right))
            st.sync()
            st.done(dve.tensor_copy(b_nt[:, :], b_nti[:, :]))
            st.sync()
            st.done(dve.tensor_tensor_scan(b_end[:, :], ones[:, 0:E0], b_nt[:, :], 0.0, ALU.mult, ALU.add))
            st.sync()
            st.done(dve.tensor_tensor(b_start[:, :], b_end[:, :], b_nt[:, :], ALU.subtract))
            st.sync()
            st.done(dve.tensor_scalar(b_start[:, :], b_start[:, :], float(P), None, ALU.mult))
            tiles = iota[:, 0:TILES0]
            st.done(dve.memset(b_te[:, :], 0.0))
            st.done(dve.memset(b_ts[:, :], 0.0))
            for e in range(E0 - 1):
                st.sync()
                st.done(dve.tensor_scalar(b_tt[:, :], tiles, b_end[:, e:e + 1], b_end[:, e:e + 1], ALU.is_ge, ALU.mult))
                st.done(dve.scalar_tensor_tensor(b_te[:, :], tiles, b_end[:, e:e + 1], b_te[:, :], ALU.is_ge, ALU.add))
                st.sync()
                st.done(dve.tensor_tensor(b_ts[:, :], b_ts[:, :], b_tt[:, :], ALU.max))
            st.sync()
            st.done(dve.tensor_copy(b_tei[:, :], b_te[:, :]))
            st.done(dve.tensor_tensor(b_tt[:, :], tiles, b_ts[:, :], ALU.subtract))
            st.sync()
            st.done(dve.tensor_scalar(b_tt[:, :], b_tt[:, :], float(P), None, ALU.mult))
            st.sync()
            st.done(dve.scalar_tensor_tensor(b_tt[:, :], b_te[:, :], float(REGION), b_tt[:, :], ALU.mult, ALU.add))
            st.sync()
            st.done(dve.tensor_scalar(b_ts[:, :], tiles, b_end[:, E0 - 1:E0], None, ALU.is_lt))
            st.done(dve.tensor_scalar(b_tt[:, :], b_tt[:, :], b_zrow[:, E0 - 1:E0], None, ALU.subtract))
            st.sync()
            st.done(dve.tensor_tensor(b_tt[:, :], b_tt[:, :], b_ts[:, :], ALU.mult))
            st.sync()
            st.done(dve.tensor_scalar(b_rowi[:, :], b_tt[:, :], b_zrow[:, E0 - 1:E0], None, ALU.add))
            st.sync()
            dve.sem_inc(s_bplan, 1)
            with dve.Fori(0, TILES0 // 2) as i:
                st.loop(i, TILES0 // 2, 2)
                for j in range(2):
                    dve.wait_ge(s_bsg, i * 2 + (j + 1))
                    st.done(dve.scalar_tensor_tensor(b_hid[:, j, :], b_sg[:, j, :], 1.0, PS[:, 2 * j, :], ALU.add, ALU.mult))
                    st.sync()
                    dve.wait_ge(s_bh2, i * 2 + (j + 1))
                    dve.scalar_tensor_tensor(b_hid[:, j, :], b_hid[:, j, :], 0.5, PS[:, 2 * j + 1, :], ALU.mult,
                                             ALU.mult).then_inc(s_bhid, 1)
                st.end()
            finish_stage(dve, 2)
            dve.sem_inc(s_bgatf, G)

            def low_weights(pair):
                for h in range(2):
                    head = pair * 2 + h
                    dve.wait_ge(s_cwh, pair * 5 + (2 * h + 1))
                    ws = [w[:, :, bass.ds(head, 1), :].rearrange("p k a c -> p k (a c)") for w in c_wqk]
                    dve.tensor_tensor(ws[1], PS[:, 2 * h, 0:KD * P].rearrange("p (k c) -> p k c", k=KD), ws[0].bitcast(F32),
                                      ALU.subtract).then_inc(s_cwl, 1)
                    dve.wait_ge(s_cwh, pair * 5 + (2 * h + 2))
                    ws = [w[:, :, bass.ds(head * DQ, DQ)] for w in c_wv]
                    dve.tensor_tensor(ws[1], PS[:, 2 * h + 1, 0:KD * DQ].rearrange("p (k c) -> p k c", k=KD), ws[0].bitcast(F32),
                                      ALU.subtract).then_inc(s_cwl, 1)

            def add_experts(g, q):
                t = tile_of(g * G, q)
                dve.wait_ge(s_bgat[q], g * (16 * K0) + 16 * K0)
                st.done(dve.scalar_tensor_tensor(t, b_gat[:, q, 0, :], b_prA[:, bass.ds(g * G + q, 1), 0], t, ALU.mult, ALU.add))
                st.sync()
                dve.scalar_tensor_tensor(t, b_gat[:, q, 1, :], b_prA[:, bass.ds(g * G + q, 1), 1], t, ALU.mult,
                                         ALU.add).then_inc(s_x2, 1)
                dve.wait_ge(s_x2, g * G + (q + 1))
                dve.sem_inc(s_bgatf, 1)

            def moments(g):
                for q in range(G):
                    st.done(dve.bn_stats(stat[:, q, :], tile_of(g * G, q)))
                collect_moments(dve, st, g * G, G, stat, mv)

            def late_group(g):
                for q in range(G):
                    add_experts(g, q)
                moments(g)

            assert NPAIR == NG and S // GT * 2 == G
            with dve.Fori(0, NG // 2) as g:
                st.loop(g, NG // 2, 3 * G + 2)
                for r in range(2):
                    low_weights(g * 2 + r)
                    for q in range(r * (G // 2), (r + 1) * (G // 2)):
                        add_experts(g, q)
                moments(g)
                st.end()
            all_rstds(dve, st, 0, NT // 2)

            def batch_moments(b):
                for g in range(QT // G):
                    moments(b * (QT // G) + g)

            def make_xn(batch, g):
                if g:
                    dve.wait_ge(s_ctp, batch * (KD * S // GT) + g * KD)
                for q in range(G):
                    t = batch * QT + (g * G + q)
                    dve.tensor_scalar(xn[:, q, :], tile_of(t, 0), means[:, bass.ds(t, 1)], rstds[:, bass.ds(t, 1)],
                                      ALU.subtract, ALU.mult).then_inc(s_cxn, 1)

            def low_xT(batch, g):
                for k in range(KD):
                    dve.wait_ge(s_cxh, batch * (KD * S // GT) + (g * KD + k + 1))
                    dve.tensor_tensor(c_xT[1][:, k, g * GT:(g + 1) * GT], PS[:, 2 + k, :],
                                      c_xT[0][:, k, g * GT:(g + 1) * GT].bitcast(F32), ALU.subtract).then_inc(s_turn[k], 1)

            def split_lo(H, h, c, k):
                cols = slice(c * 512, (c + 1) * 512)
                dst, rows, hi = ((c_q2[h][0:DQ, cols], slice(0, DQ), c_q1[h]), (c_k1[h][DQ:P, cols], slice(DQ, P), c_k1[h]))[k]
                dve.wait_ge(s_cqs, H * 6 + (c * 3 + k + 2))
                dve.tensor_tensor(dst, PS[rows, c, :], hi[0:DQ, cols].bitcast(F32), ALU.subtract).then_inc(s_cks, 1)

            def maximum(H, n):
                t, c = CHUNKS[n]
                w = min(512, (t + 1) * P - c * 512)
                dst = c_max[:, t:t + 1] if t < QT // 2 else c_max2[:, c, t - QT // 2:t - QT // 2 + 1]
                dve.wait_ge(s_cS, H * len(CHUNKS) + (n + 1))
                dve.tensor_reduce(dst, PS[:, 2 + n % 2, 0:w], AX_X, ALU.max).then_inc(s_turn[n % 2], 1)

            def max_rows(H, h, used):
                for r in range(2):
                    dve.wait_ge(s_turn[r], used[r] + 1)
                dve.tensor_tensor(c_max[:, QT // 2:QT], c_max2[:, 0, :], c_max2[:, 1, :], ALU.max).then_inc(s_cmx, 1)
                dve.wait_ge(s_cmT, H + 1)
                dve.tensor_tensor(c_q2[h][DQ:DQ + QT, :].rearrange("p (t q) -> p t q", t=QT),
                                  PS[0:QT, 2:3, 0:P].broadcast_to([QT, QT, P]), c_block[:, :, :], ALU.mult).then_inc(s_turn[0], 1)
                dve.wait_ge(s_turn[0], used[0] + 2)
                dve.sem_inc(s_cm, 1)

            def normalise_y(H, h, c, yT):
                dve.wait_ge(s_cD, H * NC2 + (c + 1 + NC2))
                dve.wait_ge(s_cyn, H * (2 * NC2) + (2 * c + 2 * NC2))
                dve.reciprocal(c_rden[:, :], PS[:, 6 + c, 256:512]).then_inc(s_cr, 1)
                dve.wait_ge(s_cr, H * NC2 + (c + 1))
                for a in range(2):
                    dst = yT[h * DQ:(h + 1) * DQ, c * 512:(c + 1) * 512].rearrange("p (n a q) -> p n a q", n=2, a=2)[:, :, a, :]
                    dve.tensor_tensor(dst, PS[a * DQ:(a + 1) * DQ, 6 + c, 0:256].rearrange("p (n q) -> p n q", n=2),
                                      c_rden[a * DQ:(a + 1) * DQ, :].rearrange("p (n q) -> p n q", n=2), ALU.mult).then_inc(s_cyn, 1)

            def add_z(b, pair):
                for n in range(QT // 2):
                    dve.wait_ge(s_cz, pair * (QT // 2) + (n + 1))
                    x = X[:, bass.ds(b * QT + 2 * n, 2), :].rearrange("p a d -> p (a d)")
                    dve.scalar_tensor_tensor(x, PS[:, 2 + n % 2, :], Z_SCALE, x, ALU.mult, ALU.add).then_inc(s_turn[n % 2], 1)

            def head_steps(b, hp, h, nxt, first, par):
                pair = b * NPAIR + hp
                H = pair * 2 + h
                final = isinstance(hp, int) and hp == NPAIR - 1
                fetch = nxt and final
                follows = nxt or not (final and h == 1)
                zs = h == 0 and not first
                if fetch and h == 0:
                    make_xn(b + 1, 0)
                    split_lo(H + 1, 1 - h, 1, 0)
                    make_xn(b + 1, 1)
                    split_lo(H + 1, 1 - h, 1, 1)
                    for g in range(S // GT):
                        low_xT(b + 1, g)
                    for n in range(4):
                        maximum(H + 1, n)
                elif follows:
                    for k in range(2):
                        for n in range(k * 2, k * 2 + 2):
                            maximum(H + 1, n)
                        split_lo(H + 1, 1 - h, 1, k)
                if h == 1 or not first:
                    normalise_y(H - 1, 1 - h, 1, c_yT[par if h else 1 - par])
                if follows:
                    for n in range(4, 10):
                        maximum(H + 1, n)
                normalise_y(H, h, 0, c_yT[par])
                if follows:
                    for n in range(10, len(CHUNKS)):
                        maximum(H + 1, n)
                    max_rows(H + 1, 1 - h, [turns(r, heads=H + 1, pairs=pair - 1 if zs else pair, vs=b + 1,
                                                  xts=b + (2 if fetch else 1)) + len(CHUNKS) // 2 for r in range(2)])
                if nxt or not final:
                    for k in range(2):
                        split_lo(H + 2, h, 0, k)
                if zs:
                    add_z(b, pair - 1)

            def batch_steps(b, nxt):
                def pair_steps(hp, first, par):
                    for h in range(2):
                        head_steps(b, hp, h, nxt, first, par)
                pair_steps(0, True, 0)
                with dve.Fori(0, NPAIR // 2 - 1) as i:
                    for n in range(2):
                        pair_steps(i * 2 + (n + 1), False, 1 - n)
                pair_steps(NPAIR - 1, False, 1)
                if not nxt:
                    all_rstds(dve, st, 0, NT - QT)
                normalise_y(b * NH + (NH - 1), 1, 1, c_yT[1])
                add_z(b, b * NPAIR + (NPAIR - 1))
                for r in range(2):
                    dve.wait_ge(s_turn[r], turns(r, heads=b * NH + (NH + 1 if nxt else NH), pairs=b * NPAIR + NPAIR,
                                                 vs=b + 1, xts=b + (2 if nxt else 1)) + (QT // 2 + 1 if nxt else 1))
                dve.sem_inc(s_pass, 1)
                if nxt:
                    batch_moments(b)

            for g in range(S // GT):
                make_xn(0, g)
                for q in range(2 * g, 2 * g + 2):
                    add_experts(NG // 2, q)
                low_xT(0, g)
            moments(NG // 2)
            for g in range(NG // 2 + 1, NG - 1):
                late_group(g)
            dve.wait_ge(s_cset, 2)
            for m in (c_maskq, c_maskk):
                st.done(dve.tensor_scalar(m[:, :], m[:, :], BIG, None, ALU.mult))
            for h in range(2):
                st.done(dve.memset(c_k2[h][DQ:DQ + QT, :].bitcast(F32), 1.0))
            st.sync()
            dve.sem_inc(s_cset, 1)
            for q in range(G):
                add_experts(NG - 1, q)
            for n in range(4):
                split_lo(0, 0, n // 2, n % 2)
            for n in range(len(CHUNKS)):
                maximum(0, n)
            max_rows(0, 0, [turns(r, heads=0, pairs=0, vs=1, xts=1) + len(CHUNKS) // 2 for r in range(2)])
            for k in range(2):
                split_lo(1, 1, 0, k)
            moments(NG - 1)
            all_rstds(dve, st, NT // 2, NT // 2)
            with dve.Fori(0, B - 1) as b:
                st.loop(b, B - 1, (QT // G) * (2 * G + 2))
                batch_steps(b, True)
                st.end()
            batch_steps(B - 1, False)
            finish_stage(dve, 3)
            st.done(dve.memset(d_sum[:, :], 0.0))
            st.sync()
            dve.sem_inc(s_dxnf, RBUF)
            dve.wait_ge(s_dl, 16 * 5)

            def rows_of(g, n):
                dve.wait_ge(s_dxnf, g + 1)
                apply_norm(dve, g * G, d_rows[n], s_dxn)

            def route_group(g, n, ahead):
                dve.wait_ge(s_dth, g + 1)
                st.done(dve.tensor_scalar(d_sc[:, :, :], d_th[n % 2][:, :, :], 0.5, 0.5, ALU.mult, ALU.add))
                st.sync()
                st.done(dve.tensor_tensor(d_sel[:, :, :], d_sc[:, :, :], d_bias[:, :, :].broadcast_to([P, G, E1]), ALU.add))
                st.sync()
                dve.memset(rtmp[:, :], 0.0)
                for q in range(G):
                    st.done(dve.max(d_top[:, q, :], d_sel[:, q, :]))
                st.sync()
                dve.memset(rtmp[:, :], 0.0)
                for q in range(G):
                    st.done(dve.max_index(d_ix[:, q, :], d_top[:, q, :], d_sel[:, q, :]))
                st.sync()
                idx = d_idx[:, :, 0].rearrange("p (g k) -> p g k", g=G)
                st.done(dve.tensor_copy(idx, d_ix[:, :, 0:K1]))
                st.sync()
                st.done(dve.tensor_tensor(d_oh[:, :, :, :].rearrange("p g k e -> p (g k) e"),
                                          iota[:, 0:E1].rearrange("p (a e) -> p a e", a=1).broadcast_to([P, G * K1, E1]),
                                          d_idx[:, :, :].broadcast_to([P, G * K1, E1]), ALU.is_equal))
                st.sync()
                st.done(dve.tensor_reduce(d_ohf[:, :, :], d_oh[:, :, :, :].rearrange("p g k e -> p g e k"), AX_X, ALU.add))
                st.sync()
                st.done(dve.tensor_copy(d_ohs[:, :, :], d_ohf[:, :, :]))
                st.sync()
                dve.sem_inc(s_doh, 1)
                st.done(dve.tensor_reduce(d_gsum[:, :], d_ohs[:, :, :].rearrange("p g e -> p e g"), AX_X, ALU.add))
                for k in range(K1):
                    st.done(dve.tensor_tensor(d_tmp2[:, :, k, :], d_oh[:, :, k, :], d_sc[:, :, :], ALU.mult))
                dve.wait_ge(s_dpre, g + 1)
                pre = PS[:, 2, 0:G * E1].rearrange("p (g e) -> p g e", g=G)
                for k in range(K1):
                    st.done(dve.tensor_tensor(d_tmp[:, :, k, :], d_oh[:, :, k, :], pre, ALU.mult))
                st.sync()
                st.done(dve.tensor_tensor(d_sum[:, :], d_sum[:, :], d_gsum[:, :], ALU.add))
                st.done(dve.tensor_reduce(d_pos[:, :, :].rearrange("p g k -> p (g k)"),
                                          d_tmp[:, :, :, :].rearrange("p g k e -> p (g k) e"), AX_X, ALU.add))
                st.sync()
                st.done(dve.tensor_scalar(d_skip[:, :, :], d_pos[:, :, :], float(C1), float(BIGSLOT), ALU.is_ge, ALU.mult))
                st.done(dve.tensor_scalar(d_ok[:, :, :], d_pos[:, :, :], float(C1), None, ALU.is_lt))
                st.done(dve.tensor_scalar(d_cl[:, :, :], d_pos[:, :, :], float(C1 - 1), None, ALU.min))
                st.sync()
                st.done(dve.tensor_tensor(d_skip[:, :, :], d_skip[:, :, :], d_pos[:, :, :], ALU.add))
                st.done(dve.scalar_tensor_tensor(d_gix[:, bass.ds(g * G, G), :], idx, float(C1), d_cl[:, :, :], ALU.mult, ALU.add))
                st.sync()
                st.done(dve.scalar_tensor_tensor(d_slot[n][:, :, :], idx, float(C1), d_skip[:, :, :], ALU.mult, ALU.add))
                st.sync()
                dve.sem_inc(s_dslot, 1)
                if ahead:
                    rows_of(g + 2, (n + 2) % RBUF)
                st.done(dve.tensor_reduce(d_w[:, :, :].rearrange("p g k -> p (g k)"),
                                          d_tmp2[:, :, :, :].rearrange("p g k e -> p (g k) e"), AX_X, ALU.add))
                st.sync()
                st.done(dve.tensor_reduce(d_ws[:, :], d_w[:, :, :], AX_X, ALU.add))
                st.sync()
                st.done(dve.tensor_scalar(d_ws[:, :], d_ws[:, :], 1e-12, None, ALU.max))
                st.sync()
                st.done(dve.reciprocal(d_ws[:, :], d_ws[:, :]))
                st.sync()
                for q in range(G):
                    st.done(dve.tensor_scalar(d_w[:, q, :], d_w[:, q, :], d_ws[:, q:q + 1], None, ALU.mult))
                st.sync()
                st.done(dve.tensor_tensor(d_wA[:, bass.ds(g * G, G), :], d_w[:, :, :], d_ok[:, :, :], ALU.mult))
                dve.wait_ge(s_dst, g + 1)
                st.done(dve.scalar_tensor_tensor(d_sh[:, :], d_sth[:, :], 1.0, PS[:, 3, :], ALU.add, ALU.mult))
                st.sync()
                st.done(dve.scalar_tensor_tensor(d_sh[:, :], d_sh[:, :], 0.5, PS[:, 4, :], ALU.mult, ALU.mult))
                st.sync()
                dve.sem_inc(s_dsg, 1)
                for n in range(G // 2):
                    x = X[:, bass.ds(g * G + 2 * n, 2), :].rearrange("p a d -> p (a d)")
                    dve.wait_ge(s_dsy, g * (G // 2) + (n + 1))
                    dve.tensor_tensor(x, PS[:, 5, :], x, ALU.add).then_inc(s_dsa, 1)

            for g in range(2):
                rows_of(g, g)
            for g in range(NG - QT // G, NG):
                for q in range(G):
                    st.done(dve.bn_stats(stat[:, q, :], tile_of(g * G, q)))
                collect_moments(dve, st, g * G, G, stat, mv)
            all_rstds(dve, st, NT - QT, QT)
            with dve.Fori(0, NG // RBUF - 1) as i:
                st.loop(i, NG // RBUF - 1, RBUF * (3 * G + 2 * K1 + 22))
                for n in range(RBUF):
                    route_group(i * RBUF + n, n, True)
                st.end()
            for n in range(RBUF):
                route_group(NG - RBUF + n, n, n < RBUF - 2)
            def low_rows(e, j):
                dve.wait_ge(s_deT, e + 1)
                dve.tensor_tensor(d_xeT[1][:, j, :, :].rearrange("p k c -> p (k c)"), PS[:, j, :],
                                  d_xeT[0][:, j, :, :].rearrange("p k c -> p (k c)").bitcast(F32), ALU.subtract).then_inc(s_deL, 1)

            def gate_hidden(e, q, quarter, ahead):
                j = q % 2
                dve.wait_ge(s_deth, e + 1)
                dve.wait_ge(s_deg, e + 1)
                st.done(dve.scalar_tensor_tensor(d_eh[:, j, :], d_eth[:, j, :], 1.0, PS[:, 2 + j, 0:C1], ALU.add, ALU.mult))
                st.sync()
                dve.scalar_tensor_tensor(d_eh[:, j, :], d_eh[:, j, :], 0.5, PS[:, 2 + j, C1:2 * C1], ALU.mult, ALU.mult).then_inc(s_dep, 1)
                if ahead:
                    low_rows(e + 2, j)
                dve.wait_ge(s_dw[q], quarter * 48 + 48)
                dve.wait_ge(s_dey, e + 1)
                dve.tensor_copy(d_wf[:, q, 2 * D:3 * D], d_wb[:, q, 2 * D:3 * D]).then_inc(s_dec2, 1)

            def low_hidden(e, j):
                dve.wait_ge(s_dehh, e + 1)
                dve.tensor_tensor(d_ehs[1][:, j, :], d_eh[:, j, :], d_ehs[0][:, j, :].bitcast(F32), ALU.subtract).then_inc(s_deg, 1)

            for j in range(2):
                low_rows(j, j)
            gate_hidden(0, 0, 0, True)
            with dve.Fori(0, E1 // EBUF - 1) as i:
                st.loop(i, E1 // EBUF - 1, EBUF)
                for r in range(EBUF):
                    e = i * EBUF + (r + 1)
                    gate_hidden(e, (r + 1) % EBUF, i + (r + 1) // EBUF, True)
                    low_hidden(e - 1, r % 2)
                st.end()
            for q in range(1, EBUF):
                e = E1 - EBUF + q
                gate_hidden(e, q, E1 // EBUF - 1, q < EBUF - 2)
                low_hidden(e - 1, (q - 1) % 2)
            low_hidden(E1 - 1, 1)
            dve.sem_inc(s_dgatf, G)
            dve.wait_ge(s_dsa, NT // 2 + 1)
            with dve.Fori(0, NG) as g:
                st.loop(g, NG, G * (K1 - 1))
                for q in range(G):
                    t = tile_of(g * G, q)
                    dve.wait_ge(s_dgat[q], g * (16 * K1) + 16 * K1)
                    for k in range(K1):
                        ins = dve.scalar_tensor_tensor(t, d_gat[:, q, k, :], d_wA[:, bass.ds(g * G + q, 1), k], t, ALU.mult, ALU.add)
                        if k < K1 - 1:
                            st.done(ins)
                            st.sync()
                    ins.then_inc(s_x4, 1)
                    dve.wait_ge(s_x4, g * G + (q + 1))
                    dve.sem_inc(s_dgatf, 1)
                st.end()

        def transpose_experts(pe, e0, gates=None):
            with pe.Fori(0, E0P) as f:
                if gates is not None:
                    pe.wait_ge(s_agev, gates)
                pe.wait_ge(s_braw, (e0 + f) * 16 + 16)
                for k in range(KD):
                    for a in range(HT):
                        ins = pe.transpose(PS[:, 2 * k + a // 4, (a % 4) * P:(a % 4 + 1) * P], b_raw[:, a, k * P:(k + 1) * P], ident[:, :])
                    ins.then_inc(s_btw, 1)
                pe.wait_ge(s_btw, (e0 + f) * 3 + 2)
                pe.sem_inc(s_brawf, 1)
                pe.wait_ge(s_braw3, (e0 + f) * 16 + 16)
                for k in range(KH):
                    for a in range(KD):
                        c = (k % 2) * D + a * P
                        ins = pe.transpose(PS[:, 4 + k // 2, c:c + P], b_raw3[:, a, k * P:(k + 1) * P], ident[:, :])
                ins.then_inc(s_btw, 1)
                pe.wait_ge(s_btw, (e0 + f) * 3 + 3)
                pe.sem_inc(s_braw3f, 1)
                pe.wait_ge(s_bwe, (e0 + f) * (KD + KH) + KD + KH)

        @block.tensor
        def _(pe):
            pe.wait_ge(s_const, 1)
            pe.sem_inc(s_brawf, 1)
            pe.sem_inc(s_braw3f, 1)
            pe.wait_ge(s_aw, 16 * 18)
            for k in range(KD):
                for g in range(4):
                    c = (k * 4 + g) * N
                    pe.transpose(PS[:, 0, c:c + N], a_wraw[:, g, k * P:(k + 1) * P], ident[0:N, 0:N])
            for k in range(KD):
                ins = pe.transpose(PS[0:N, 1, k * P:(k + 1) * P], a_wpraw[:, k, :], ident[:, :])
            ins.then_inc(s_wt, 1)
            pe.wait_ge(s_we, 1)
            with pe.Fori(0, B // 2) as p:
                for g in range(GP):
                    pe.wait_ge(s_axn, p * (GP * G) + G * (g + 1))
                    if g >= 2:
                        pe.wait_ge(s_axT, (p * GP + (g - 1)) * KD)
                    transpose_group(pe, 6 - 2 * (g % 2), a_rows[g % 2]).then_inc(s_atp, 1)
                pe.wait_ge(s_axT, (p * GP + GP) * KD)
                pe.sem_inc(s_pass, 1)
                transpose_experts(pe, p * (2 * E0P))
                for g in range(4):
                    if g >= 2:
                        pe.wait_ge(s_agev, p * 4 + (g - 1))
                    for c in range(NC2):
                        for b in range(2):
                            for k in range(KD):
                                ins = pe.matmul(PS[b * N:(b + 1) * N, 2 * (g % 2) + c, :], a_wT[:, k, g, :],
                                                a_xT[:, k, b * S + c * 512:b * S + (c + 1) * 512],
                                                start=(k == 0), stop=(k == KD - 1))
                    ins.then_inc(s_agate, 1)
                transpose_experts(pe, p * (2 * E0P) + E0P, p * 4 + 4)
                pe.wait_ge(s_ah, p + 1)
                for n in range(2 * QT):
                    b, t = n // QT, n % QT
                    if n >= 2:
                        pe.wait_ge(s_x1, p * (2 * QT) + (n - 1))
                    pe.matmul(PS[:, 4 + n % 2, 0:D], a_h[:, t * P:(t + 1) * P], a_wpT[b][:, :], start=True, stop=True).then_inc(s_ay, 1)
                pe.wait_ge(s_x1, p * (2 * QT) + 2 * QT)
            finish_stage(pe, 1)
            pe.wait_ge(s_bw, 16)
            for k in range(KD):
                ins = pe.transpose(PS[:, 6, k * E0:(k + 1) * E0], b_gw[:, k * P:(k + 1) * P], ident[0:E0, 0:E0])
            ins.then_inc(s_wt, 1)
            pe.wait_ge(s_we, 2)

            def router_scores(g, n):
                pe.wait_ge(s_bxn, g * G + G)
                if not (isinstance(g, int) and g == 0):
                    pe.wait_ge(s_bxT, g)
                transpose_group(pe, 6, b_rows[n]).then_inc(s_btp, 1)
                pe.wait_ge(s_bxT, g + 1)
                for q in range(G):
                    for k in range(KD):
                        ins = pe.matmul(PS[:, 2 * (n % 2), q * E0:(q + 1) * E0], b_xT[n % 2][:, k, q * P:(q + 1) * P], b_gwT[:, k, :],
                                        start=(k == 0), stop=(k == KD - 1))
                ins.then_inc(s_bsc, 1)

            def count_before(g):
                pe.wait_ge(s_boh, g + 1)
                for q in range(G):
                    dst = PS[:, 1, q * E0:(q + 1) * E0]
                    pe.matmul(dst, onesb[:, :], b_sum[:, :], start=True, stop=False)
                    for r in range(q):
                        pe.matmul(dst, onesb[:, :], b_ohs[:, r, :], start=False, stop=False)
                    ins = pe.matmul(dst, tri[:, :], b_ohs[:, q, :], start=False, stop=True)
                ins.then_inc(s_bpre, 1)

            for g in range(2):
                router_scores(g, g)
            with pe.Fori(0, NG // RBUF - 1) as i:
                for n in range(RBUF):
                    count_before(i * RBUF + n)
                    router_scores(i * RBUF + (n + 2), (n + 2) % RBUF)
            for n in range(RBUF):
                count_before(NG - RBUF + n)
                if n < RBUF - 2:
                    router_scores(NG - RBUF + n + 2, n + 2)
            pe.wait_ge(s_boh, NG + 1)
            pe.matmul(PS[:, 0, 0:E0], onesb[:, :], b_sum[:, :], start=True, stop=True).then_inc(s_bcnt, 1)
            pe.wait_ge(s_bplan, 2)
            pe.sem_inc(s_btt, 2)
            pe.sem_inc(s_bhid, 2)
            pe.sem_inc(s_bye, 2)

            def expert_of(n):
                return pe.value_load(b_tei[0:1, bass.ds(n, 1)], min_val=0, max_val=E0 - 1)

            def transpose_rows(n, half, j):
                pe.wait_ge(s_bin[j], half * 16 + 16)
                if not (isinstance(n, int) and n == 0):
                    pe.wait_ge(s_btT, n)
                for k in range(KD):
                    ins = pe.transpose(PS[:, 4, k * P:(k + 1) * P], b_xt[:, j, k * P:(k + 1) * P], ident[:, :])
                ins.then_inc(s_btt, 1)

            def hidden(n, j, c, e):
                if c == 0:
                    pe.wait_ge(s_btT, n + 1)
                    pe.wait_ge(s_bhid, n + 1)
                    pe.sem_inc(s_pass, 1)
                for k in range(KD):
                    ins = pe.matmul(PS[:, 2 * j + c, :], b_tT[:, j, k, :], b_w12T[:, k, bass.ds(e * (2 * H0) + c * H0, H0)],
                                    start=(k == 0), stop=(k == KD - 1))
                ins.then_inc((s_bh1, s_bh2)[c], 1)

            def transpose_hidden(n, j):
                pe.wait_ge(s_bhid, n + 3)
                for k in range(KH):
                    ins = pe.transpose(PS[:, 5, k * P:(k + 1) * P], b_hid[:, j, k * P:(k + 1) * P], ident[:, :])
                ins.then_inc(s_bht, 1)

            def second_layer(n, j, e):
                pe.wait_ge(s_bhT, n + 1)
                pe.wait_ge(s_bye, n + 1)
                pe.sem_inc(s_pass, 1)
                for k in range(KH):
                    ins = pe.matmul(PS[:, 6 + j, 0:D], b_hT[:, j, k, :], b_w3T[:, k, bass.ds(e * D, D)],
                                    start=(k == 0), stop=(k == KH - 1))
                ins.then_inc(s_by, 1)

            transpose_rows(0, 0, 0)
            e = expert_of(0)
            for c in range(2):
                hidden(0, 0, c, e)
            transpose_rows(1, 0, 1)
            with pe.Fori(0, TILES0 // 2 - 1) as i:
                for j in (1, 0):
                    n = i * 2 + (2 - j)
                    e = expert_of(n)
                    hidden(n, j, 0, e)
                    transpose_hidden(n - 1, 1 - j)
                    hidden(n, j, 1, e)
                    transpose_rows(n + 1, i + 1, 1 - j)
                    second_layer(n - 1, 1 - j, expert_of(n - 1))
            last = TILES0 - 1
            e = expert_of(last)
            hidden(last, 1, 0, e)
            transpose_hidden(last - 1, 0)
            hidden(last, 1, 1, e)
            second_layer(last - 1, 0, expert_of(last - 1))
            transpose_hidden(last, 1)
            second_layer(last, 1, expert_of(last))
            finish_stage(pe, 2)
            pe.sem_inc(s_cPu, PBUF)
            pe.sem_inc(s_cPa, PBUF)
            pe.sem_inc(s_cP, 2)
            pe.sem_inc(s_cyn, 2 * NC2)
            pe.sem_inc(s_cD, NC2)
            for r in range(2):
                pe.sem_inc(s_turn[r], 1)
            with pe.Fori(0, NPAIR) as hp:
                for h in range(2):
                    pe.wait_ge(s_cst, hp * (4 + KD) + (2 * h + 2))
                    for k in range(KD):
                        ins = pe.transpose(PS[:, 2 * h, k * P:(k + 1) * P], c_qkst[h][:, k * P:(k + 1) * P], ident[:, :])
                    ins.then_inc(s_cwt, 1)
                    for k in range(KD):
                        ins = pe.transpose(PS[:, 2 * h + 1, k * DQ:(k + 1) * DQ], c_vst[h][:, k * P:(k + 1) * P], ident[0:DQ, 0:DQ])
                    ins.then_inc(s_cwt, 1)
                pe.wait_ge(s_cst, hp * (4 + KD) + (4 + KD))
                for k in range(KD):
                    ins = pe.transpose(PS[:, 4, k * P:(k + 1) * P], c_wst[:, k, :, :].rearrange("p h v -> p (h v)"), ident[:, :])
                ins.then_inc(s_cwt, 1)
                pe.wait_ge(s_cwh, hp * 5 + 5)
                pe.wait_ge(s_cwl, hp * 4 + 4)
            parts = ((0, 0), (1, 0), (0, 1))

            def transpose_x(batch, g, use):
                pe.wait_ge(s_cxn, batch * QT + (g + 1) * G)
                for k in range(KD):
                    pe.wait_ge(s_turn[k], use[k] + (g + 1))
                    for q in range(G):
                        ins = pe.transpose(PS[:, 2 + k, q * P:(q + 1) * P], xn[:, q, k * P:(k + 1) * P], ident[:, :])
                    ins.then_inc(s_ctp, 1)

            def values(batch, a, use):
                for t in range(QT):
                    pe.wait_ge(s_turn[t % 2], use[t % 2] + (t // 2 + 1))
                    for n, (x, w) in enumerate(parts):
                        for k in range(KD):
                            ins = pe.matmul(PS[:, 2 + t % 2, :], c_xT[x][:, k, t * P:(t + 1) * P], c_wv[w][:, k, a * 512:(a + 1) * 512],
                                            start=(n == 0 and k == 0), stop=(n == 2 and k == KD - 1))
                    ins.then_inc(s_cv, 1)

            def project(nth, h, step, taken=None):
                c, n = step // len(parts), step % len(parts)
                w, x = parts[n]
                if step == 0:
                    pe.wait_ge(s_cw[h], nth * 32 + 32)
                if n == 0 and taken is not None:
                    pe.wait_ge(s_cks, taken + 2 * c)
                for k in range(KD):
                    ins = pe.matmul(PS[:, c, :], c_st[h][w][:, k, :], c_xT[x][:, k, c * 512:(c + 1) * 512],
                                    start=(n == 0 and k == 0), stop=(n == 2 and k == KD - 1))
                if n == len(parts) - 1:
                    ins.then_inc(s_cqk, 1)

            def scores(H, h, n, use):
                t, c = CHUNKS[n]
                w = min(512, (t + 1) * P - c * 512)
                if n in (0, 4):
                    pe.wait_ge(s_cks, H * 4 + (4 if n else 2))
                last = (t + 1) * P <= (c + 1) * 512
                pe.wait_ge(s_turn[n % 2], use[n % 2] + (n // 2 + 1))
                ins = pe.matmul(PS[:, 2 + n % 2, 0:max(w, 256)], c_q1[h][:, t * P:(t + 1) * P], c_k1[h][:, c * 512:c * 512 + max(w, 256)],
                                start=True, stop=not last)
                if last:
                    ins = pe.matmul(PS[:, 2 + n % 2, w - P:w], identb[:, :], c_maskq[:, :], start=False, stop=True)
                ins.then_inc(s_cS, 1)

            def transpose_max(H, use):
                pe.wait_ge(s_cmx, H + 1)
                pe.wait_ge(s_turn[0], use[0] + (len(CHUNKS) // 2 + 1))
                pe.transpose(PS[0:QT, 2, 0:P], c_max[:, :], ident[:, :]).then_inc(s_cmT, 1)

            def scores_t(H, h, m):
                c, j = BLOCKS[m]
                off = max(0, j * P - c * 512)
                skip = P if off == 512 - P else 0
                q = slice(c * 512 + off - skip, (c + 1) * 512)
                n = 512 - off + skip
                diagonal = j * P >= c * 512
                if m == 0:
                    pe.wait_ge(s_cm, H + 1)
                    pe.wait_ge(s_ck2, H + 1)
                pe.wait_ge(s_cP, H * len(BLOCKS) + (m + 1))
                pe.matmul(PS[:, 4 + m % 2, 0:n], c_k1[h][:, j * P:(j + 1) * P], c_q1[h][:, q], start=True, stop=False)
                ins = pe.matmul(PS[:, 4 + m % 2, 0:n], c_k2[h][:, j * P:(j + 1) * P], c_q2[h][:, q], start=False, stop=not diagonal)
                if diagonal:
                    ins = pe.matmul(PS[:, 4 + m % 2, skip:skip + P], identb[:, :], c_maskk[:, :], start=False, stop=True)
                ins.then_inc(s_cT, 1)

            def outputs(H, nth, h, m):
                c, j = BLOCKS[m]
                t0 = max(0, j - 4 * c)
                p = c_p[:, m % PBUF, :].rearrange("p (n a q) -> p n a q", n=2, a=2)
                if m == 0:
                    pe.wait_ge(s_cvh[h], nth * 16 + 16)
                pe.wait_ge(s_cP, H * len(BLOCKS) + (m + 3))
                for a in range(2):
                    tiles = [t for t in (a, a + 2) if t >= t0]
                    if not tiles:
                        continue
                    first, n = (tiles[0] - t0), len(tiles)
                    if n == 2:
                        moving = p[:, :, first % 2, :]
                        dst = PS[a * DQ:(a + 1) * DQ, 6 + c, 0:256].rearrange("p (n q) -> p n q", n=2)
                    else:
                        moving = c_p[:, m % PBUF, first * P:(first + 1) * P]
                        dst = PS[a * DQ:(a + 1) * DQ, 6 + c, P:2 * P]
                    ins = pe.matmul(dst, c_vh[h][:, j, :], moving, start=(j == 0), stop=(t0 == 2 + a))
                ins.then_inc(s_cPu, 1)

            def denominators(H, c):
                pe.wait_ge(s_cPa, H * len(BLOCKS) + (PBUF + (4, len(BLOCKS))[c]))
                d = c_den[c][:, :].rearrange("p (n a q) -> p n a q", n=2, a=2)
                for a in range(2):
                    ins = pe.matmul(PS[a * DQ:(a + 1) * DQ, 6 + c, 256:512].rearrange("p (n q) -> p n q", n=2),
                                    ones[:, 0:DQ], d[:, :, a, :], start=True, stop=True)
                ins.then_inc(s_cD, 1)

            def z_of(pair, hp, yT, n, use):
                pe.wait_ge(s_turn[n % 2], use[n % 2] + (n // 2 + 1))
                for a in range(2):
                    t = 2 * n + a
                    ins = pe.matmul(PS[:, 2 + n % 2, a * D:(a + 1) * D], yT[:, t * P:(t + 1) * P],
                                    c_wo[:, bass.ds(hp, 1), :].rearrange("p a d -> p (a d)"), start=True, stop=True)
                ins.then_inc(s_cz, 1)

            def head_products(b, hp, h, nxt, first, par):
                pair = b * NPAIR + hp
                H = pair * 2 + h
                final = isinstance(hp, int) and hp == NPAIR - 1
                fetch = nxt and final
                follows = nxt or not (final and h == 1)
                zs = h == 0 and not first
                use = [turns(r, heads=H + 1, pairs=pair - 1 if zs else pair, vs=b + 1, xts=b + (2 if fetch else 1)) for r in range(2)]
                chunks = {0: (0, 1), 1: (2, 3), 3: (4, 5), 4: (6, 7), 5: (8, 9), 6: (10, 11)}
                if fetch and h == 0:
                    chunks.update({0: (), 1: (), 2: (0, 1, 2, 3)})
                for m in range(len(BLOCKS)):
                    c, j = BLOCKS[m]
                    if m == 0 and (h or not first):
                        denominators(H - 1, 1)
                    if j == 0:
                        pe.wait_ge(s_cyn, H * (2 * NC2) + (2 * c + 2))
                    outputs(H, pair, h, m)
                    if m == 5:
                        denominators(H, 0)
                    if fetch and h == 0 and m < 2:
                        transpose_x(b + 1, m, [u - S // GT for u in use])
                    if follows:
                        for n in chunks.get(m, ()):
                            scores(H + 1, 1 - h, n, use)
                    if 3 <= m <= 8 and (nxt or not final):
                        if fetch and h == 0 and m == 3:
                            for k in range(KD):
                                pe.wait_ge(s_turn[k], use[k] + 1)
                        project(pair + 1, h, m - 3, H * 4 + 6)
                    if follows and m == 8:
                        transpose_max(H + 1, use)
                    if zs and m in (9, 10):
                        if m == 9:
                            pe.wait_ge(s_cyn, pair * (4 * NC2) + 2 * NC2)
                        used = [use[r] + (7, 6)[r] for r in range(2)]
                        for n in range((m - 9) * 2, (m - 9) * 2 + 2):
                            z_of(pair - 1, hp - 1, c_yT[1 - par], n, used)
                    if m + 2 < len(BLOCKS):
                        scores_t(H, h, m + 2)
                    elif follows:
                        scores_t(H + 1, 1 - h, m + 2 - len(BLOCKS))

            def batch_products(b, nxt):
                def pair_products(hp, first, par):
                    for h in range(2):
                        head_products(b, hp, h, nxt, first, par)
                pair_products(0, True, 0)
                with pe.Fori(0, NPAIR // 2 - 1) as i:
                    for n in range(2):
                        pair_products(i * 2 + (n + 1), False, 1 - n)
                pair_products(NPAIR - 1, False, 1)
                pair = b * NPAIR + (NPAIR - 1)
                heads = b * NH + (NH + 1 if nxt else NH)
                xts = b + (2 if nxt else 1)
                denominators(b * NH + (NH - 1), 1)
                use = [turns(r, heads=heads, pairs=pair, vs=b + 1, xts=xts) for r in range(2)]
                if nxt:
                    values(b + 1, 0, use)
                pe.wait_ge(s_cyn, pair * (4 * NC2) + 6 * NC2)
                for n in range(QT // 2):
                    z_of(pair, NPAIR - 1, c_yT[1], n, [u + (QT // 2 if nxt else 0) for u in use])
                if nxt:
                    values(b + 1, 1, [u + (QT // 2 + QT // 4) for u in use])

            for g in range(S // GT):
                transpose_x(0, g, [turns(r, heads=0, pairs=0, vs=0, xts=0) for r in range(2)])
            for k in range(KD):
                pe.wait_ge(s_turn[k], turns(k, heads=0, pairs=0, vs=0, xts=1) + 1)
            for a in range(2):
                values(0, a, [turns(r, heads=0, pairs=0, vs=0, xts=1) + a * (QT // 2) for r in range(2)])
            for step in range(NC2 * len(parts)):
                project(0, 0, step)
            use0 = [turns(r, heads=0, pairs=0, vs=1, xts=1) for r in range(2)]
            pe.wait_ge(s_cset, 3)
            for n in range(len(CHUNKS)):
                scores(0, 0, n, use0)
            transpose_max(0, use0)
            for step in range(NC2 * len(parts)):
                project(0, 1, step, 2)
            for m in range(2):
                scores_t(0, 0, m)
            with pe.Fori(0, B - 1) as b:
                batch_products(b, True)
            batch_products(B - 1, False)
            pe.wait_ge(s_cks, B * NH * 4)
            pe.wait_ge(s_dcast, 3)
            for k in range(KD):
                pe.transpose(PS[:, 0, k * E1:(k + 1) * E1], d_gwf[:, k * P:(k + 1) * P], ident[0:E1, 0:E1])
                for a in range(2):
                    c = (k * 2 + a) * I1
                    pe.transpose(PS[:, 1, c:c + I1], d_rawf[:, a, k * P:(k + 1) * P], ident[:, :])
                ins = pe.transpose(PS[:, 4, k * P:(k + 1) * P], d_raw2f[:, k, :], ident[:, :])
            ins.then_inc(s_wt, 1)
            finish_stage(pe, 3)
            pe.wait_ge(s_we, 3)
            for n, sem in ((EBUF, s_det), (EBUF, s_dec), (EBUF, s_dec2), (EBUF, s_deh), (EBUF, s_dey), (2, s_deL), (2, s_dep), (2, s_deg), (2, s_dye), (1, s_dsa)):
                pe.sem_inc(sem, n)

            def router_scores(g, n):
                j = n % 2
                pe.wait_ge(s_dxn, g * G + G)
                if not (isinstance(g, int) and g == 0):
                    pe.wait_ge(s_dxT, g)
                transpose_group(pe, 6, d_rows[n]).then_inc(s_dtp, 1)
                pe.wait_ge(s_dxT, g + 1)
                for q in range(G):
                    for k in range(KD):
                        ins = pe.matmul(PS[:, j, q * E1:(q + 1) * E1], d_xT[j][:, k, q * P:(q + 1) * P], d_gwT[:, k, :],
                                        start=(k == 0), stop=(k == KD - 1))
                ins.then_inc(s_dsc, 1)

            def shared_hidden(j):
                for a in range(2):
                    for k in range(KD):
                        ins = pe.matmul(PS[:, 3 + a, :], d_s1T[:, k, a, :], d_xT[j][:, k, :], start=(k == 0), stop=(k == KD - 1))
                ins.then_inc(s_dsh, 1)

            def count_before(g):
                pe.wait_ge(s_doh, g + 1)
                for q in range(G):
                    dst = PS[:, 2, q * E1:(q + 1) * E1]
                    pe.matmul(dst, onesb[:, :], d_sum[:, :], start=True, stop=False)
                    for r in range(q):
                        pe.matmul(dst, onesb[:, :], d_ohs[:, r, :], start=False, stop=False)
                    ins = pe.matmul(dst, tri[:, :], d_ohs[:, q, :], start=False, stop=True)
                ins.then_inc(s_dpre, 1)

            def shared_y(g):
                pe.wait_ge(s_dsg, g + 1)
                for n in range(G // 2):
                    pe.wait_ge(s_dsa, g * (G // 2) + (n + 1))
                    for a in range(2):
                        q = 2 * n + a
                        ins = pe.matmul(PS[:, 5, a * D:(a + 1) * D], d_sh[:, q * P:(q + 1) * P], d_s2T[:, :], start=True, stop=True)
                    ins.then_inc(s_dsy, 1)

            def group_step(g, n, ahead):
                count_before(g)
                shared_hidden(n % 2)
                if ahead:
                    router_scores(g + 2, (n + 2) % RBUF)
                shared_y(g)

            for g in range(2):
                router_scores(g, g)
            with pe.Fori(0, NG // RBUF - 1) as i:
                for n in range(RBUF):
                    group_step(i * RBUF + n, n, True)
            for n in range(RBUF):
                group_step(NG - RBUF + n, n, n < RBUF - 2)

            def transpose_rows(e, quarter, q):
                pe.wait_ge(s_dxe[q], quarter * 16 + 16)
                pe.wait_ge(s_deL, e + 1)
                for k in range(KD):
                    for a in range(C1 // P):
                        c = k * C1 + a * P
                        ins = pe.transpose(PS[:, q % 2, c:c + P], d_xe[:, q, a, k * P:(k + 1) * P], ident[:, :])
                ins.then_inc(s_det, 1)

            def hidden(e, q):
                pe.wait_ge(s_deL, e + 3)
                pe.wait_ge(s_dec, e + (EBUF + 1))
                pe.wait_ge(s_dep, e + 1)
                for a in range(2):
                    for k in range(KD):
                        c = a * D + k * I1
                        for n in range(2):
                            ins = pe.matmul(PS[:, 2 + q % 2, a * C1:(a + 1) * C1], d_wf[:, q, c:c + I1], d_xeT[n][:, q % 2, k, :],
                                            start=(k == 0 and n == 0), stop=(k == KD - 1 and n == 1))
                ins.then_inc(s_deh, 1)

            def second_layer(e, q):
                pe.wait_ge(s_deg, e + 3)
                pe.wait_ge(s_dec2, e + (EBUF + 1))
                pe.wait_ge(s_dye, e + 1)
                for a in range(C1 // P):
                    for n in range(2):
                        ins = pe.matmul(PS[:, 4 + q % 2, a * D:(a + 1) * D], d_ehs[n][:, q % 2, a * P:(a + 1) * P], d_wf[:, q, 2 * D:3 * D],
                                        start=(n == 0), stop=(n == 1))
                ins.then_inc(s_dey, 1)

            for e in range(2):
                transpose_rows(e, 0, e)
            for e in range(2):
                hidden(e, e)
                transpose_rows(e + 2, 0, e + 2)
            with pe.Fori(0, E1 // EBUF - 1) as i:
                for r in range(EBUF):
                    e = i * EBUF + (r + 2)
                    hidden(e, (r + 2) % EBUF)
                    transpose_rows(e + 2, i + 1, r)
                    second_layer(e - 2, r)
            for e in range(E1 - 2, E1):
                hidden(e, e % EBUF)
                second_layer(e - 2, (e - 2) % EBUF)
            for e in range(E1 - 2, E1):
                second_layer(e, e % EBUF)


_INS = ['L0_attn_x', 'L0_attn_ln_w', 'L0_attn_ln_b', 'L0_attn_Wi', 'L0_attn_bi', 'L0_attn_Wf', 'L0_attn_bf',
        'L0_attn_Wz', 'L0_attn_bz', 'L0_attn_Wo', 'L0_attn_bo', 'L0_attn_Wp', 'L0_attn_bp', 'L0_ffn_w12',
        'L0_ffn_w3', 'L0_ffn_gate_w', 'L1_attn_Q', 'L1_attn_K', 'L1_attn_V', 'L1_attn_W', 'L1_ffn_gate_w',
        'L1_ffn_bias', 'L1_ffn_W1', 'L1_ffn_W3', 'L1_ffn_W2', 'L1_ffn_sw1', 'L1_ffn_sw3', 'L1_ffn_sw2']
_OUTS = [((4, 1024, 256), 'float32')]


def kernel(**inputs):
    import numpy as _np
    import concourse.bacc as _bacc
    from concourse import mybir as _mybir
    from concourse.bass_utils import run_bass_kernel_spmd as _run

    nc = _bacc.Bacc("TRN2", target_bir_lowering=False, num_devices=1)
    arrays, args = {}, []
    for name in _INS:
        a = _np.ascontiguousarray(inputs[name])
        arrays[f"in_{name}_dram"] = a
        args.append(nc.dram_tensor(f"in_{name}_dram", a.shape, _mybir.dt.from_np(a.dtype), kind="ExternalInput").ap())
    for i, (shape, dtype) in enumerate(_OUTS):
        dt = _mybir.dt.from_np(_np.dtype(dtype))
        args.append(nc.dram_tensor(f"out_{i}_dram", shape, dt, kind="ExternalOutput").ap())
    network(nc, *args)
    r = _run(nc, [arrays], core_ids=[0])
    return r.results[0]["out_0_dram"]
```
